# Optimizing a Trainium2 kernel written in Bass

```python
import numpy as np
import jax
import jax.numpy as jnp

def _softmax(x, axis=-1):
    return jax.nn.softmax(x, axis=axis)

def _gelu(x):
    return jax.nn.gelu(x, approximate=True)

def _silu(x):
    return jax.nn.silu(x)

def _sigmoid(x):
    return jax.nn.sigmoid(x)

def _layernorm(x, axis=-1, eps=1e-05):
    m = jnp.mean(x, axis=axis, keepdims=True)
    v = jnp.var(x, axis=axis, keepdims=True)
    return (x - m) / jnp.sqrt(v + eps)

def _scatter_add(tgt, idx, src, axis=0):
    return tgt.at[idx].add(src)

def _segment_sum(src, seg, n):
    return jax.ops.segment_sum(src, seg, n)
kernel_name = 'mk_seq_postln_d2_jaxref_r4_adf02a'

def setup_inputs(seed: int=0):
    np.random.seed(seed)
    _w = jnp.asarray

    def _L0_attn_setup():
        import jax, jax.numpy as jnp
        import numpy as np
        B, S, D = (2, 1024, 512)
        LN_EPS = 1e-05
        key = jax.random.key(seed)
        ks = jax.random.split(key, 4)
        s = 0.02
        return {'hidden_states': jax.random.normal(ks[0], (B, S, D), jnp.float32), 'attention_mask': jnp.ones((B, S), jnp.int32), 'ln_g': jnp.ones((D,), jnp.float32), 'ln_b': jnp.zeros((D,), jnp.float32), 'Wq': jax.random.normal(ks[1], (D, D), jnp.float32) * s, 'bq': jnp.zeros((D,), jnp.float32), 'Wqa': jnp.zeros((D, D), jnp.float32), 'bqa': jnp.ones((D,), jnp.float32), 'Wk': jax.random.normal(ks[2], (D, D), jnp.float32) * s, 'bk': jnp.zeros((D,), jnp.float32), 'Wka': jnp.zeros((D, D), jnp.float32), 'bka': jnp.ones((D,), jnp.float32), 'Wv': jax.random.normal(ks[3], (D, D), jnp.float32) * s, 'bv': jnp.zeros((D,), jnp.float32)}
    _L0_attn_in = _L0_attn_setup()

    def _L0_ffn_setup():
        import jax, jax.numpy as jnp
        import numpy as np
        ZERO_POINT = 128.0

        def _dequant(wq, scale):
            return (wq.astype(jnp.float32) - ZERO_POINT) * scale[:, None]
        key = jax.random.key(seed)
        ks = jax.random.split(key, 7)
        H, I = (512, 2048)
        B, S = (2, 512)
        hidden_state = jax.random.normal(ks[0], (B, S, H), dtype=jnp.float32)
        gate_w = jax.random.randint(ks[1], (I, H), 0, 64, dtype=jnp.int32)
        up_w = jax.random.randint(ks[2], (I, H), 0, 64, dtype=jnp.int32)
        down_w = jax.random.randint(ks[3], (H, I), 0, 64, dtype=jnp.int32)
        gate_scale = jax.random.uniform(ks[4], (I,), dtype=jnp.float32) * 0.02
        up_scale = jax.random.uniform(ks[5], (I,), dtype=jnp.float32) * 0.02
        down_scale = jax.random.uniform(ks[6], (H,), dtype=jnp.float32) * 0.02
        return {'hidden_state': hidden_state, 'gate_w': gate_w, 'gate_scale': gate_scale, 'up_w': up_w, 'up_scale': up_scale, 'down_w': down_w, 'down_scale': down_scale}
    _L0_ffn_in = _L0_ffn_setup()

    def _L1_attn_setup():
        import jax, jax.numpy as jnp
        import numpy as np
        B, S, HID = (2, 512, 512)
        H, D, K = (16, 128, 4)
        ROPE_BASE = 1000000.0
        EPS_NORM = 1e-06

        def _silu(u):
            return u * jax.nn.sigmoid(u)

        def _causal_dwconv(x_bsc, w_ck):
            C, Kw = w_ck.shape
            y = jax.lax.conv_general_dilated(x_bsc.transpose(0, 2, 1), w_ck[:, None, :], (1,), [(Kw - 1, 0)], dimension_numbers=('NCH', 'OIH', 'NCH'), feature_group_count=C)
            return y.transpose(0, 2, 1)

        def _lag(u, s):
            if s == 0:
                return u
            pad = [(0, 0), (s, 0)] + [(0, 0)] * (u.ndim - 2)
            return jnp.pad(u, pad)[:, :u.shape[1]]
        key = jax.random.key(seed)
        ks = jax.random.split(key, 12)
        p = lambda k, shape: jax.random.normal(k, shape, jnp.float32) * 0.02
        x = jax.random.normal(ks[0], (B, S, HID), jnp.float32)
        return {'x': x, 'Wq': p(ks[1], (HID, H * D)), 'Wk': p(ks[2], (HID, H * D)), 'Wv': p(ks[3], (HID, H * D)), 'Wz': p(ks[4], (HID, H * D)), 'Wa': p(ks[5], (HID, H)), 'Wb': p(ks[6], (HID, H)), 'conv_q_w': p(ks[7], (H * D, K)), 'conv_k_w': p(ks[8], (H * D, K)), 'conv_v_w': p(ks[9], (H * D, K)), 'norm_w': jnp.ones((H * D,), jnp.float32), 'Wout': p(ks[10], (H * D, HID))}
    _L1_attn_in = _L1_attn_setup()

    def _L1_ffn_setup():
        import jax, jax.numpy as jnp
        import numpy as np
        GOLDEN_CENTER = 1.0 / np.e
        GOLDEN_LOWER = 0.5 - np.log(4.0 / 3.0)
        GOLDEN_UPPER = 0.5

        def _golden_weights(x, Wr, temperature):
            inh = jax.nn.sigmoid(x @ Wr / temperature)
            in_zone = (inh >= GOLDEN_LOWER) & (inh <= GOLDEN_UPPER)
            distance = jnp.abs(inh - GOLDEN_CENTER)
            weights = jnp.exp(-distance / 0.1) * in_zone.astype(x.dtype)
            wsum = jnp.sum(weights, axis=-1, keepdims=True)
            no_expert = wsum < 1e-08
            fb = jnp.exp(-distance / 0.3)
            _, top2 = jax.lax.top_k(fb, 2)
            fb_mask = jnp.sum(jax.nn.one_hot(top2, weights.shape[-1], dtype=x.dtype), axis=-2)
            fb_w = fb * fb_mask
            fb_w = fb_w / jnp.maximum(jnp.sum(fb_w, axis=-1, keepdims=True), 1e-08)
            weights = jnp.where(no_expert, fb_w, weights)
            weights = weights / jnp.maximum(jnp.sum(weights, axis=-1, keepdims=True), 1e-08)
            return weights
        key = jax.random.key(seed)
        ks = jax.random.split(key, 5)
        B, T, D, E, F = (2, 512, 512, 8, 512)
        s_in = 1.0 / np.sqrt(D)
        s_f = 1.0 / np.sqrt(F)
        return {'x': jax.random.normal(ks[0], (B, T, D), dtype=jnp.float32), 'Wg': jax.random.normal(ks[1], (E, D, F), dtype=jnp.float32) * s_in, 'Wu': jax.random.normal(ks[2], (E, D, F), dtype=jnp.float32) * s_in, 'Wd': jax.random.normal(ks[3], (E, F, D), dtype=jnp.float32) * s_f, 'Wr': jax.random.normal(ks[4], (D, E), dtype=jnp.float32) * s_in, 'temperature': jnp.ones((1,), dtype=jnp.float32)}
    _L1_ffn_in = _L1_ffn_setup()
    _d = {'L0_attn_hidden_states': _L0_attn_in['hidden_states'], 'L0_attn_attention_mask': _L0_attn_in['attention_mask'], 'L0_attn_ln_g': _L0_attn_in['ln_g'], 'L0_attn_ln_b': _L0_attn_in['ln_b'], 'L0_attn_Wq': _L0_attn_in['Wq'], 'L0_attn_bq': _L0_attn_in['bq'], 'L0_attn_Wqa': _L0_attn_in['Wqa'], 'L0_attn_bqa': _L0_attn_in['bqa'], 'L0_attn_Wk': _L0_attn_in['Wk'], 'L0_attn_bk': _L0_attn_in['bk'], 'L0_attn_Wka': _L0_attn_in['Wka'], 'L0_attn_bka': _L0_attn_in['bka'], 'L0_attn_Wv': _L0_attn_in['Wv'], 'L0_attn_bv': _L0_attn_in['bv'], 'L0_ffn_gate_w': _L0_ffn_in['gate_w'], 'L0_ffn_gate_scale': _L0_ffn_in['gate_scale'], 'L0_ffn_up_w': _L0_ffn_in['up_w'], 'L0_ffn_up_scale': _L0_ffn_in['up_scale'], 'L0_ffn_down_w': _L0_ffn_in['down_w'], 'L0_ffn_down_scale': _L0_ffn_in['down_scale'], 'L1_attn_Wq': _L1_attn_in['Wq'], 'L1_attn_Wk': _L1_attn_in['Wk'], 'L1_attn_Wv': _L1_attn_in['Wv'], 'L1_attn_Wz': _L1_attn_in['Wz'], 'L1_attn_Wa': _L1_attn_in['Wa'], 'L1_attn_Wb': _L1_attn_in['Wb'], 'L1_attn_conv_q_w': _L1_attn_in['conv_q_w'], 'L1_attn_conv_k_w': _L1_attn_in['conv_k_w'], 'L1_attn_conv_v_w': _L1_attn_in['conv_v_w'], 'L1_attn_norm_w': _L1_attn_in['norm_w'], 'L1_attn_Wout': _L1_attn_in['Wout'], 'L1_ffn_Wg': _L1_ffn_in['Wg'], 'L1_ffn_Wu': _L1_ffn_in['Wu'], 'L1_ffn_Wd': _L1_ffn_in['Wd'], 'L1_ffn_Wr': _L1_ffn_in['Wr'], 'L1_ffn_temperature': _L1_ffn_in['temperature']}
    _x0 = _d['L0_attn_hidden_states']
    _d['L0_attn_hidden_states'] = jax.random.normal(jax.random.fold_in(jax.random.key(seed), 1), (4, 512, 512), dtype=_x0.dtype)
    del _x0
    return _d

def reference(L0_attn_hidden_states, L0_attn_attention_mask, L0_attn_ln_g, L0_attn_ln_b, L0_attn_Wq, L0_attn_bq, L0_attn_Wqa, L0_attn_bqa, L0_attn_Wk, L0_attn_bk, L0_attn_Wka, L0_attn_bka, L0_attn_Wv, L0_attn_bv, L0_ffn_gate_w, L0_ffn_gate_scale, L0_ffn_up_w, L0_ffn_up_scale, L0_ffn_down_w, L0_ffn_down_scale, L1_attn_Wq, L1_attn_Wk, L1_attn_Wv, L1_attn_Wz, L1_attn_Wa, L1_attn_Wb, L1_attn_conv_q_w, L1_attn_conv_k_w, L1_attn_conv_v_w, L1_attn_norm_w, L1_attn_Wout, L1_ffn_Wg, L1_ffn_Wu, L1_ffn_Wd, L1_ffn_Wr, L1_ffn_temperature):

    def _L0_attn_ref(hidden_states, attention_mask, ln_g, ln_b, Wq, bq, Wqa, bqa, Wk, bk, Wka, bka, Wv, bv):
        import jax, jax.numpy as jnp
        import numpy as np
        B, S, D = (2, 1024, 512)
        LN_EPS = 1e-05
        mu = jnp.mean(hidden_states, axis=-1, keepdims=True)
        var = jnp.var(hidden_states, axis=-1, keepdims=True)
        h = (hidden_states - mu) * jax.lax.rsqrt(var + LN_EPS) * ln_g + ln_b
        lin = lambda x, W, b: x @ W.T + b
        scale = 1.0 / jnp.sqrt(jnp.float32(D))
        query = lin(h, Wq, bq)
        keys = lin(h, Wk, bk)
        values = lin(h, Wv, bv)
        qw = jnp.exp(lin(query, Wqa, bqa) * scale)
        qw = qw / jnp.cumsum(qw, axis=1)
        pooled_query = jnp.cumsum(qw * query, axis=1)
        mixed_keys = pooled_query * keys
        kw = jnp.exp(lin(mixed_keys, Wka, bka) * scale)
        kw = kw / jnp.cumsum(kw, axis=1)
        pooled_keys = jnp.cumsum(kw * mixed_keys, axis=1)
        return pooled_keys * values

    def _L0_ffn_ref(hidden_state, gate_w, gate_scale, up_w, up_scale, down_w, down_scale):
        import jax, jax.numpy as jnp
        import numpy as np
        ZERO_POINT = 128.0

        def _dequant(wq, scale):
            return (wq.astype(jnp.float32) - ZERO_POINT) * scale[:, None]
        Wg = _dequant(gate_w, gate_scale)
        Wu = _dequant(up_w, up_scale)
        Wd = _dequant(down_w, down_scale)
        g = jnp.einsum('bsh,ih->bsi', hidden_state, Wg)
        u = jnp.einsum('bsh,ih->bsi', hidden_state, Wu)
        h = jax.nn.silu(g) * u
        return jnp.einsum('bsi,hi->bsh', h, Wd)

    def _L1_attn_ref(x, Wq, Wk, Wv, Wz, Wa, Wb, conv_q_w, conv_k_w, conv_v_w, norm_w, Wout):
        import jax, jax.numpy as jnp
        import numpy as np
        B, S, HID = (2, 512, 512)
        H, D, K = (16, 128, 4)
        ROPE_BASE = 1000000.0
        EPS_NORM = 1e-06

        def _silu(u):
            return u * jax.nn.sigmoid(u)

        def _causal_dwconv(x_bsc, w_ck):
            C, Kw = w_ck.shape
            y = jax.lax.conv_general_dilated(x_bsc.transpose(0, 2, 1), w_ck[:, None, :], (1,), [(Kw - 1, 0)], dimension_numbers=('NCH', 'OIH', 'NCH'), feature_group_count=C)
            return y.transpose(0, 2, 1)

        def _lag(u, s):
            if s == 0:
                return u
            pad = [(0, 0), (s, 0)] + [(0, 0)] * (u.ndim - 2)
            return jnp.pad(u, pad)[:, :u.shape[1]]
        Bc, Sc, _ = x.shape
        q = _silu(x @ Wq)
        k = _silu(x @ Wk)
        v = _silu(x @ Wv)
        z = x @ Wz
        a = x @ Wa
        b = x @ Wb
        q = _causal_dwconv(q, conv_q_w)
        k = _causal_dwconv(k, conv_k_w)
        v = _causal_dwconv(v, conv_v_w)
        q = q.reshape(Bc, Sc, H, D)
        k = k.reshape(Bc, Sc, H, D)
        v = v.reshape(Bc, Sc, H, D)
        inv = 1.0 / ROPE_BASE ** (jnp.arange(0, D, 2, dtype=jnp.float32) / D)
        fr = jnp.arange(Sc, dtype=jnp.float32)[:, None] * inv[None, :]
        cos = jnp.concatenate([jnp.cos(fr), jnp.cos(fr)], -1)[None, :, None, :]
        sin = jnp.concatenate([jnp.sin(fr), jnp.sin(fr)], -1)[None, :, None, :]

        def rot_half(u):
            u1, u2 = jnp.split(u, 2, axis=-1)
            return jnp.concatenate([-u2, u1], axis=-1)
        q = q * cos + rot_half(q) * sin
        k = k * cos + rot_half(k) * sin
        q = q / jnp.maximum(jnp.linalg.norm(q, axis=-1, keepdims=True), 1e-12)
        k = k / jnp.maximum(jnp.linalg.norm(k, axis=-1, keepdims=True), 1e-12)
        scale = 1.0 / D ** 0.5
        out = jnp.zeros_like(v)
        for s in range(K):
            k_s = _lag(k, s)
            v_s = _lag(v, s)
            a_s = _lag(a, s)
            attn = jnp.einsum('bshd,bshd->bsh', q, k_s) * scale
            gate = jax.nn.sigmoid(a_s * b)
            out = out + (attn * gate)[..., None] * v_s
        out = out.reshape(Bc, Sc, H * D)
        rms = jax.lax.rsqrt(jnp.mean(out * out, axis=-1, keepdims=True) + EPS_NORM)
        out = out * rms * norm_w * _silu(z)
        return out @ Wout

    def _L1_ffn_ref(x, Wg, Wu, Wd, Wr, temperature):
        import jax, jax.numpy as jnp
        import numpy as np
        GOLDEN_CENTER = 1.0 / np.e
        GOLDEN_LOWER = 0.5 - np.log(4.0 / 3.0)
        GOLDEN_UPPER = 0.5

        def _golden_weights(x, Wr, temperature):
            inh = jax.nn.sigmoid(x @ Wr / temperature)
            in_zone = (inh >= GOLDEN_LOWER) & (inh <= GOLDEN_UPPER)
            distance = jnp.abs(inh - GOLDEN_CENTER)
            weights = jnp.exp(-distance / 0.1) * in_zone.astype(x.dtype)
            wsum = jnp.sum(weights, axis=-1, keepdims=True)
            no_expert = wsum < 1e-08
            fb = jnp.exp(-distance / 0.3)
            _, top2 = jax.lax.top_k(fb, 2)
            fb_mask = jnp.sum(jax.nn.one_hot(top2, weights.shape[-1], dtype=x.dtype), axis=-2)
            fb_w = fb * fb_mask
            fb_w = fb_w / jnp.maximum(jnp.sum(fb_w, axis=-1, keepdims=True), 1e-08)
            weights = jnp.where(no_expert, fb_w, weights)
            weights = weights / jnp.maximum(jnp.sum(weights, axis=-1, keepdims=True), 1e-08)
            return weights
        weights = _golden_weights(x, Wr, temperature)
        gate = jnp.einsum('btd,edf->betf', x, Wg)
        up = jnp.einsum('btd,edf->betf', x, Wu)
        h = jax.nn.silu(gate) * up
        e_out = jnp.einsum('betf,efd->betd', h, Wd)
        out = jnp.einsum('bte,betd->btd', weights, e_out)
        return out
    x = L0_attn_hidden_states
    x = _layernorm(x + _L0_attn_ref(x, L0_attn_attention_mask, L0_attn_ln_g, L0_attn_ln_b, L0_attn_Wq, L0_attn_bq, L0_attn_Wqa, L0_attn_bqa, L0_attn_Wk, L0_attn_bk, L0_attn_Wka, L0_attn_bka, L0_attn_Wv, L0_attn_bv), axis=-1)
    x = _layernorm(x + _L0_ffn_ref(x, L0_ffn_gate_w, L0_ffn_gate_scale, L0_ffn_up_w, L0_ffn_up_scale, L0_ffn_down_w, L0_ffn_down_scale), axis=-1)
    x = _layernorm(x + _L1_attn_ref(x, L1_attn_Wq, L1_attn_Wk, L1_attn_Wv, L1_attn_Wz, L1_attn_Wa, L1_attn_Wb, L1_attn_conv_q_w, L1_attn_conv_k_w, L1_attn_conv_v_w, L1_attn_norm_w, L1_attn_Wout), axis=-1)
    x = _layernorm(x + _L1_ffn_ref(x, L1_ffn_Wg, L1_ffn_Wu, L1_ffn_Wd, L1_ffn_Wr, L1_ffn_temperature), axis=-1)
    return x

_drawn_inputs = setup_inputs


def setup_inputs(seed=0):
    import zlib

    import numpy as np

    out = dict(_drawn_inputs(seed))
    spreads = {'L0_attn_ln_g': (1.0, 0.2),
     'L0_attn_ln_b': (0.0, 0.1),
     'L0_attn_bq': (0.0, 0.1),
     'L0_attn_Wqa': (0.0, 0.312),
     'L0_attn_bqa': (1.0, 0.6),
     'L0_attn_bk': (0.0, 0.1),
     'L0_attn_Wka': (0.0, 0.295),
     'L0_attn_bka': (1.0, 0.6),
     'L0_attn_bv': (0.0, 0.1),
     'L1_attn_norm_w': (1.0, 0.6)}
    factors = {'L1_attn_Wa': 7.663, 'L1_attn_Wb': 8.0}
    for name, (base, spread) in spreads.items():
        noise = np.random.default_rng([zlib.crc32(name.encode()), seed]).standard_normal(out[name].shape)
        drawn = base * np.exp(spread * noise) if base else spread * noise
        out[name] = jnp.asarray(drawn.astype(out[name].dtype))
    for name, factor in factors.items():
        out[name] = (out[name] * factor).astype(out[name].dtype)
    return out
```

```python
import math
from contextlib import ExitStack

import numpy as np

import concourse.bass as bass
from concourse import mybir

F32 = mybir.dt.float32
F32R = mybir.dt.float32r
I32 = mybir.dt.int32
ALU = mybir.AluOpType
ACT = mybir.ActivationFunctionType
AX = mybir.AxisListType

P = 128
BATCH, SEQ, HID = 4, 512, 512
TOK = BATCH * SEQ
KC = HID // P
NTT = TOK // P
TPB = SEQ // P
HEADS, HDIM, LAGS = 16, 128, 4
INNER = 2048
EXPERTS, EXPERT_WIDTH = 8, 512
UNIT = 256
FPU = UNIT // P
LN_EPS = 1e-5
RMS_EPS = 1e-6
ROPE_BASE = 1000000.0


def f32(ap):
    return ap.bitcast(F32)


def product(pe, out, left, right, first=True, last=True):
    n = len(left)
    for k in range(n):
        (lh, ll), (rh, rl) = left[k], right[k]
        pe.matmul(out, lh, rh, start=first and k == 0, stop=False)
        pe.matmul(out, lh, rl, start=False, stop=False)
        done = pe.matmul(out, ll, rh, start=False, stop=last and k == n - 1)
    return done


class Sems:

    def __init__(self, nc, ctx, prefix):
        self.nc, self.ctx, self.prefix = nc, ctx, prefix

    def __call__(self, name):
        return self.ctx.enter_context(self.nc.semaphore(f"{self.prefix}_{name}"))


def wait_apart(eng, sem, value):
    eng.wait_ge(sem, value)
    if not isinstance(value, int):
        eng.nop(nofuse=True)


class Chain:

    def __init__(self, eng, sem, base=0, apart=False):
        self.eng, self.sem, self.n, self.base, self.apart = eng, sem, 0, base, apart

    def link(self, ins):
        ins.then_inc(self.sem, 1)
        self.n += 1
        (wait_apart if self.apart else type(self.eng).wait_ge)(self.eng, self.sem, self.base + self.n)


def norm_and_turn(nc, name, mem, normalise=True, turn=True):
    x_tok, xT_hi, xT_lo, ident = mem["x_tok"], mem["xT_hi"], mem["xT_lo"], mem["ident"]
    with ExitStack() as ctx:
        sem = Sems(nc, ctx, name)
        stats = ctx.enter_context(nc.sbuf_tensor(f"{name}_stats", [P, 2, 6], F32))
        mv = ctx.enter_context(nc.sbuf_tensor(f"{name}_mv", [P, 2, 2], F32))
        std = ctx.enter_context(nc.sbuf_tensor(f"{name}_std", [P, 2], F32))
        rstd = ctx.enter_context(nc.sbuf_tensor(f"{name}_rstd", [P, 2], F32))
        xn = ctx.enter_context(nc.sbuf_tensor(f"{name}_xn", [P, 2, HID], F32))
        turned = [ctx.enter_context(nc.psum_tensor(f"{name}_turned{j}", [P, KC, P], F32)) for j in range(2)]
        s_own = sem("own")
        s_var = sem("var")
        s_std = sem("std")
        s_xn = sem("xn")
        s_turn = sem("turn")
        s_hi = sem("hi")
        s_lo = sem("lo")
        per_tile = 4 if normalise else 0

        with nc.Block() as block:
            @block.vector
            def _(dve):
                with dve.Fori(0, NTT // 2) as i:
                    for j in range(2):
                        row = x_tok[:, bass.ds((2 * i + j) * HID, HID)]
                        chain = Chain(dve, s_own, i * (2 * per_tile) + j * per_tile, apart=True)
                        if normalise:
                            chain.link(dve.bn_stats(stats[:, j, :], row))
                            chain.link(dve.bn_aggr(mv[:, j, :], stats[:, j, :]))
                            dve.tensor_scalar(std[:, j:j + 1], mv[:, j, 1:2], LN_EPS, None,
                                              ALU.add).then_inc(s_var, 1)
                            dve.wait_ge(s_std, 2 * i + (j + 1))
                            if turn:
                                dve.wait_ge(s_hi, i * 2 + j)
                            chain.link(dve.tensor_scalar(xn[:, j, :], row, mv[:, j, 0:1], rstd[:, j:j + 1],
                                                         ALU.subtract, ALU.mult))
                            chain.link(dve.tensor_copy(row, xn[:, j, :]))
                            dve.sem_inc(s_xn, 1)
                        else:
                            if turn:
                                wait_apart(dve, s_hi, i * 2 + j)
                            dve.tensor_copy(xn[:, j, :], row).then_inc(s_xn, 1)
                        if turn:
                            dve.wait_ge(s_hi, 2 * i + (j + 1))
                            cols = bass.ds((2 * i + j) * P, P)
                            dve.tensor_tensor(xT_lo[:, :, cols], turned[j][:, :, :], f32(xT_hi[:, :, cols]),
                                              ALU.subtract).then_inc(s_lo, 1)

            @block.gpsimd
            def _(pool):
                if not normalise:
                    return
                with pool.Fori(0, NTT // 2) as i:
                    for j in range(2):
                        pool.wait_ge(s_var, 2 * i + (j + 1))
                        pool.tensor_tensor(rstd[:, j:j + 1], std[:, j:j + 1], mem["minus_half"][:, 0:1],
                                           ALU.pow).then_inc(s_std, 1)

            @block.scalar
            def _(act):
                if not turn:
                    return
                with act.Fori(0, NTT // 2) as i:
                    for j in range(2):
                        if turn:
                            wait_apart(act, s_turn, 2 * i + (j + 1))
                            cols = bass.ds((2 * i + j) * P, P)
                            act.activation(xT_hi[:, :, cols], turned[j][:, :, :], ACT.Copy).then_inc(s_hi, 1)

            @block.tensor
            def _(pe):
                if not turn:
                    return
                with pe.Fori(0, NTT // 2) as i:
                    for j in range(2):
                        pe.wait_ge(s_xn, 2 * i + (j + 1))
                        pe.wait_ge(s_lo, 2 * i + j)
                        for k in range(KC):
                            last = pe.transpose(turned[j][:, k, :], xn[:, j, k * P:(k + 1) * P], ident[:, :])
                        last.then_inc(s_turn, 1)


def gated_units(nc, name, mem, w_gate, w_up, w_down, units, scales=None, expert_weight=None):
    x_tok, xT_hi, xT_lo = mem["x_tok"], mem["xT_hi"], mem["xT_lo"]
    quantised = scales is not None
    with ExitStack() as ctx:
        sem = Sems(nc, ctx, name)

        def sb(what, shape, dt=F32):
            return ctx.enter_context(nc.sbuf_tensor(f"{name}_{what}", shape, dt))

        def bank(what):
            return ctx.enter_context(nc.psum_tensor(f"{name}_{what}", [P, 512], F32))

        W = KC * UNIT
        raw = [[sb(f"raw{p}{m}", [P, W], I32 if quantised else F32) for m in range(3)] for p in range(2)]
        w_hi = [[sb(f"whi{p}{m}", [P, W], F32R) for m in range(3)] for p in range(2)]
        w_lo = [[sb(f"wlo{p}{m}", [P, W], F32R) for m in range(3)] for p in range(2)]
        gated = [sb(f"gated{r}", [P, SEQ]) for r in range(2)]
        inner = [sb(f"inner{r}", [P, SEQ]) for r in range(2)]
        in_hi = [sb(f"inhi{r}", [P, FPU, SEQ], F32R) for r in range(2)]
        in_lo = [sb(f"inlo{r}", [P, FPU, SEQ], F32R) for r in range(2)]
        if quantised:
            scale_gate = sb("sgate", [P, units * FPU])
            scale_up = sb("sup", [P, units * FPU])
            scale_down = sb("sdown", [P, HID])
            flat = [[raw[p][m][:, :].bitcast(F32) for m in range(3)] for p in range(2)]
        else:
            flat = [[raw[p][m][:, :] for m in range(3)] for p in range(2)]
        G = [bank(f"G{r}") for r in range(2)]
        U = [bank(f"U{r}") for r in range(2)]
        D = [bank(f"D{r}") for r in range(TPB)]

        s_const = sem("const")
        s_raw = [sem(f"raw{p}") for p in range(2)]
        s_deq = sem("deq")
        s_whi = sem("whi")
        s_wlo = sem("wlo")
        s_g = sem("g")
        s_u = sem("u")
        s_silu = sem("silu")
        s_h = sem("h")
        s_hhi = sem("hhi")
        s_hlo = sem("hlo")
        s_d = sem("d")
        s_acc = sem("acc")
        NB = 2
        CH = FPU * BATCH

        def rotated(eng, before, body):
            before()
            with eng.Fori(0, units // 2 - 1) as i:
                body(i, False)
            body(units // 2 - 1, True)

        def weight_split_hi(act, pair, u, p):
            for m in range(3):
                if quantised:
                    act.wait_ge(s_deq, u * 3 + (m + 1))
                elif m == 0:
                    act.wait_ge(s_raw[p], pair * 48 + 48)
                act.activation(w_hi[p][m][:, :], flat[p][m], ACT.Copy).then_inc(s_whi, 1)

        with nc.Block() as block:
            @block.sync
            def _(sp):
                if quantised:
                    for t, src in ((scale_gate, scales[0]), (scale_up, scales[1]), (scale_down, scales[2])):
                        sp.dma_start(t[:, :], src).then_inc(s_const, 16)

                def load(u, p):
                    for m, w in enumerate((w_gate, w_up, w_down)):
                        src = w[u, :, :] if isinstance(u, int) else w[bass.ds(u, 1), :, :].rearrange("a p n -> (a p) n")
                        sp.dma_start(raw[p][m][:, :], src).then_inc(s_raw[p], 16)

                for p in range(2):
                    load(p, p)
                with sp.Fori(1, units // 2) as i:
                    for p in range(2):
                        wait_apart(sp, s_wlo, (2 * i + (p - 1)) * 3)
                        load(2 * i + p, p)

            @block.tensor
            def _(pe):
                pe.sem_inc(s_d, 2 * TPB)

                def gate_up(u, t, p):
                    if t == 0:
                        pe.wait_ge(s_whi, u * 3 + 3)
                        pe.wait_ge(s_wlo, u * 3 + 3)
                    for f in range(FPU):
                        r = u * CH + (t * FPU + f)
                        pe.wait_ge(s_h, r + 1)
                        cols = slice(t * SEQ, (t + 1) * SEQ)
                        for m, (out, done) in enumerate(((G, s_g), (U, s_u))):
                            left = [(w_hi[p][m][:, k * UNIT + f * P:k * UNIT + (f + 1) * P],
                                     w_lo[p][m][:, k * UNIT + f * P:k * UNIT + (f + 1) * P]) for k in range(KC)]
                            right = [(xT_hi[:, k, cols], xT_lo[:, k, cols]) for k in range(KC)]
                            product(pe, out[f][:, :], left, right).then_inc(done, 1)

                def down(u, t, p):
                    s = u * BATCH + t
                    pe.wait_ge(s_hlo, s * FPU + 2 + FPU)
                    for tt in range(TPB):
                        pe.wait_ge(s_acc, s * TPB + (tt + 1))
                        at = slice(tt * P, (tt + 1) * P)
                        left = [(in_hi[t % 2][:, f, at], in_lo[t % 2][:, f, at]) for f in range(FPU)]
                        right = [(w_hi[p][2][:, f * HID:(f + 1) * HID], w_lo[p][2][:, f * HID:(f + 1) * HID])
                                 for f in range(FPU)]
                        product(pe, D[tt][:, :], left, right).then_inc(s_d, 1)

                def body(i, last):
                    steps = [(2 * i + p, t, p) for p in range(2) for t in range(BATCH)]
                    for n, step in enumerate(steps):
                        if n + 1 < len(steps):
                            gate_up(*steps[n + 1])
                        elif not last:
                            gate_up(2 * i + 2, 0, 0)
                        down(*step)

                rotated(pe, lambda: gate_up(0, 0, 0), body)

            @block.scalar
            def _(act):
                act.activation(gated[0][:, 0:1], mem["ident"][:, 0:1], ACT.Silu)
                if quantised:
                    act.wait_ge(s_const, 48)
                weight_split_hi(act, 0, 0, 0)

                def step(u, t, p):
                    for f in range(FPU):
                        r = u * CH + (t * FPU + f)
                        act.wait_ge(s_g, r + 1)
                        wait_apart(act, s_h, r + 1)
                        if quantised:
                            sc = scale_gate[:, bass.ds(u * FPU + f, 1)]
                            act.activation(gated[f][:, :], G[f][:, :], ACT.Silu, scale=sc).then_inc(s_silu, 1)
                        else:
                            act.activation(gated[f][:, :], G[f][:, :], ACT.Silu).then_inc(s_silu, 1)
                        act.wait_ge(s_h, r + 3)
                        act.wait_ge(s_d, (u * BATCH + t) * TPB + TPB)
                        act.activation(in_hi[t % 2][:, f, :], inner[f][:, :], ACT.Copy).then_inc(s_hhi, 1)

                def body(i, last):
                    for p in range(2):
                        for t in range(BATCH):
                            step(2 * i + p, t, p)
                            if t == 1 and not (last and p):
                                act.wait_ge(s_d, (2 * i + p) * (BATCH * TPB) + 2 * TPB)
                                weight_split_hi(act, i + p, 2 * i + p + 1, 1 - p)

                rotated(act, lambda: None, body)

            @block.gpsimd
            def _(pool):
                pool.sem_inc(s_hlo, 2)

                def weight_split_lo(u, p):
                    for m in range(3):
                        pool.wait_ge(s_whi, u * 3 + (m + 1))
                        pool.tensor_tensor(w_lo[p][m][:, :], flat[p][m], f32(w_hi[p][m][:, :]),
                                           ALU.subtract).then_inc(s_wlo, 1)

                weight_split_lo(0, 0)

                def body(i, last):
                    for p in range(2):
                        for t in range(BATCH):
                            for f in range(FPU):
                                r = (2 * i + p) * CH + (t * FPU + f)
                                pool.wait_ge(s_hhi, r + 1)
                                pool.tensor_tensor(in_lo[t % 2][:, f, :], inner[f][:, :],
                                                   f32(in_hi[t % 2][:, f, :]), ALU.subtract).then_inc(s_hlo, 1)
                            if t == 1 and not (last and p):
                                weight_split_lo(2 * i + p + 1, 1 - p)

                rotated(pool, lambda: None, body)

            @block.vector
            def _(dve):
                dve.sem_inc(s_h, NB)
                dve.sem_inc(s_acc, TPB)

                def dequantise(pair, p):
                    dve.wait_ge(s_raw[p], pair * 48 + 48)
                    for m in range(2):
                        dve.tensor_scalar(flat[p][m], raw[p][m][:, :], 128.0, None,
                                          ALU.subtract).then_inc(s_deq, 1)
                    for f in range(FPU):
                        last = dve.scalar_tensor_tensor(flat[p][2][:, f * HID:(f + 1) * HID],
                                                        raw[p][2][:, f * HID:(f + 1) * HID], 128.0,
                                                        scale_down[:, :], op0=ALU.subtract, op1=ALU.mult)
                    last.then_inc(s_deq, 1)

                def inner_chunks(u, t, p):
                    for f in range(FPU):
                        r = u * CH + (t * FPU + f)
                        dve.wait_ge(s_silu, r + 1)
                        dve.wait_ge(s_u, r + 1)
                        dve.wait_ge(s_hlo, r + 1)
                        if quantised:
                            ins = dve.scalar_tensor_tensor(inner[f][:, :], U[f][:, :],
                                                           scale_up[:, bass.ds(u * FPU + f, 1)], gated[f][:, :],
                                                           op0=ALU.mult, op1=ALU.mult)
                        else:
                            ins = dve.tensor_tensor(inner[f][:, :], U[f][:, :], gated[f][:, :], ALU.mult)
                        ins.then_inc(s_h, 1)

                def add(u, t, p, e):
                    for tt in range(TPB):
                        s = (u * BATCH + t) * TPB + tt
                        dve.wait_ge(s_d, s + 2 * TPB + 1)
                        dve.wait_ge(s_acc, s + 1)
                        j = t * TPB + tt
                        row = x_tok[:, j * HID:(j + 1) * HID]
                        if expert_weight is None:
                            ins = dve.tensor_tensor(row, D[tt][:, :], row, ALU.add)
                        else:
                            ins = dve.scalar_tensor_tensor(row, D[tt][:, :],
                                                           expert_weight[:, bass.ds(e + j * EXPERTS, 1)], row,
                                                           op0=ALU.mult, op1=ALU.add)
                        ins.then_inc(s_acc, 1)

                if quantised:
                    dve.wait_ge(s_const, 48)
                    dequantise(0, 0)

                def body(i, last):
                    steps = [(2 * i + p, t, p) for p in range(2) for t in range(BATCH)]
                    for n, (u, t, p) in enumerate(steps):
                        if n + 1 < len(steps):
                            inner_chunks(*steps[n + 1])
                        elif not last:
                            inner_chunks(2 * i + 2, 0, 0)
                        if quantised and t == 0 and not (last and p):
                            dequantise(i + p, 1 - p)
                        add(u, t, p, i)

                rotated(dve, lambda: inner_chunks(0, 0, 0), body)


def until(eng, sem, value):
    if not isinstance(value, int) or value > 0:
        eng.wait_ge(sem, value)


def pooled_attention(nc, mem, x, w, biases):
    x_tok, ident = mem["x_tok"], mem["ident"]
    NAMES = ("q", "qa", "k", "ka", "v")
    SCALE = 1.0 / math.sqrt(HID)
    with ExitStack() as ctx:
        sem = Sems(nc, ctx, "pool")

        def sb(what, shape, dt=F32):
            return ctx.enter_context(nc.sbuf_tensor(f"pool_{what}", shape, dt))

        w_hi = {n: sb(f"w{n}_hi", [P, KC, HID], F32R) for n in NAMES}
        w_lo = {n: sb(f"w{n}_lo", [P, KC, HID], F32R) for n in NAMES}
        h_hi, h_lo = sb("h_hi", [P, KC, SEQ], F32R), sb("h_lo", [P, KC, SEQ], F32R)
        m_hi, m_lo = sb("m_hi", [P, KC, SEQ], F32R), sb("m_lo", [P, KC, SEQ], F32R)
        xn = sb("xn", [P, TPB, HID])
        hf = [sb(f"hf{j}", [P, SEQ]) for j in range(2)]
        qf, kf, vf = sb("qf", [P, KC, SEQ]), sb("kf", [P, KC, SEQ]), sb("vf", [P, KC, SEQ])
        mixed, res = sb("mixed", [P, KC, SEQ]), sb("res", [P, KC, SEQ])
        expw = [sb(f"expw{j}", [P, SEQ]) for j in range(KC)]
        cum = sb("cum", [P, SEQ])
        ones = sb("ones", [P, 1])
        col = sb("col", [P, 7 * KC])
        scaled = sb("scaled", [P, 2 * KC])
        stats, mv = sb("stats", [P, TPB, 6]), sb("mv", [P, TPB, 2])
        var, rstd = sb("var", [P, TPB]), sb("rstd", [P, TPB])
        stats2, mv2 = sb("stats2", [P, TPB, 6]), sb("mv2", [P, TPB, 2])
        var2, rstd2 = sb("var2", [P, TPB]), sb("rstd2", [P, TPB])
        banks = [ctx.enter_context(nc.psum_tensor(f"pool_bank{j}", [P, SEQ], F32)) for j in range(4)]
        turned = [ctx.enter_context(nc.psum_tensor(f"pool_turned{j}", [P, TPB, P], F32)) for j in range(2)]
        back = [ctx.enter_context(nc.psum_tensor(f"pool_back{j}", [P, HID], F32)) for j in range(2)]
        G_, B_, BQ, BQA, BK, BKA, BV = (lambda k, n=n: col[:, n * KC + k:n * KC + k + 1] for n in range(7))
        staging = {"q": qf, "k": kf, "qa": mixed, "v": vf, "ka": res}
        ORDER = ("q", "k", "qa", "v", "ka")

        s_x = sem("x")
        s_col = sem("col")
        s_raw = {n: sem(f"raw_{n}") for n in NAMES}
        s_whi = sem("whi")
        s_wlo_d = sem("wlod")
        s_wlo_p = sem("wlop")
        s_scaled = sem("scaled")
        s_ones = sem("ones")
        s_n1 = sem("n1")
        s_r1 = sem("r1")
        s_t = sem("t")
        s_hf = sem("hf")
        s_hhi, s_hlo = sem("hhi"), sem("hlo")
        s_mm = sem("mm")
        s_ev = sem("ev")
        s_qhi, s_qlo = sem("qhi"), sem("qlo")
        s_mhi, s_mlo = sem("mhi"), sem("mlo")
        s_p1 = sem("p1")
        s_p2 = sem("p2")
        s_b = sem("b")
        s_add = sem("add")
        s_n2 = sem("n2")
        s_r2 = sem("r2")
        N1 = 4 * TPB
        N2 = 4 * TPB
        ROW = 6 * KC
        FRONT, SLOT = 3 * KC, 5 * KC

        def place(kind, b, m):
            if kind in ("v", "ka"):
                return FRONT + b * SLOT + ("v", "ka").index(kind) * KC + m
            n = ("q", "k", "qa").index(kind) * KC + m
            return n if isinstance(b, int) and b == 0 else FRONT + (b - 1) * SLOT + 2 * KC + n

        def in_slots(eng, prologue, slot):
            prologue()
            with eng.Fori(0, BATCH - 1) as i:
                slot(i, i + 1)
            slot(BATCH - 1, None)

        with nc.Block() as block:
            @block.sync
            def _(sp):
                view = x_tok[:, :].rearrange("p (j n) -> p j n", n=HID)

                def row(b):
                    sp.dma_start(view[:, b * TPB:(b + 1) * TPB, :],
                                 x[b, :, :].rearrange("(j p) n -> p j n", p=P)).then_inc(s_x, 16)
                    sp.wait_ge(s_x, (b + 1) * 16)

                def weight(n):
                    sp.dma_start(staging[n][:, :, :].rearrange("p a b -> p (a b)"), w[n]).then_inc(s_raw[n], 16)

                sp.dma_start(col[:, :], biases).then_inc(s_col, 16)
                weight("q")
                row(0)
                for n in ORDER[1:]:
                    weight(n)
                for b in range(1, BATCH):
                    row(b)

            @block.tensor
            def _(pe):
                def weights_ready(n):
                    at = ORDER.index(n)
                    pe.wait_ge(s_wlo_p if at % 2 else s_wlo_d, at // 2 + 1)

                def chunks(kind, b, rh, rl):
                    for m in range(KC):
                        at = place(kind, b, m)
                        until(pe, s_ev, at - 3)
                        product(pe, banks[m][:, :],
                                [(w_hi[kind][:, k, m * P:(m + 1) * P], w_lo[kind][:, k, m * P:(m + 1) * P])
                                 for k in range(KC)],
                                [(rh[:, k, :], rl[:, k, :]) for k in range(KC)]).then_inc(s_mm, 1)

                def turn(b):
                    pe.wait_ge(s_n1, b * N1 + N1)
                    for k in range(KC):
                        until(pe, s_hf, b * KC + (k - 1))
                        for t in range(TPB):
                            last = pe.transpose(turned[k % 2][:, t, :], xn[:, t, k * P:(k + 1) * P], ident[:, :])
                        last.then_inc(s_t, 1)

                def queries_and_keys(b, first=False):
                    if first:
                        weights_ready("q")
                    pe.wait_ge(s_hlo, b * KC + KC)
                    chunks("q", b, h_hi, h_lo)
                    if first:
                        weights_ready("k")
                    chunks("k", b, h_hi, h_lo)

                def query_weights(b):
                    pe.wait_ge(s_qlo, b * KC + KC)
                    chunks("qa", b, m_hi, m_lo)

                def prologue():
                    turn(0)
                    queries_and_keys(0, True)
                    weights_ready("qa")
                    query_weights(0)
                    weights_ready("v")
                    weights_ready("ka")

                def slot(b, nxt):
                    chunks("v", b, h_hi, h_lo)
                    pe.wait_ge(s_mlo, b * KC + KC)
                    chunks("ka", b, m_hi, m_lo)
                    if nxt is not None:
                        turn(nxt)
                        queries_and_keys(nxt)
                    pe.wait_ge(s_p2, b * ROW + (ROW + 1))
                    for t in range(TPB):
                        pe.wait_ge(s_add, b * TPB + (t + 1))
                        for m in range(KC):
                            last = pe.transpose(back[t % 2][:, m * P:(m + 1) * P], res[:, m, t * P:(t + 1) * P],
                                                ident[:, :])
                        last.then_inc(s_b, 1)
                    if nxt is not None:
                        query_weights(nxt)

                in_slots(pe, prologue, slot)

            @block.scalar
            def _(act):
                act.wait_ge(s_col, 16)
                for n, c in ((0, 3), (1, 5)):
                    act.activation(scaled[:, n * KC:(n + 1) * KC], col[:, c * KC:(c + 1) * KC], ACT.Copy,
                                   scale=SCALE).then_inc(s_scaled, 1)
                act.wait_ge(s_scaled, 2)

                def split_hi(n):
                    act.wait_ge(s_raw[n], 16)
                    act.activation(w_hi[n][:, :, :], staging[n][:, :, :], ACT.Copy).then_inc(s_whi, 1)

                def bank(kind, b, m):
                    act.wait_ge(s_mm, place(kind, b, m) + 1)
                    return banks[m][:, :]

                def turn(b, first=False):
                    for k in range(KC):
                        act.wait_ge(s_t, b * KC + (k + 1))
                        until(act, s_hlo, b * KC + (k - 1))
                        act.activation(hf[k % 2][:, :], turned[k % 2][:, :, :].rearrange("p a b -> p (a b)"),
                                       ACT.Identity, bias=B_(k), scale=G_(k)).then_inc(s_hf, 1)
                        act.wait_ge(s_hf, b * KC + (k + 1))
                        if not first:
                            act.wait_ge(s_mm, place("v", b - 1, KC - 1) + 1)
                        act.activation(h_hi[:, k, :], hf[k % 2][:, :], ACT.Copy).then_inc(s_hhi, 1)

                def queries_and_keys(b, first=False):
                    for m in range(KC):
                        src = bank("q", b, m)
                        if not first:
                            act.wait_ge(s_p1, b * ROW)
                        act.activation(qf[:, m, :], src, ACT.Identity, bias=BQ(m)).then_inc(s_ev, 1)
                        act.wait_ge(s_ev, place("q", b, m) + 1)
                        if not first:
                            act.wait_ge(s_mm, place("ka", b - 1, KC - 1) + 1)
                        act.activation(m_hi[:, m, :], qf[:, m, :], ACT.Copy).then_inc(s_qhi, 1)
                    if first:
                        split_hi("qa")
                        split_hi("v")
                    for m in range(KC):
                        act.activation(kf[:, m, :], bank("k", b, m), ACT.Identity, bias=BK(m)).then_inc(s_ev, 1)

                def exponentials(kind, b, column, free_sem, free_value):
                    for m in range(KC):
                        src = bank(kind, b, m)
                        if free_sem is not None:
                            act.wait_ge(free_sem, free_value)
                        act.activation(expw[m][:, :], src, ACT.Exp, bias=scaled[:, column + m:column + m + 1],
                                       scale=SCALE).then_inc(s_ev, 1)

                def split_mixed(b):
                    for m in range(KC):
                        act.wait_ge(s_p1, b * ROW + (m + 1) * 6)
                        act.wait_ge(s_mm, place("qa", b, KC - 1) + 1)
                        act.activation(m_hi[:, m, :], mixed[:, m, :], ACT.Copy).then_inc(s_mhi, 1)

                def prologue():
                    split_hi("q")
                    split_hi("k")
                    turn(0, True)
                    queries_and_keys(0, True)
                    exponentials("qa", 0, 0, None, 0)
                    split_hi("ka")
                    split_mixed(0)

                def slot(b, nxt):
                    for m in range(KC):
                        src = bank("v", b, m)
                        act.wait_ge(s_p2, b * ROW + 1)
                        act.activation(vf[:, m, :], src, ACT.Identity, bias=BV(m)).then_inc(s_ev, 1)
                    exponentials("ka", b, KC, s_p1, b * ROW + ROW)
                    if nxt is not None:
                        turn(nxt)
                        queries_and_keys(nxt)
                        exponentials("qa", nxt, 0, s_p2, b * ROW + (ROW + 1))
                        split_mixed(nxt)

                in_slots(act, prologue, slot)

            @block.gpsimd
            def _(pool):
                def weight_lo(at):
                    n = ORDER[at]
                    pool.wait_ge(s_whi, at + 1)
                    pool.tensor_tensor(w_lo[n][:, :, :], staging[n][:, :, :], f32(w_hi[n][:, :, :]),
                                       ALU.subtract).then_inc(s_wlo_p, 1)

                def split_lo(hi_sem, lo_sem, hi, lo, src, b):
                    for m in range(KC):
                        pool.wait_ge(hi_sem, b * KC + (m + 1))
                        pool.tensor_tensor(lo[:, m, :], src(m), f32(hi[:, m, :]), ALU.subtract).then_inc(lo_sem, 1)

                def root(b, steps, n, src, out, done):
                    pool.wait_ge(steps, b * n + 3 * TPB)
                    pool.tensor_tensor(out[:, :], src[:, :], mem["minus_half"][:, 0:TPB], ALU.pow).then_inc(done, 1)

                def front_lo(b):
                    split_lo(s_hhi, s_hlo, h_hi, h_lo, lambda m: hf[m % 2][:, :], b)
                    split_lo(s_qhi, s_qlo, m_hi, m_lo, lambda m: qf[:, m, :], b)

                def prologue():
                    root(0, s_n1, N1, var, rstd, s_r1)
                    split_lo(s_hhi, s_hlo, h_hi, h_lo, lambda m: hf[m % 2][:, :], 0)
                    weight_lo(1)
                    split_lo(s_qhi, s_qlo, m_hi, m_lo, lambda m: qf[:, m, :], 0)
                    weight_lo(3)
                    split_lo(s_mhi, s_mlo, m_hi, m_lo, lambda m: mixed[:, m, :], 0)

                def slot(b, nxt):
                    if nxt is not None:
                        root(nxt, s_n1, N1, var, rstd, s_r1)
                        front_lo(nxt)
                    root(b, s_n2, N2, var2, rstd2, s_r2)
                    if nxt is not None:
                        split_lo(s_mhi, s_mlo, m_hi, m_lo, lambda m: mixed[:, m, :], nxt)

                in_slots(pool, prologue, slot)

            @block.vector
            def _(dve):
                dve.sem_inc(s_p2, 1)
                dve.sem_inc(s_add, 2)

                def row(b, t):
                    return x_tok[:, (b * TPB + t) * HID:(b * TPB + t + 1) * HID] if isinstance(b, int) else \
                        x_tok[:, bass.ds(b * (TPB * HID) + t * HID, HID)]

                def weight_lo(at):
                    n = ORDER[at]
                    dve.wait_ge(s_whi, at + 1)
                    dve.tensor_tensor(w_lo[n][:, :, :], staging[n][:, :, :], f32(w_hi[n][:, :, :]),
                                      ALU.subtract).then_inc(s_wlo_d, 1)

                def first_norm(b, first=False):
                    wait_apart(dve, s_x, b * 16 + 16)
                    at = b * N1
                    for t in range(TPB):
                        dve.bn_stats(stats[:, t, :], row(b, t)).then_inc(s_n1, 1)
                    for t in range(TPB):
                        wait_apart(dve, s_n1, at + (t + 1))
                        dve.bn_aggr(mv[:, t, :], stats[:, t, :]).then_inc(s_n1, 1)
                    for t in range(TPB):
                        dve.wait_ge(s_n1, at + (TPB + t + 1))
                        dve.tensor_scalar(var[:, t:t + 1], mv[:, t, 1:2], LN_EPS, None, ALU.add).then_inc(s_n1, 1)
                    dve.wait_ge(s_r1, b + 1)
                    if not first:
                        dve.wait_ge(s_t, b * KC)
                    for t in range(TPB):
                        dve.tensor_scalar(xn[:, t, :], row(b, t), mv[:, t, 0:1], rstd[:, t:t + 1],
                                          ALU.subtract, ALU.mult).then_inc(s_n1, 1)

                def pooling(kind, b, m, sem_, at, gain, by, out):
                    chain = Chain(dve, sem_, at)
                    dve.wait_ge(s_ev, place(kind, b, m) + 1)
                    e = expw[m]
                    chain.link(dve.tensor_tensor_scan(cum[:, :], ones[:, :].to_broadcast([P, SEQ]), e[:, :], 0.0, ALU.mult, ALU.add))
                    chain.link(dve.reciprocal(cum[:, :], cum[:, :]))
                    chain.link(dve.tensor_tensor(e[:, :], e[:, :], cum[:, :], ALU.mult))
                    chain.link(dve.tensor_tensor(e[:, :], e[:, :], gain, ALU.mult))
                    chain.link(dve.tensor_tensor_scan(cum[:, :], ones[:, :].to_broadcast([P, SEQ]), e[:, :], 0.0, ALU.mult, ALU.add))
                    chain.link(dve.tensor_tensor(out, cum[:, :], by, ALU.mult))

                def first_pooling(b, first=False):
                    if not first:
                        dve.wait_ge(s_mlo, b * KC)
                    for m in range(KC):
                        pooling("qa", b, m, s_p1, b * ROW + 6 * m, qf[:, m, :], kf[:, m, :], mixed[:, m, :])

                def second_pooling(b):
                    dve.wait_ge(s_add, b * TPB + 2)
                    for m in range(KC):
                        pooling("ka", b, m, s_p2, b * ROW + (6 * m + 1), mixed[:, m, :], vf[:, m, :], res[:, m, :])

                def second_norm(b):
                    at = b * N2
                    for t in range(TPB):
                        dve.wait_ge(s_b, b * TPB + (t + 1))
                        dve.tensor_tensor(row(b, t), row(b, t), back[t % 2][:, :], ALU.add).then_inc(s_add, 1)
                        wait_apart(dve, s_add, b * TPB + (t + 3))
                        dve.bn_stats(stats2[:, t, :], row(b, t)).then_inc(s_n2, 1)
                    for t in range(TPB):
                        wait_apart(dve, s_n2, at + (t + 1))
                        dve.bn_aggr(mv2[:, t, :], stats2[:, t, :]).then_inc(s_n2, 1)
                    for t in range(TPB):
                        dve.wait_ge(s_n2, at + (TPB + t + 1))
                        dve.tensor_scalar(var2[:, t:t + 1], mv2[:, t, 1:2], LN_EPS, None, ALU.add).then_inc(s_n2, 1)
                    dve.wait_ge(s_r2, b + 1)
                    for t in range(TPB):
                        dve.tensor_scalar(row(b, t), row(b, t), mv2[:, t, 0:1], rstd2[:, t:t + 1],
                                          ALU.subtract, ALU.mult).then_inc(s_n2, 1)

                def prologue():
                    dve.memset(ones[:, :], 1.0).then_inc(s_ones, 1)
                    dve.wait_ge(s_ones, 1)
                    weight_lo(0)
                    first_norm(0, True)
                    weight_lo(2)
                    first_pooling(0, True)
                    weight_lo(4)

                def slot(b, nxt):
                    if nxt is not None:
                        first_norm(nxt)
                    second_pooling(b)
                    second_norm(b)
                    if nxt is not None:
                        first_pooling(nxt)

                in_slots(dve, prologue, slot)


def small_projection(nc, name, mem, w, n, by_token, n_tok, by_feature=None):
    xT_hi, xT_lo, ident = mem["xT_hi"], mem["xT_lo"], mem["ident"]
    with ExitStack() as ctx:
        sem = Sems(nc, ctx, name)
        w_f = ctx.enter_context(nc.sbuf_tensor(f"{name}_w", [P, KC, P], F32))
        w_hi = ctx.enter_context(nc.sbuf_tensor(f"{name}_w_hi", [P, KC, P], F32R))
        w_lo = ctx.enter_context(nc.sbuf_tensor(f"{name}_w_lo", [P, KC, P], F32R))
        rows = ctx.enter_context(nc.sbuf_tensor(f"{name}_rows", [P, SEQ], F32))
        prod = ctx.enter_context(nc.psum_tensor(f"{name}_prod", [P, SEQ], F32))
        turned = ctx.enter_context(nc.psum_tensor(f"{name}_turned", [P, TPB, P], F32))
        s_zero, s_w, s_hi, s_lo = sem("zero"), sem("w"), sem("hi"), sem("lo")
        s_p = sem("p")
        s_r = sem("r")
        s_t = sem("t")
        s_c = sem("c")
        s_out = sem("out")
        with nc.Block() as block:
            @block.sync
            def _(sp):
                sp.wait_ge(s_zero, 1)
                sp.dma_start(w_f[:, :, 0:n], w.rearrange("p (k n) -> p k n", n=n)).then_inc(s_w, 16)
                if by_feature is not None:
                    with sp.Fori(0, BATCH) as b:
                        wait_apart(sp, s_r, b + 1)
                        sp.dma_start(by_feature[:, bass.ds(b * SEQ, SEQ)], rows[0:n, :]).then_inc(s_out, 16)
                    sp.wait_ge(s_out, 16 * BATCH)

            @block.vector
            def _(dve):
                dve.memset(w_f[:, :, :], 0.0).then_inc(s_zero, 1)
                dve.wait_ge(s_hi, 1)
                dve.tensor_tensor(w_lo[:, :, :], w_f[:, :, :], f32(w_hi[:, :, :]), ALU.subtract).then_inc(s_lo, 1)
                with dve.Fori(0, BATCH) as b:
                    wait_apart(dve, s_t, b + 1)
                    dve.tensor_copy(by_token[:, bass.ds(b * (TPB * n_tok), TPB * n_tok)].rearrange("p (t n) -> p t n", n=n_tok),
                                    turned[:, :, 0:n_tok]).then_inc(s_c, 1)

            @block.scalar
            def _(act):
                act.wait_ge(s_w, 16)
                act.activation(w_hi[:, :, :], w_f[:, :, :], ACT.Copy).then_inc(s_hi, 1)
                for b in range(BATCH):
                    act.wait_ge(s_p, b + 1)
                    if b:
                        act.wait_ge(s_t, b)
                        if by_feature is not None:
                            act.wait_ge(s_out, 16 * b)
                    act.activation(rows[:, :], prod[:, :], ACT.Copy).then_inc(s_r, 1)

            @block.tensor
            def _(pe):
                pe.wait_ge(s_lo, 1)
                for b in range(BATCH):
                    cols = slice(b * SEQ, (b + 1) * SEQ)
                    if b:
                        pe.wait_ge(s_r, b)
                    product(pe, prod[:, :], [(w_hi[:, k, :], w_lo[:, k, :]) for k in range(KC)],
                            [(xT_hi[:, k, cols], xT_lo[:, k, cols]) for k in range(KC)]).then_inc(s_p, 1)
                    pe.wait_ge(s_r, b + 1)
                    if b:
                        pe.wait_ge(s_c, b)
                    for t in range(TPB):
                        last = pe.transpose(turned[:, t, :], rows[:, t * P:(t + 1) * P], ident[:, :])
                    last.then_inc(s_t, 1)


def lagged_attention(nc, mem, w_heads, w_out, conv, norm_w, tables, band, lag_a, lag_b, saved):
    x_tok, xT_hi, xT_lo, ident = mem["x_tok"], mem["xT_hi"], mem["xT_lo"], mem["ident"]
    PAD = LAGS - 1
    BAND = P + PAD
    STEPS = HEADS * BATCH
    CONV = LAGS
    with ExitStack() as ctx:
        sem = Sems(nc, ctx, "lag")

        def sb(what, shape, dt=F32):
            return ctx.enter_context(nc.sbuf_tensor(f"lag_{what}", shape, dt))

        def bank(what, shape=(P, SEQ)):
            return ctx.enter_context(nc.psum_tensor(f"lag_{what}", list(shape), F32))

        raw, raw_out = sb("raw", [P, 4, KC, HDIM]), sb("raw_out", [P, HID])
        w_hi = [sb(f"w_hi{p}", [P, 4, KC, HDIM], F32R) for p in range(2)]
        w_lo = [sb(f"w_lo{p}", [P, 4, KC, HDIM], F32R) for p in range(2)]
        wo_hi = [sb(f"wo_hi{p}", [P, HID], F32R) for p in range(2)]
        wo_lo = [sb(f"wo_lo{p}", [P, HID], F32R) for p in range(2)]
        act_in = [[sb(f"silu{n}{p}", [P, PAD + SEQ]) for p in range(2)] for n in "qkv"]
        cq, ck = sb("cq", [P, SEQ]), sb("ck", [P, SEQ])
        cv = [sb(f"cv{p}", [P, SEQ]) for p in range(2)]
        swapped = [sb(f"swapped{n}", [P, SEQ]) for n in "qk"]
        rot_q = [sb(f"rot_q{p}", [P, SEQ + PAD]) for p in range(2)]
        rot_k = [sb(f"rot_k{p}", [P, SEQ]) for p in range(2)]
        squares = sb("squares", [P, 2, SEQ])
        b_row = sb("b_row", [P, SEQ + PAD])
        gate = sb("gate", [P, TPB, BAND])
        prob = sb("prob", [P, TPB, BAND])
        values = sb("values", [P, TPB, HDIM])
        o_tok = sb("o_tok", [P, TPB, HDIM])
        y = sb("y", [P, SEQ])
        y_hi, y_lo = sb("y_hi", [P, SEQ], F32R), sb("y_lo", [P, SEQ], F32R)
        cos_sin = sb("cos_sin", [P, 2, SEQ])
        band_t, conv_t, norm_t = sb("band", [P, BAND]), sb("conv", [P, HEADS * 3 * LAGS]), sb("norm", [P, HEADS])
        norm2 = sb("norm2", [P, 2 * TPB])
        rnorm = [sb(f"rnorm{p}", [P, 2 * TPB]) for p in range(2)]
        ones = sb("ones", [P, 1])
        ssum = mem["ssum"]

        A, B = bank("A"), bank("B")
        scores = bank("scores", (P, TPB, 256))
        NORM_AT = 160
        VT, O = bank("VT"), bank("O")
        OP = [bank(f"OP{j}") for j in range(2)]

        s_const = sem("const")
        s_init = sem("init")
        s_save = sem("save")
        s_zero = sem("zero")
        s_raw = sem("raw")
        s_whi, s_wlo = sem("whi"), sem("wlo")
        s_q, s_k, s_v, s_z = sem("q"), sem("k"), sem("v"), sem("z")
        s_sq, s_sk, s_sv, s_sz = sem("sq"), sem("sk"), sem("sv"), sem("sz")
        s_cqk = sem("cqk")
        s_cv = sem("cv")
        s_swap = [sem(f"swap_{n}") for n in "qk"]
        s_cos = sem("cos")
        s_rot = sem("rot")
        s_sqr = sem("sqr")
        s_s = sem("s")
        s_n2 = sem("n2")
        s_rn = sem("rn")
        s_b = sem("b")
        s_gate = sem("gate")
        s_p1 = sem("p1")
        s_p2 = sem("p2")
        s_vt, s_val = sem("vt"), sem("val")
        s_o, s_otok, s_ot = sem("o"), sem("otok"), sem("ot")
        s_osq = sem("osq")
        s_y, s_yhi, s_ylo = sem("y"), sem("yhi"), sem("ylo")
        s_op = sem("op")
        s_acc = sem("acc")

        def slots(eng, task):
            def slot(i, c):
                steps = []
                for lag in range(4):
                    ok = not isinstance(i, int) or 0 <= 8 * i + c - lag < STEPS
                    steps.append(Step(i, c - lag) if ok else None)
                task(*steps)

            for c in range(3):
                slot(0, c)
            with eng.Fori(0, STEPS // 8 - 1) as i:
                for c in range(3, 11):
                    slot(i, c)
            for c in range(3, 11):
                slot(STEPS // 8 - 1, c)

        class Step:

            def __init__(self, i, c):
                if not isinstance(i, int):
                    self.s, self.head = i * 8 + c, i * 2 + c // BATCH
                else:
                    self.s, self.head = 8 * i + c, 2 * i + c // BATCH
                self.b, self.buf, self.wbuf = c % BATCH, c % 2, (c // BATCH) % 2
                self.known = isinstance(i, int)

            def past(self, eng, sem_, per=1, back=1):
                until(eng, sem_, (self.s - (back - 1)) * per)

            def past_apart(self, eng, sem_):
                self.past(eng, sem_)
                if not self.known:
                    eng.nop(nofuse=True)

            def now(self, eng, sem_, per=1, part=None):
                eng.wait_ge(sem_, self.s * per + (per if part is None else part))

        def next_head(st):
            return not st.known or st.head + 1 < HEADS

        def at(t, col):
            return t[:, bass.ds(col, 1)]

        with nc.Block() as block:
            @block.sync
            def _(sp):
                def load(head):
                    one = slice(head, head + 1) if isinstance(head, int) else bass.ds(head, 1)
                    sp.dma_start(raw[:, :, :, :].rearrange("p a k n -> p (a k n)"),
                                 w_heads[one, :, :].rearrange("a p n -> (a p) n")).then_inc(s_raw, 16)
                    sp.dma_start(raw_out[:, :], w_out[one, :, :].rearrange("a p n -> (a p) n")).then_inc(s_raw, 16)

                load(0)
                sp.dma_start(saved, x_tok[:, :]).then_inc(s_save, 16)
                for t, src in ((cos_sin[:, :, :].rearrange("p a n -> p (a n)"), tables), (band_t[:, :], band),
                               (conv_t[:, :], conv), (norm_t[:, :], norm_w)):
                    sp.dma_start(t, src).then_inc(s_const, 16)

                def task(f, l1, l2, l3):
                    if f:
                        if f.b == 0 and next_head(f):
                            wait_apart(sp, s_wlo, f.head * 5 + 5)
                            load(f.head + 1)
                        f.past_apart(sp, s_gate)
                        row = f.head + HEADS
                        src = lag_b[slice(row, row + 1) if isinstance(row, int) else bass.ds(row, 1),
                                    f.b * SEQ:(f.b + 1) * SEQ]
                        sp.dma_start(b_row[:, 0:SEQ], src.to_broadcast([P, SEQ])).then_inc(s_b, 16)
                        for n, c in enumerate((cq, ck)):
                            f.now(sp, s_cqk, 8, 7 + n)
                            if not f.known:
                                sp.nop(nofuse=True)
                            f.past(sp, s_rot, 4)
                            for half in range(2):
                                to, of = half * 64, 64 - half * 64
                                sp.dma_start(swapped[n][to:to + 64, :], c[of:of + 64, :]).then_inc(s_swap[n], 16)

                slots(sp, task)

            @block.tensor
            def _(pe):
                def projection(st, n, out, done):
                    cols = slice(st.b * SEQ, (st.b + 1) * SEQ)
                    product(pe, out[:, :],
                            [(w_hi[st.wbuf][:, n, k, :], w_lo[st.wbuf][:, n, k, :]) for k in range(KC)],
                            [(xT_hi[:, k, cols], xT_lo[:, k, cols]) for k in range(KC)]).then_inc(done, 1)

                def task(f, l1, l2, l3):
                    if f:
                        if f.b == 0:
                            pe.wait_ge(s_wlo, f.head * 5 + 5)
                        f.past(pe, s_sv)
                        projection(f, 0, A, s_q)
                        if l3:
                            l3.now(pe, s_sz)
                        projection(f, 1, B, s_k)
                    if l2:
                        l2.now(pe, s_p2)
                        l2.now(pe, s_val)
                        l2.past(pe, s_y)
                        for t in range(TPB):
                            out = O[:, t * HDIM:(t + 1) * HDIM]
                            last = pe.matmul(out, prob[:, t, 0:P], values[:, t, :], start=True, stop=True)
                            if t:
                                last = pe.matmul(out[0:PAD, :], prob[:, t - 1, P:BAND], values[:, t - 1, :],
                                                 start=False, stop=True, skip_group_check=True)
                        last.then_inc(s_o, 1)
                    if f:
                        f.now(pe, s_sq)
                        projection(f, 2, A, s_v)
                    if l2:
                        l2.now(pe, s_otok)
                        for t in range(TPB):
                            last = pe.transpose(O[:, t * P:(t + 1) * P], o_tok[:, t, :], ident[:, :])
                        last.then_inc(s_ot, 1)
                        if f:
                            f.now(pe, s_sk)
                        elif l1:
                            l1.now(pe, s_sk)
                        if l3:
                            l3.now(pe, s_sz)
                        projection(l2, 3, B, s_z)
                    if l3:
                        l3.now(pe, s_ylo)
                        for t in range(TPB):
                            pe.wait_ge(s_acc, l3.s * TPB + (t + 1))
                            tok = slice(t * P, (t + 1) * P)
                            product(pe, OP[t % 2][:, :], [(y_hi[:, tok], y_lo[:, tok])],
                                    [(wo_hi[l3.wbuf][:, :], wo_lo[l3.wbuf][:, :])]).then_inc(s_op, 1)
                    if l1:
                        l1.now(pe, s_sqr, 2)
                        l1.past(pe, s_p1)
                        for n in range(2):
                            for t in range(TPB):
                                col = NORM_AT + n * TPB + t
                                pe.matmul(scores[:, 0, col:col + 1], squares[:, n, t * P:(t + 1) * P], ones[:, :],
                                          start=True, stop=True)
                        l1.now(pe, s_rot, 4)
                        for t in range(TPB):
                            last = pe.matmul(scores[:, t, 0:BAND], rot_k[l1.buf][:, t * P:(t + 1) * P],
                                             rot_q[l1.buf][:, t * P:t * P + BAND], start=True, stop=True)
                        last.then_inc(s_s, 1)
                        l1.now(pe, s_cv, CONV)
                        l1.past(pe, s_val)
                        for t in range(TPB):
                            last = pe.transpose(VT[:, t * P:(t + 1) * P], cv[l1.buf][:, t * P:(t + 1) * P], ident[:, :])
                        last.then_inc(s_vt, 1)

                pe.wait_ge(s_init, 2)
                slots(pe, task)

            @block.scalar
            def _(act):
                def split_hi(head, buf, mats):
                    act.wait_ge(s_raw, head * 32 + 32)
                    for n in mats:
                        if n < 4:
                            act.activation(w_hi[buf][:, n, :, :], raw[:, n, :, :], ACT.Copy).then_inc(s_whi, 1)
                        else:
                            act.activation(wo_hi[buf][:, :], raw_out[:, :], ACT.Copy).then_inc(s_whi, 1)

                split_hi(0, 0, range(5))
                act.wait_ge(s_init, 2)

                def task(f, l1, l2, l3):
                    if f:
                        for n, (done, src, out) in enumerate(((s_q, A, s_sq), (s_k, B, s_sk))):
                            f.now(act, done)
                            f.past(act, s_cqk, 8, 2)
                            act.activation(act_in[n][f.buf][:, PAD:], src[:, :], ACT.Silu).then_inc(out, 1)
                    if l2:
                        l2.now(act, s_o)
                        l2.past(act, s_ot)
                        l2.past(act, s_osq)
                        for t in range(TPB):
                            last = act.activation(o_tok[:, t, :], O[:, t * HDIM:(t + 1) * HDIM], ACT.Copy,
                                                  scale=rnorm[l2.buf][:, t:t + 1])
                        last.then_inc(s_otok, 1)
                    if f:
                        f.now(act, s_v)
                        f.past(act, s_cv, CONV, 2)
                        act.activation(act_in[2][f.buf][:, PAD:], A[:, :], ACT.Silu).then_inc(s_sv, 1)
                    if l1:
                        l1.now(act, s_b, 16)
                        l1.past_apart(act, s_p1)
                        for t in range(TPB):
                            tok = l1.b * TPB + t
                            last = act.activation(gate[:, t, :], b_row[:, t * P:t * P + BAND], ACT.Tanh,
                                                  scale=at(lag_a, l1.head + tok * HEADS))
                        last.then_inc(s_gate, 1)
                    if l2:
                        l2.now(act, s_otok)
                        l2.past_apart(act, s_ylo)
                        for t in range(TPB):
                            tok = l2.b * TPB + t
                            last = act.activation(y[:, t * P:(t + 1) * P], o_tok[:, t, :], ACT.Square,
                                                  accum_out=at(ssum, l2.head + tok * HEADS))
                        last.then_inc(s_osq, 1)
                        l2.now(act, s_z)
                        l2.now(act, s_osq)
                        act.activation(y[:, :], B[:, :], ACT.Silu).then_inc(s_sz, 1)
                        l2.now(act, s_y)
                        l2.past(act, s_op, TPB)
                        act.activation(y_hi[:, :], y[:, :], ACT.Copy).then_inc(s_yhi, 1)
                    if f:
                        f.past(act, s_s)
                        for n, c in enumerate((cq, ck)):
                            f.now(act, s_cqk, 8, 7 + n)
                            act.activation(squares[:, n, :], c[:, :], ACT.Square).then_inc(s_sqr, 1)
                    if l1:
                        l1.now(act, s_vt)
                        l1.now(act, s_rn)
                        l1.past(act, s_o)
                        for t in range(TPB):
                            last = act.activation(values[:, t, :], VT[:, t * P:(t + 1) * P], ACT.Copy,
                                                  scale=rnorm[l1.buf][:, TPB + t:TPB + t + 1])
                        last.then_inc(s_val, 1)
                    if f and f.b >= 2 and next_head(f):
                        if f.b == 3:
                            f.past(act, s_op, TPB, 3)
                        else:
                            f.past(act, s_z, 1, 3)
                        split_hi(f.head + 1, 1 - f.wbuf, range(3) if f.b == 2 else range(3, 5))

                slots(act, task)

            @block.gpsimd
            def _(pool):
                def split_lo(head, buf, mats):
                    for n in mats:
                        pool.wait_ge(s_whi, head * 5 + (n + 1))
                        if n < 4:
                            pool.tensor_tensor(w_lo[buf][:, n, :, :], raw[:, n, :, :], f32(w_hi[buf][:, n, :, :]),
                                               ALU.subtract).then_inc(s_wlo, 1)
                        else:
                            pool.tensor_tensor(wo_lo[buf][:, :], raw_out[:, :], f32(wo_hi[buf][:, :]),
                                               ALU.subtract).then_inc(s_wlo, 1)

                split_lo(0, 0, range(5))
                pool.wait_ge(s_const, 64)

                def task(f, l1, l2, l3):
                    if f:
                        f.past(pool, s_s, 1, 2)
                        for n, (c, out) in enumerate(((cq, rot_q[f.buf][:, 0:SEQ]), (ck, rot_k[f.buf][:, :]))):
                            f.now(pool, s_cqk, 8, 7 + n)
                            pool.tensor_tensor(out, c[:, :], cos_sin[:, 0, :], ALU.mult).then_inc(s_cos, 1)
                    if l2:
                        l2.now(pool, s_yhi)
                        pool.tensor_tensor(y_lo[:, :], y[:, :], f32(y_hi[:, :]), ALU.subtract).then_inc(s_ylo, 1)
                    if l1:
                        l1.now(pool, s_n2)
                        pool.tensor_tensor(rnorm[l1.buf][:, :], norm2[:, :], mem["minus_half"][:, 0:2 * TPB],
                                           ALU.pow).then_inc(s_rn, 1)
                        l1.now(pool, s_p1)
                        pool.tensor_tensor(prob[:, :, :], prob[:, :, :],
                                           band_t[:, :].unsqueeze(1).to_broadcast([P, TPB, BAND]),
                                           ALU.mult).then_inc(s_p2, 1)
                    if f and f.b >= 2 and next_head(f):
                        split_lo(f.head + 1, 1 - f.wbuf, range(3) if f.b == 2 else range(3, 5))

                slots(pool, task)

            @block.vector
            def _(dve):
                dve.sem_inc(s_acc, 2)
                for n in range(3):
                    for p in range(2):
                        dve.memset(act_in[n][p][:, 0:PAD], 0.0)
                for p in range(2):
                    dve.memset(rot_q[p][:, SEQ:], 0.0)
                dve.memset(b_row[:, SEQ:], 0.0)
                dve.memset(ones[:, :], 1.0).then_inc(s_init, 1)
                dve.tensor_scalar(lag_a, lag_a, 0.5, None, ALU.mult).then_inc(s_init, 1)
                dve.wait_ge(s_save, 16)
                dve.memset(x_tok[:, :], 0.0).then_inc(s_zero, 1)
                dve.wait_ge(s_const, 64)

                def tap(n, st, src, out, j):
                    wj = at(conv_t, st.head * (3 * LAGS) + (n * LAGS + j))
                    x = src[:, j:j + SEQ]
                    if j == 0:
                        return dve.tensor_scalar(out, x, wj, None, ALU.mult)
                    return dve.scalar_tensor_tensor(out, x, wj, out, op0=ALU.mult, op1=ALU.add)

                def task(f, l1, l2, l3):
                    if f:
                        f.now(dve, s_sq)
                        for n in range(2):
                            f.past(dve, s_swap[n], 32)
                        f.past(dve, s_cos, 2)
                        f.past(dve, s_sqr, 2)
                        for j in range(LAGS):
                            for n, out in enumerate((cq, ck)):
                                if j == 0 and n == 1:
                                    f.now(dve, s_sk)
                                if j:
                                    f.now(dve, s_cqk, 8, 2 * j + n - 1)
                                tap(n, f, act_in[n][f.buf], out[:, :], j).then_inc(s_cqk, 1)
                    if f:
                        f.now(dve, s_sv)
                        for j in range(LAGS):
                            if j:
                                f.now(dve, s_cv, CONV, j)
                            tap(2, f, act_in[2][f.buf], cv[f.buf][:, :], j).then_inc(s_cv, 1)
                    if l2:
                        l2.now(dve, s_ot)
                        l2.now(dve, s_sz)
                        dve.scalar_tensor_tensor(y[:, :], O[:, :], at(norm_t, l2.head), y[:, :],
                                                 op0=ALU.mult, op1=ALU.mult).then_inc(s_y, 1)
                    if l3:
                        for t in range(TPB):
                            row = x_tok[:, (l3.b * TPB + t) * HID:(l3.b * TPB + t + 1) * HID]
                            dve.wait_ge(s_op, l3.s * TPB + (t + 1))
                            dve.wait_ge(s_acc, l3.s * TPB + (t + 1))
                            dve.tensor_tensor(row, OP[t % 2][:, :], row, ALU.add).then_inc(s_acc, 1)
                    if f:
                        for n, (rot, sw) in enumerate(((rot_q[f.buf][:, 0:SEQ], swapped[0]),
                                                       (rot_k[f.buf][:, :], swapped[1]))):
                            f.now(dve, s_swap[n], 32)
                            dve.tensor_tensor(sw[:, :], sw[:, :], cos_sin[:, 1, :], ALU.mult).then_inc(s_rot, 1)
                        for n, (rot, sw) in enumerate(((rot_q[f.buf][:, 0:SEQ], swapped[0]),
                                                       (rot_k[f.buf][:, :], swapped[1]))):
                            f.now(dve, s_cos, 2, n + 1)
                            f.now(dve, s_rot, 4, n + 1)
                            dve.tensor_tensor(rot, rot, sw[:, :], ALU.add).then_inc(s_rot, 1)
                    if l1:
                        l1.now(dve, s_s)
                        l1.past(dve, s_rn)
                        dve.tensor_scalar(norm2[:, :], scores[:, 0, NORM_AT:NORM_AT + 2 * TPB], 1e-24, None,
                                          ALU.max).then_inc(s_n2, 1)
                        l1.now(dve, s_gate)
                        l1.past(dve, s_o)
                        dve.scalar_tensor_tensor(prob[:, :, :], gate[:, :, :], 1.0, scores[:, :, 0:BAND],
                                                 op0=ALU.add, op1=ALU.mult).then_inc(s_p1, 1)

                slots(dve, task)

    with ExitStack() as ctx:
        sem = Sems(nc, ctx, "rms")
        res = ctx.enter_context(nc.sbuf_tensor("rms_res", [P, NTT * HID], F32))
        ms = ctx.enter_context(nc.sbuf_tensor("rms_ms", [P, NTT], F32))
        s_load, s_own, s_root = sem("load"), sem("own"), sem("root")
        with nc.Block() as block:
            @block.sync
            def _(sp):
                sp.dma_start(res[:, :], saved).then_inc(s_load, 16)

            @block.gpsimd
            def _(pool):
                pool.wait_ge(s_own, 2)
                pool.tensor_tensor(ms[:, :], ms[:, :], mem["minus_half"][:, 0:NTT], ALU.pow).then_inc(s_root, 1)

            @block.vector
            def _(dve):
                chain = Chain(dve, s_own)
                chain.link(dve.tensor_reduce(ms[:, :], ssum[:, :].rearrange("p (j h) -> p j h", h=HEADS), AX.X, ALU.add))
                dve.tensor_scalar(ms[:, :], ms[:, :], 1.0 / (HEADS * HDIM), RMS_EPS, ALU.mult, ALU.add).then_inc(s_own, 1)
                dve.wait_ge(s_root, 1)
                dve.wait_ge(s_load, 16)
                with dve.Fori(0, NTT) as j:
                    row = x_tok[:, bass.ds(j * HID, HID)]
                    dve.scalar_tensor_tensor(row, row, ms[:, bass.ds(j, 1)], res[:, bass.ds(j * HID, HID)],
                                             op0=ALU.mult, op1=ALU.add)


def route(nc, logits, temperature, number):
    CENTER, LOWER, UPPER = 1.0 / math.e, 0.5 - math.log(4.0 / 3.0), 0.5
    E = EXPERTS
    with ExitStack() as ctx:
        sem = Sems(nc, ctx, "route")

        def tile(what):
            t = ctx.enter_context(nc.sbuf_tensor(f"route_{what}", [P, NTT * E], F32))
            return t[:, :].rearrange("p (j e) -> p j e", e=E)

        def token(what):
            t = ctx.enter_context(nc.sbuf_tensor(f"route_{what}", [P, NTT], F32))
            return t[:, :]

        inh, dist, zone, wz, fb = tile("inh"), tile("dist"), tile("zone"), tile("wz"), tile("fb")
        key, picked, both, left = tile("key"), tile("picked"), tile("both"), tile("left")
        best, total, none, some = token("best"), token("total"), token("none"), token("some")
        num = ctx.enter_context(nc.sbuf_tensor("route_num", [P, E], F32))
        temp = ctx.enter_context(nc.sbuf_tensor("route_temp", [P, 1], F32))
        inv_t = ctx.enter_context(nc.sbuf_tensor("route_inv_t", [P, 1], F32))
        s_in, s_own, s_t, s_inh, s_dist, s_exp = (sem(n) for n in ("in", "own", "t", "inh", "dist", "exp"))
        out = logits.rearrange("p (j e) -> p j e", e=E)
        over = lambda t: t.unsqueeze(2).to_broadcast([P, NTT, E])
        with nc.Block() as block:
            @block.sync
            def _(sp):
                sp.dma_start(num[:, :], number).then_inc(s_in, 16)
                sp.dma_start(temp[:, :], temperature.rearrange("(a n) -> a n", a=1).to_broadcast([P, 1])).then_inc(s_in, 16)

            @block.scalar
            def _(act):
                act.wait_ge(s_t, 1)
                act.activation(inh, out, ACT.Sigmoid, scale=inv_t[:, :]).then_inc(s_inh, 1)
                act.wait_ge(s_dist, 1)
                act.activation(dist, dist, ACT.Abs).then_inc(s_exp, 1)
                act.wait_ge(s_exp, 1)
                act.activation(wz, dist, ACT.Exp, scale=-1.0 / 0.1).then_inc(s_exp, 1)
                act.activation(fb, dist, ACT.Exp, scale=-1.0 / 0.3).then_inc(s_exp, 1)

            @block.vector
            def _(dve):
                dve.wait_ge(s_in, 32)
                dve.reciprocal(inv_t[:, :], temp[:, :]).then_inc(s_t, 1)
                step = Chain(dve, s_own).link
                dve.wait_ge(s_inh, 1)
                dve.tensor_scalar(dist, inh, CENTER, None, ALU.subtract).then_inc(s_dist, 1)
                step(dve.tensor_scalar(zone, inh, LOWER, None, ALU.is_ge))
                step(dve.scalar_tensor_tensor(zone, inh, UPPER, zone, op0=ALU.is_le, op1=ALU.mult))
                dve.wait_ge(s_exp, 3)
                step(dve.tensor_tensor(wz, wz, zone, ALU.mult))
                step(dve.tensor_reduce(total, wz, AX.X, ALU.add))
                step(dve.tensor_scalar(none, total, 1e-8, None, ALU.is_lt))
                step(dve.tensor_copy(left, fb))
                for n in range(2):
                    step(dve.tensor_reduce(best, left, AX.X, ALU.max))
                    step(dve.tensor_tensor(key, left, over(best), ALU.is_ge))
                    step(dve.scalar_tensor_tensor(key, key, -float(E),
                                                  num[:, :].unsqueeze(1).to_broadcast([P, NTT, E]),
                                                  op0=ALU.mult, op1=ALU.add))
                    step(dve.tensor_reduce(best, key, AX.X, ALU.min))
                    step(dve.tensor_tensor(picked, key, over(best), ALU.is_equal))
                    if n == 0:
                        step(dve.tensor_copy(both, picked))
                        step(dve.scalar_tensor_tensor(left, picked, -4.0, left, op0=ALU.mult, op1=ALU.add))
                    else:
                        step(dve.tensor_tensor(both, both, picked, ALU.add))
                step(dve.tensor_tensor(fb, fb, both, ALU.mult))
                step(dve.tensor_reduce(total, fb, AX.X, ALU.add))
                step(dve.tensor_scalar(total, total, 1e-8, None, ALU.max))
                step(dve.reciprocal(total, total))
                step(dve.tensor_tensor(fb, fb, over(total), ALU.mult))
                step(dve.tensor_scalar(some, none, -1.0, 1.0, ALU.mult, ALU.add))
                step(dve.tensor_tensor(wz, wz, over(some), ALU.mult))
                step(dve.tensor_tensor(fb, fb, over(none), ALU.mult))
                step(dve.tensor_tensor(wz, wz, fb, ALU.add))
                step(dve.tensor_reduce(total, wz, AX.X, ALU.add))
                step(dve.tensor_scalar(total, total, 1e-8, None, ALU.max))
                step(dve.reciprocal(total, total))
                step(dve.tensor_tensor(out, wz, over(total), ALU.mult))


def program(nc, a, out):
    lag_b = nc.dram_tensor("lag_b_scratch", [2 * HEADS, TOK], F32, kind="Internal").ap()
    saved = nc.dram_tensor("residual_scratch", [P, NTT * HID], F32, kind="Internal").ap()
    with ExitStack() as ctx:
        mem = {}
        for name, shape in (("x_tok", [P, NTT * HID]), ("ident", [P, P]), ("minus_half", [P, NTT])):
            mem[name] = ctx.enter_context(nc.sbuf_tensor(name, shape, F32))
        s_id = ctx.enter_context(nc.semaphore("s_ident"))
        with nc.Block() as block:
            @block.sync
            def _(sp):
                sp.dma_start(mem["ident"][:, :], a["identity"]).then_inc(s_id, 16)
                sp.wait_ge(s_id, 16)

            @block.vector
            def _(dve):
                dve.memset(mem["minus_half"][:, :], -0.5)

        pooled_attention(nc, mem, a["x"], {n: a["w_" + n] for n in ("q", "qa", "k", "ka", "v")}, a["columns"])
        for name in ("xT_hi", "xT_lo"):
            mem[name] = ctx.enter_context(nc.sbuf_tensor(name, [P, KC, TOK], F32R))
        norm_and_turn(nc, "turn0", mem, normalise=False)
        gated_units(nc, "dense", mem, a["dense_gate"], a["dense_up"], a["dense_down"], INNER // UNIT,
                    scales=(a["dense_gate_scale"], a["dense_up_scale"], a["dense_down_scale"].to_broadcast([P, HID])))
        norm_and_turn(nc, "norm1", mem)
        with nc.sbuf_tensor("lag_a", [P, NTT * HEADS], F32) as lag_a, nc.sbuf_tensor("ssum", [P, NTT * HEADS], F32) as ssum:
            mem["ssum"] = ssum
            small_projection(nc, "factors", mem, a["head_factors"], 2 * HEADS, lag_a[:, :], HEADS, lag_b)
            lagged_attention(nc, mem, a["head_weights"], a["head_out"], a["conv"], a["head_norm"], a["rotation"],
                             a["band"], lag_a[:, :], lag_b, saved)
        norm_and_turn(nc, "norm2", mem)
        with nc.sbuf_tensor("expert_weight", [P, NTT * EXPERTS], F32) as expert_weight:
            small_projection(nc, "router", mem, a["router"], EXPERTS, expert_weight[:, :], EXPERTS)
            route(nc, expert_weight[:, :], a["temperature"], a["numbers"])
            gated_units(nc, "experts", mem, a["expert_gate"], a["expert_up"], a["expert_down"],
                        EXPERTS * EXPERT_WIDTH // UNIT, expert_weight=expert_weight[:, :])
        norm_and_turn(nc, "norm3", mem, turn=False)
        s_out = ctx.enter_context(nc.semaphore("s_out"))
        with nc.Block() as block:
            @block.sync
            def _(sp):
                sp.dma_start(out.rearrange("(j p) n -> p j n", p=P),
                             mem["x_tok"][:, :].rearrange("p (j n) -> p j n", n=HID)).then_inc(s_out, 16)
                sp.wait_ge(s_out, 16)


def kernel(**inputs):
    import concourse.bacc as bacc
    from concourse.bass_utils import run_bass_kernel_spmd

    v = {k: np.asarray(t) for k, t in inputs.items()}

    def rows_first(w):
        return w.reshape(KC, P, -1).transpose(1, 0, 2).reshape(P, -1)

    def columns(t):
        return t.reshape(-1, P).T

    def by_unit_in(w):
        return w.reshape(KC, P, -1, UNIT).transpose(2, 1, 0, 3).reshape(-1, P, KC * UNIT)

    def by_unit_out(w):
        return w.reshape(-1, FPU, P, HID).transpose(0, 2, 1, 3).reshape(-1, P, FPU * HID)

    def experts_in(w):
        return w.reshape(EXPERTS, KC, P, -1, UNIT).transpose(0, 3, 2, 1, 4).reshape(-1, P, KC * UNIT)

    inv = (1.0 / ROPE_BASE ** (np.arange(0, HDIM, 2, dtype=np.float32) / HDIM)).astype(np.float32)
    angle = np.arange(SEQ, dtype=np.float32)[:, None] * inv[None, :]
    cos, sin = np.cos(angle).astype(np.float32).T, np.sin(angle).astype(np.float32).T
    rotation = np.concatenate([np.concatenate([cos, cos], 0), np.concatenate([-sin, sin], 0)], 1)
    lag = np.arange(P + LAGS - 1)[None, :] - np.arange(P)[:, None]
    band = np.where((lag >= 0) & (lag < LAGS), 0.5 / math.sqrt(HDIM), 0.0).astype(np.float32)

    arrays = {
        "x": v["L0_attn_hidden_states"],
        "identity": np.eye(P, dtype=np.float32),
        "columns": np.concatenate([columns(v["L0_attn_" + n]) for n in
                                   ("ln_g", "ln_b", "bq", "bqa", "bk", "bka", "bv")], 1),
        **{"w_" + n: rows_first(v["L0_attn_W" + n].T) for n in ("q", "qa", "k", "ka", "v")},
        "dense_gate": by_unit_in(v["L0_ffn_gate_w"].T),
        "dense_up": by_unit_in(v["L0_ffn_up_w"].T),
        "dense_down": by_unit_out(v["L0_ffn_down_w"].T),
        "dense_gate_scale": columns(v["L0_ffn_gate_scale"]),
        "dense_up_scale": columns(v["L0_ffn_up_scale"]),
        "dense_down_scale": v["L0_ffn_down_scale"].reshape(1, HID),
        "head_weights": np.stack([v["L1_attn_W" + n].reshape(KC, P, HEADS, HDIM) for n in "qkvz"], 0)
                          .transpose(3, 2, 0, 1, 4).reshape(HEADS, P, 4 * KC * HDIM),
        "head_out": v["L1_attn_Wout"].reshape(HEADS, P, HID),
        "head_factors": rows_first(np.concatenate([v["L1_attn_Wa"], v["L1_attn_Wb"]], 1)),
        "conv": np.stack([v[f"L1_attn_conv_{n}_w"].reshape(HEADS, HDIM, LAGS) for n in "qkv"], 0)
                  .transpose(2, 1, 0, 3).reshape(P, HEADS * 3 * LAGS),
        "head_norm": v["L1_attn_norm_w"].reshape(HEADS, P).T,
        "rotation": rotation,
        "band": band,
        "router": rows_first(v["L1_ffn_Wr"]),
        "temperature": v["L1_ffn_temperature"],
        "numbers": np.broadcast_to(np.arange(EXPERTS, dtype=np.float32), (P, EXPERTS)),
        "expert_gate": experts_in(v["L1_ffn_Wg"]),
        "expert_up": experts_in(v["L1_ffn_Wu"]),
        "expert_down": by_unit_out(v["L1_ffn_Wd"].reshape(-1, HID)),
    }
    nc = bacc.Bacc("TRN2", target_bir_lowering=False, num_devices=1)
    host, dram = {}, {}
    for name, t in arrays.items():
        host["in_" + name] = np.ascontiguousarray(t)
        dram[name] = nc.dram_tensor("in_" + name, t.shape, mybir.dt.from_np(t.dtype), kind="ExternalInput").ap()
    out = nc.dram_tensor("out", (TOK, HID), F32, kind="ExternalOutput").ap()
    program(nc, dram, out)
    result = run_bass_kernel_spmd(nc, [host], core_ids=[0])
    return result.results[0]["out"].reshape(BATCH, SEQ, HID)
```

```python
import math
from contextlib import ExitStack, contextmanager

import numpy as np

import concourse.bass as bass
from concourse import mybir

F32 = mybir.dt.float32
F32R = mybir.dt.float32r
I32 = mybir.dt.int32
ALU = mybir.AluOpType
ACT = mybir.ActivationFunctionType
AX = mybir.AxisListType

P = 128
BATCH, SEQ, HID = 4, 512, 512
TOK = BATCH * SEQ
KC = HID // P
NTT = TOK // P
TPB = SEQ // P
HEADS, HDIM, LAGS = 16, 128, 4
INNER = 2048
EXPERTS, EXPERT_WIDTH = 8, 512
UNIT = 256
FPU = UNIT // P
LN_EPS = 1e-5
RMS_EPS = 1e-6
ROPE_BASE = 1000000.0


def f32(ap):
    return ap.bitcast(F32)


def product(pe, out, left, right, first=True, last=True):
    n = len(left)
    for k in range(n):
        (lh, ll), (rh, rl) = left[k], right[k]
        pe.matmul(out, lh, rh, start=first and k == 0, stop=False)
        pe.matmul(out, lh, rl, start=False, stop=False)
        done = pe.matmul(out, ll, rh, start=False, stop=last and k == n - 1)
    return done


class Sems:

    def __init__(self, nc, prefix):
        self.nc, self.prefix = nc, prefix

    def __call__(self, name):
        return self.nc.alloc_semaphore(name=f"{self.prefix}_{name}")


@contextmanager
def phase(nc):
    with nc.cleanup_on_exit(), ExitStack() as ctx:
        yield ctx


def wait_apart(eng, sem, value):
    eng.wait_ge(sem, value)
    if not isinstance(value, int):
        eng.nop(nofuse=True)


class Chain:

    def __init__(self, eng, sem, base=0, apart=False):
        self.eng, self.sem, self.n, self.base, self.apart = eng, sem, 0, base, apart

    def link(self, ins):
        ins.then_inc(self.sem, 1)
        self.n += 1
        (wait_apart if self.apart else type(self.eng).wait_ge)(self.eng, self.sem, self.base + self.n)


class Part:

    def early(self, sp):
        pass

    early_scalar = sync = scalar = vector = gpsimd = tensor = early


class Norm(Part):

    def __init__(self, nc, ctx, name, mem, rows=None, banks=None, normalise=True, rms=None, store=None):
        sem = Sems(nc, name)
        self.mem, self.normalise, self.turn, self.rms, self.store = mem, normalise, banks is not None, rms, store
        self.rows = rows
        self.turned = banks and [b.rearrange("p (k n) -> p k n", n=P) for b in banks]
        small = lambda what, shape: ctx.enter_context(nc.sbuf_tensor(f"{name}_{what}", shape, F32))
        self.stats, self.mv = small("stats", [P, TPB, 6]), small("mv", [P, TPB, 2])
        self.std, self.rstd = small("std", [P, TPB]), small("rstd", [P, TPB])
        if rms:
            self.ms = small("ms", [P, NTT])
            self.saved, self.res, self.ssum = rms
            self.s_ms = sem("ms")
            self.s_root = sem("root")
            self.s_res = sem("res")
            self.s_sum = sem("sum")
        self.s_stat = sem("stat")
        self.s_aggr = sem("aggr")
        self.s_var = sem("var")
        self.s_std = sem("std")
        self.s_row = sem("row")
        self.s_xn = sem("xn")
        self.s_turn = sem("turn")
        self.s_hi = sem("hi")
        self.s_lo = sem("lo")
        self.s_store = sem("store")

    def row(self, g, t):
        return self.mem["x_tok"][:, bass.ds((g * TPB + t) * HID, HID)]

    def load(self, sp, g):
        for t in range(TPB):
            sp.dma_start(self.res[t], self.saved[:, bass.ds((g * TPB + t) * HID, HID)]).then_inc(self.s_res, 16)

    def early(self, sp):
        if self.rms:
            self.load(sp, 0)

    def sync(self, sp):
        if self.rms:
            with sp.Fori(1, BATCH) as g:
                wait_apart(sp, self.s_sum, g * TPB)
                self.load(sp, g)
        if self.store is not None:
            with sp.Fori(0, BATCH) as g:
                wait_apart(sp, self.s_row, g * TPB + TPB)
                sp.dma_start(self.store.rearrange("(j p) n -> p j n", p=P)[:, bass.ds(g * TPB, TPB), :],
                             self.mem["x_tok"][:, bass.ds(g * (TPB * HID), TPB * HID)]
                             .rearrange("p (j n) -> p j n", n=HID)).then_inc(self.s_store, 16)
            sp.wait_ge(self.s_store, 16 * BATCH)

    def statistics(self, dve, g):
        if self.rms:
            wait_apart(dve, self.s_res, (g + 1) * (16 * TPB))
            for t in range(TPB):
                dve.scalar_tensor_tensor(self.row(g, t), self.row(g, t), self.ms[:, bass.ds(g * TPB + t, 1)],
                                         self.res[t], op0=ALU.mult, op1=ALU.add).then_inc(self.s_sum, 1)
            wait_apart(dve, self.s_sum, g * TPB + TPB)
        for t in range(TPB):
            dve.bn_stats(self.stats[:, t, :], self.row(g, t)).then_inc(self.s_stat, 1)
        wait_apart(dve, self.s_stat, g * TPB + TPB)
        for t in range(TPB):
            dve.bn_aggr(self.mv[:, t, :], self.stats[:, t, :]).then_inc(self.s_aggr, 1)
        wait_apart(dve, self.s_aggr, g * TPB + TPB)
        dve.tensor_scalar(self.std[:, :], self.mv[:, :, 1], LN_EPS, None, ALU.add).then_inc(self.s_var, 1)

    def normalised(self, dve, g):
        if self.normalise:
            wait_apart(dve, self.s_std, g + 1)
        outs = [(self.row, self.s_row)] if self.normalise else []
        if self.turn:
            if not isinstance(g, int) or g:
                wait_apart(dve, self.s_lo, g * TPB + TPB)
            outs.insert(0, (lambda g, t: self.rows[t], self.s_xn))
        for out, done in outs:
            for t in range(TPB):
                if self.normalise:
                    ins = dve.tensor_scalar(out(g, t), self.row(g, t), self.mv[:, t, 0:1], self.rstd[:, t:t + 1],
                                            ALU.subtract, ALU.mult)
                else:
                    ins = dve.tensor_copy(out(g, t), self.row(g, t))
                ins.then_inc(done, 1)

    def vector(self, dve):
        if self.turn:
            dve.sem_inc(self.s_lo, TPB)
        if self.rms:
            dve.tensor_reduce(self.ms[:, :], self.ssum.rearrange("p (j h) -> p j h", h=HEADS), AX.X,
                              ALU.add).then_inc(self.s_ms, 1)
            dve.wait_ge(self.s_ms, 1)
            dve.tensor_scalar(self.ms[:, :], self.ms[:, :], 1.0 / (HEADS * HDIM), RMS_EPS,
                              ALU.mult, ALU.add).then_inc(self.s_ms, 1)
            dve.wait_ge(self.s_root, 1)

        def group(g, last):
            self.normalised(dve, g)
            if not last and self.normalise:
                self.statistics(dve, g + 1)
            if self.turn:
                for t in range(TPB):
                    wait_apart(dve, self.s_hi, g * TPB + (t + 1))
                    cols = bass.ds((g * TPB + t) * P, P)
                    dve.tensor_tensor(self.mem["xT_lo"][:, :, cols], self.turned[t],
                                      f32(self.mem["xT_hi"][:, :, cols]), ALU.subtract).then_inc(self.s_lo, 1)

        if self.normalise:
            self.statistics(dve, 0)
        with dve.Fori(0, BATCH - 1) as g:
            group(g, False)
        group(BATCH - 1, True)

    def gpsimd(self, pool):
        half = self.mem["minus_half"]
        if self.rms:
            pool.wait_ge(self.s_ms, 2)
            pool.tensor_tensor(self.ms[:, :], self.ms[:, :], half[:, 0:NTT], ALU.pow).then_inc(self.s_root, 1)
        if self.normalise:
            with pool.Fori(0, BATCH) as g:
                wait_apart(pool, self.s_var, g + 1)
                pool.tensor_tensor(self.rstd[:, :], self.std[:, :], half[:, 0:TPB], ALU.pow).then_inc(self.s_std, 1)

    def scalar(self, act):
        if self.turn:
            with act.Fori(0, BATCH) as g:
                for t in range(TPB):
                    wait_apart(act, self.s_turn, g * TPB + (t + 1))
                    cols = bass.ds((g * TPB + t) * P, P)
                    act.activation(self.mem["xT_hi"][:, :, cols], self.turned[t], ACT.Copy).then_inc(self.s_hi, 1)

    def tensor(self, pe):
        if self.turn:
            with pe.Fori(0, BATCH) as g:
                for t in range(TPB):
                    pe.wait_ge(self.s_xn, g * TPB + (t + 1))
                    pe.wait_ge(self.s_lo, g * TPB + (t + 1))
                    for k in range(KC):
                        last = pe.transpose(self.turned[t][:, k, :], self.rows[t][:, k * P:(k + 1) * P],
                                            self.mem["ident"][:, :])
                    last.then_inc(self.s_turn, 1)
            pe.wait_ge(self.s_lo, NTT + TPB)


def gated_units(nc, name, mem, w_gate, w_up, w_down, units, before, scales=None, expert_weight=None):
    x_tok, xT_hi, xT_lo = mem["x_tok"], mem["xT_hi"], mem["xT_lo"]
    quantised = scales is not None
    with phase(nc) as ctx:
        sem = Sems(nc, name)

        def sb(what, shape, dt=F32):
            return ctx.enter_context(nc.sbuf_tensor(f"{name}_{what}", shape, dt))

        def bank(what):
            return ctx.enter_context(nc.psum_tensor(f"{name}_{what}", [P, 512], F32))

        W = KC * UNIT
        raw = [[sb(f"raw{p}{m}", [P, W], I32 if quantised else F32) for m in range(3)] for p in range(2)]
        w_hi = [[sb(f"whi{p}{m}", [P, W], F32R) for m in range(3)] for p in range(2)]
        w_lo = [[sb(f"wlo{p}{m}", [P, W], F32R) for m in range(3)] for p in range(2)]
        gated = [sb(f"gated{r}", [P, SEQ]) for r in range(2)]
        inner = [sb(f"inner{r}", [P, SEQ]) for r in range(2)]
        in_hi = [sb(f"inhi{r}", [P, FPU, SEQ], F32R) for r in range(2)]
        in_lo = [sb(f"inlo{r}", [P, FPU, SEQ], F32R) for r in range(2)]
        if quantised:
            scale_gate = sb("sgate", [P, units * FPU])
            scale_up = sb("sup", [P, units * FPU])
            scale_down = sb("sdown", [P, HID])
            flat = [[raw[p][m][:, :].bitcast(F32) for m in range(3)] for p in range(2)]
        else:
            flat = [[raw[p][m][:, :] for m in range(3)] for p in range(2)]
        G = [bank(f"G{r}") for r in range(2)]
        U = [bank(f"U{r}") for r in range(2)]
        D = [bank(f"D{r}") for r in range(TPB)]

        s_const = sem("const")
        s_raw = [sem(f"raw{p}") for p in range(2)]
        s_deq = sem("deq")
        s_whi = sem("whi")
        s_wlo = sem("wlo")
        s_g = sem("g")
        s_u = sem("u")
        s_silu = sem("silu")
        s_h = sem("h")
        s_hhi = sem("hhi")
        s_hlo = sem("hlo")
        s_d = sem("d")
        s_acc = sem("acc")
        spare = [flat[1][m][:, k * HID:(k + 1) * HID] for m in range(3) for k in range(W // HID)]
        spare += [t[:, :] for t in (*gated, *inner)]
        s_ahead = sem("ahead")
        ahead = before(ctx, spare, [w_hi[1][0][:, k * HID:(k + 1) * HID] for k in range(2)],
                       [b[:, :] for b in (*D, *G, *U)])
        NB = 2
        CH = FPU * BATCH

        def rotated(eng, before, body):
            before()
            with eng.Fori(0, units // 2 - 1) as i:
                body(i, False)
            body(units // 2 - 1, True)

        def weight_split_hi(act, pair, u, p):
            for m in range(3):
                if quantised:
                    act.wait_ge(s_deq, u * 3 + (m + 1))
                elif m == 0:
                    act.wait_ge(s_raw[p], pair * 48 + 48)
                act.activation(w_hi[p][m][:, :], flat[p][m], ACT.Copy).then_inc(s_whi, 1)

        with nc.Block() as block:
            @block.sync
            def _(sp):
                if quantised:
                    for t, src in ((scale_gate, scales[0]), (scale_up, scales[1]), (scale_down, scales[2])):
                        sp.dma_start(t[:, :], src).then_inc(s_const, 16)

                def load(u, p):
                    for m, w in enumerate((w_gate, w_up, w_down)):
                        src = w[u, :, :] if isinstance(u, int) else w[bass.ds(u, 1), :, :].rearrange("a p n -> (a p) n")
                        sp.dma_start(raw[p][m][:, :], src).then_inc(s_raw[p], 16)

                for part in ahead:
                    part.early(sp)
                load(0, 0)
                for part in ahead:
                    part.sync(sp)
                sp.wait_ge(s_ahead, 1)
                load(1, 1)
                with sp.Fori(1, units // 2) as i:
                    for p in range(2):
                        wait_apart(sp, s_wlo, (2 * i + (p - 1)) * 3)
                        load(2 * i + p, p)

            @block.tensor
            def _(pe):
                for part in ahead:
                    part.tensor(pe)
                pe.sem_inc(s_ahead, 1)
                pe.sem_inc(s_d, 2 * TPB)

                def gate_up(u, t, p):
                    if t == 0:
                        pe.wait_ge(s_whi, u * 3 + 3)
                        pe.wait_ge(s_wlo, u * 3 + 3)
                    for f in range(FPU):
                        r = u * CH + (t * FPU + f)
                        pe.wait_ge(s_h, r + 1)
                        cols = slice(t * SEQ, (t + 1) * SEQ)
                        for m, (out, done) in enumerate(((G, s_g), (U, s_u))):
                            left = [(w_hi[p][m][:, k * UNIT + f * P:k * UNIT + (f + 1) * P],
                                     w_lo[p][m][:, k * UNIT + f * P:k * UNIT + (f + 1) * P]) for k in range(KC)]
                            right = [(xT_hi[:, k, cols], xT_lo[:, k, cols]) for k in range(KC)]
                            product(pe, out[f][:, :], left, right).then_inc(done, 1)

                def down(u, t, p):
                    s = u * BATCH + t
                    pe.wait_ge(s_hlo, s * FPU + 2 + FPU)
                    for tt in range(TPB):
                        pe.wait_ge(s_acc, s * TPB + (tt + 1))
                        at = slice(tt * P, (tt + 1) * P)
                        left = [(in_hi[t % 2][:, f, at], in_lo[t % 2][:, f, at]) for f in range(FPU)]
                        right = [(w_hi[p][2][:, f * HID:(f + 1) * HID], w_lo[p][2][:, f * HID:(f + 1) * HID])
                                 for f in range(FPU)]
                        product(pe, D[tt][:, :], left, right).then_inc(s_d, 1)

                def body(i, last):
                    steps = [(2 * i + p, t, p) for p in range(2) for t in range(BATCH)]
                    for n, step in enumerate(steps):
                        if n + 1 < len(steps):
                            gate_up(*steps[n + 1])
                        elif not last:
                            gate_up(2 * i + 2, 0, 0)
                        down(*step)

                rotated(pe, lambda: gate_up(0, 0, 0), body)

            @block.scalar
            def _(act):
                if quantised:
                    act.wait_ge(s_const, 48)
                weight_split_hi(act, 0, 0, 0)
                for part in ahead:
                    part.early_scalar(act)
                for part in ahead:
                    part.scalar(act)

                def step(u, t, p):
                    for f in range(FPU):
                        r = u * CH + (t * FPU + f)
                        act.wait_ge(s_g, r + 1)
                        wait_apart(act, s_h, r + 1)
                        if quantised:
                            sc = scale_gate[:, bass.ds(u * FPU + f, 1)]
                            act.activation(gated[f][:, :], G[f][:, :], ACT.Silu, scale=sc).then_inc(s_silu, 1)
                        else:
                            act.activation(gated[f][:, :], G[f][:, :], ACT.Silu).then_inc(s_silu, 1)
                        act.wait_ge(s_h, r + 3)
                        act.wait_ge(s_d, (u * BATCH + t) * TPB + TPB)
                        act.activation(in_hi[t % 2][:, f, :], inner[f][:, :], ACT.Copy).then_inc(s_hhi, 1)

                def body(i, last):
                    for p in range(2):
                        for t in range(BATCH):
                            step(2 * i + p, t, p)
                            if t == 1 and not (last and p):
                                act.wait_ge(s_d, (2 * i + p) * (BATCH * TPB) + 2 * TPB)
                                weight_split_hi(act, i + p, 2 * i + p + 1, 1 - p)

                rotated(act, lambda: None, body)

            @block.gpsimd
            def _(pool):
                pool.sem_inc(s_hlo, 2)

                def weight_split_lo(u, p):
                    for m in range(3):
                        pool.wait_ge(s_whi, u * 3 + (m + 1))
                        pool.tensor_tensor(w_lo[p][m][:, :], flat[p][m], f32(w_hi[p][m][:, :]),
                                           ALU.subtract).then_inc(s_wlo, 1)

                for part in ahead:
                    part.gpsimd(pool)
                weight_split_lo(0, 0)

                def body(i, last):
                    for p in range(2):
                        for t in range(BATCH):
                            for f in range(FPU):
                                r = (2 * i + p) * CH + (t * FPU + f)
                                pool.wait_ge(s_hhi, r + 1)
                                pool.tensor_tensor(in_lo[t % 2][:, f, :], inner[f][:, :],
                                                   f32(in_hi[t % 2][:, f, :]), ALU.subtract).then_inc(s_hlo, 1)
                            if t == 1 and not (last and p):
                                weight_split_lo(2 * i + p + 1, 1 - p)

                rotated(pool, lambda: None, body)

            @block.vector
            def _(dve):
                dve.sem_inc(s_h, NB)
                dve.sem_inc(s_acc, TPB)

                def dequantise(pair, p):
                    dve.wait_ge(s_raw[p], pair * 48 + 48)
                    for m in range(2):
                        dve.tensor_scalar(flat[p][m], raw[p][m][:, :], 128.0, None,
                                          ALU.subtract).then_inc(s_deq, 1)
                    for f in range(FPU):
                        last = dve.scalar_tensor_tensor(flat[p][2][:, f * HID:(f + 1) * HID],
                                                        raw[p][2][:, f * HID:(f + 1) * HID], 128.0,
                                                        scale_down[:, :], op0=ALU.subtract, op1=ALU.mult)
                    last.then_inc(s_deq, 1)

                def inner_chunks(u, t, p):
                    for f in range(FPU):
                        r = u * CH + (t * FPU + f)
                        dve.wait_ge(s_silu, r + 1)
                        dve.wait_ge(s_u, r + 1)
                        dve.wait_ge(s_hlo, r + 1)
                        if quantised:
                            ins = dve.scalar_tensor_tensor(inner[f][:, :], U[f][:, :],
                                                           scale_up[:, bass.ds(u * FPU + f, 1)], gated[f][:, :],
                                                           op0=ALU.mult, op1=ALU.mult)
                        else:
                            ins = dve.tensor_tensor(inner[f][:, :], U[f][:, :], gated[f][:, :], ALU.mult)
                        ins.then_inc(s_h, 1)

                def add(u, t, p, e):
                    for tt in range(TPB):
                        s = (u * BATCH + t) * TPB + tt
                        dve.wait_ge(s_d, s + 2 * TPB + 1)
                        dve.wait_ge(s_acc, s + 1)
                        j = t * TPB + tt
                        row = x_tok[:, j * HID:(j + 1) * HID]
                        if expert_weight is None:
                            ins = dve.tensor_tensor(row, D[tt][:, :], row, ALU.add)
                        else:
                            ins = dve.scalar_tensor_tensor(row, D[tt][:, :],
                                                           expert_weight[:, bass.ds(e + j * EXPERTS, 1)], row,
                                                           op0=ALU.mult, op1=ALU.add)
                        ins.then_inc(s_acc, 1)

                if quantised:
                    dve.wait_ge(s_const, 48)
                    dequantise(0, 0)
                for part in ahead:
                    part.vector(dve)

                def body(i, last):
                    steps = [(2 * i + p, t, p) for p in range(2) for t in range(BATCH)]
                    for n, (u, t, p) in enumerate(steps):
                        if n + 1 < len(steps):
                            inner_chunks(*steps[n + 1])
                        elif not last:
                            inner_chunks(2 * i + 2, 0, 0)
                        if quantised and t == 0 and not (last and p):
                            dequantise(i + p, 1 - p)
                        add(u, t, p, i)

                rotated(dve, lambda: inner_chunks(0, 0, 0), body)


def until(eng, sem, value):
    if not isinstance(value, int) or value > 0:
        eng.wait_ge(sem, value)


def pooled_attention(nc, mem, x, w, biases):
    x_tok, ident = mem["x_tok"], mem["ident"]
    NAMES = ("q", "qa", "k", "ka", "v")
    SCALE = 1.0 / math.sqrt(HID)
    with phase(nc) as ctx:
        sem = Sems(nc, "pool")

        def sb(what, shape, dt=F32):
            return ctx.enter_context(nc.sbuf_tensor(f"pool_{what}", shape, dt))

        w_hi = {n: sb(f"w{n}_hi", [P, KC, HID], F32R) for n in NAMES}
        w_lo = {n: sb(f"w{n}_lo", [P, KC, HID], F32R) for n in NAMES}
        h_hi, h_lo = sb("h_hi", [P, KC, SEQ], F32R), sb("h_lo", [P, KC, SEQ], F32R)
        m_hi, m_lo = sb("m_hi", [P, KC, SEQ], F32R), sb("m_lo", [P, KC, SEQ], F32R)
        xn = sb("xn", [P, TPB, HID])
        hf = [sb(f"hf{j}", [P, SEQ]) for j in range(2)]
        qf, kf, vf = sb("qf", [P, KC, SEQ]), sb("kf", [P, KC, SEQ]), sb("vf", [P, KC, SEQ])
        mixed, res = sb("mixed", [P, KC, SEQ]), sb("res", [P, KC, SEQ])
        expw = [sb(f"expw{j}", [P, SEQ]) for j in range(KC)]
        cum = sb("cum", [P, SEQ])
        ones = sb("ones", [P, 1])
        col = sb("col", [P, 7 * KC])
        scaled = sb("scaled", [P, 2 * KC])
        stats, mv = sb("stats", [P, TPB, 6]), sb("mv", [P, TPB, 2])
        var, rstd = sb("var", [P, TPB]), sb("rstd", [P, TPB])
        stats2, mv2 = sb("stats2", [P, TPB, 6]), sb("mv2", [P, TPB, 2])
        var2, rstd2 = sb("var2", [P, TPB]), sb("rstd2", [P, TPB])
        banks = [ctx.enter_context(nc.psum_tensor(f"pool_bank{j}", [P, SEQ], F32)) for j in range(4)]
        turned = [ctx.enter_context(nc.psum_tensor(f"pool_turned{j}", [P, TPB, P], F32)) for j in range(2)]
        back = [ctx.enter_context(nc.psum_tensor(f"pool_back{j}", [P, HID], F32)) for j in range(2)]
        G_, B_, BQ, BQA, BK, BKA, BV = (lambda k, n=n: col[:, n * KC + k:n * KC + k + 1] for n in range(7))
        staging = {"q": qf, "k": kf, "qa": mixed, "v": vf, "ka": res}
        ORDER = ("q", "k", "qa", "v", "ka")

        s_x = sem("x")
        s_col = sem("col")
        s_raw = {n: sem(f"raw_{n}") for n in NAMES}
        s_whi = sem("whi")
        s_wlo_d = sem("wlod")
        s_wlo_p = sem("wlop")
        s_scaled = sem("scaled")
        s_ones = sem("ones")
        s_n1 = sem("n1")
        s_r1 = sem("r1")
        s_t = sem("t")
        s_hf = sem("hf")
        s_hhi, s_hlo = sem("hhi"), sem("hlo")
        s_mm = sem("mm")
        s_ev = sem("ev")
        s_qhi, s_qlo = sem("qhi"), sem("qlo")
        s_mhi, s_mlo = sem("mhi"), sem("mlo")
        s_p1 = sem("p1")
        s_p2 = sem("p2")
        s_b = sem("b")
        s_add = sem("add")
        s_n2 = sem("n2")
        s_r2 = sem("r2")
        N1 = 4 * TPB
        N2 = 4 * TPB
        ROW = 6 * KC
        FRONT, SLOT = 3 * KC, 5 * KC

        def place(kind, b, m):
            if kind in ("v", "ka"):
                return FRONT + b * SLOT + ("v", "ka").index(kind) * KC + m
            n = ("q", "k", "qa").index(kind) * KC + m
            return n if isinstance(b, int) and b == 0 else FRONT + (b - 1) * SLOT + 2 * KC + n

        def in_slots(eng, prologue, slot):
            prologue()
            with eng.Fori(0, BATCH - 1) as i:
                slot(i, i + 1)
            slot(BATCH - 1, None)

        with nc.Block() as block:
            @block.sync
            def _(sp):
                view = x_tok[:, :].rearrange("p (j n) -> p j n", n=HID)

                def row(b):
                    sp.dma_start(view[:, b * TPB:(b + 1) * TPB, :],
                                 x[b, :, :].rearrange("(j p) n -> p j n", p=P)).then_inc(s_x, 16)
                    sp.wait_ge(s_x, (b + 1) * 16)

                def weight(n):
                    sp.dma_start(staging[n][:, :, :].rearrange("p a b -> p (a b)"), w[n]).then_inc(s_raw[n], 16)

                sp.dma_start(col[:, :], biases).then_inc(s_col, 16)
                weight("q")
                row(0)
                for n in ORDER[1:]:
                    weight(n)
                for b in range(1, BATCH):
                    row(b)

            @block.tensor
            def _(pe):
                def weights_ready(n):
                    at = ORDER.index(n)
                    pe.wait_ge(s_wlo_p if at % 2 else s_wlo_d, at // 2 + 1)

                def chunks(kind, b, rh, rl):
                    for m in range(KC):
                        at = place(kind, b, m)
                        until(pe, s_ev, at - 3)
                        product(pe, banks[m][:, :],
                                [(w_hi[kind][:, k, m * P:(m + 1) * P], w_lo[kind][:, k, m * P:(m + 1) * P])
                                 for k in range(KC)],
                                [(rh[:, k, :], rl[:, k, :]) for k in range(KC)]).then_inc(s_mm, 1)

                def turn(b):
                    pe.wait_ge(s_n1, b * N1 + N1)
                    for k in range(KC):
                        until(pe, s_hf, b * KC + (k - 1))
                        for t in range(TPB):
                            last = pe.transpose(turned[k % 2][:, t, :], xn[:, t, k * P:(k + 1) * P], ident[:, :])
                        last.then_inc(s_t, 1)

                def queries_and_keys(b, first=False):
                    if first:
                        weights_ready("q")
                    pe.wait_ge(s_hlo, b * KC + KC)
                    chunks("q", b, h_hi, h_lo)
                    if first:
                        weights_ready("k")
                    chunks("k", b, h_hi, h_lo)

                def query_weights(b):
                    pe.wait_ge(s_qlo, b * KC + KC)
                    chunks("qa", b, m_hi, m_lo)

                def prologue():
                    turn(0)
                    queries_and_keys(0, True)
                    weights_ready("qa")
                    query_weights(0)
                    weights_ready("v")
                    weights_ready("ka")

                def slot(b, nxt):
                    chunks("v", b, h_hi, h_lo)
                    pe.wait_ge(s_mlo, b * KC + KC)
                    chunks("ka", b, m_hi, m_lo)
                    if nxt is not None:
                        turn(nxt)
                        queries_and_keys(nxt)
                    pe.wait_ge(s_p2, b * ROW + (ROW + 1))
                    for t in range(TPB):
                        pe.wait_ge(s_add, b * TPB + (t + 1))
                        for m in range(KC):
                            last = pe.transpose(back[t % 2][:, m * P:(m + 1) * P], res[:, m, t * P:(t + 1) * P],
                                                ident[:, :])
                        last.then_inc(s_b, 1)
                    if nxt is not None:
                        query_weights(nxt)

                in_slots(pe, prologue, slot)

            @block.scalar
            def _(act):
                act.wait_ge(s_col, 16)
                for n, c in ((0, 3), (1, 5)):
                    act.activation(scaled[:, n * KC:(n + 1) * KC], col[:, c * KC:(c + 1) * KC], ACT.Copy,
                                   scale=SCALE).then_inc(s_scaled, 1)
                act.wait_ge(s_scaled, 2)

                def split_hi(n):
                    act.wait_ge(s_raw[n], 16)
                    act.activation(w_hi[n][:, :, :], staging[n][:, :, :], ACT.Copy).then_inc(s_whi, 1)

                def bank(kind, b, m):
                    act.wait_ge(s_mm, place(kind, b, m) + 1)
                    return banks[m][:, :]

                def turn(b, first=False):
                    for k in range(KC):
                        act.wait_ge(s_t, b * KC + (k + 1))
                        until(act, s_hlo, b * KC + (k - 1))
                        act.activation(hf[k % 2][:, :], turned[k % 2][:, :, :].rearrange("p a b -> p (a b)"),
                                       ACT.Identity, bias=B_(k), scale=G_(k)).then_inc(s_hf, 1)
                        act.wait_ge(s_hf, b * KC + (k + 1))
                        if not first:
                            act.wait_ge(s_mm, place("v", b - 1, KC - 1) + 1)
                        act.activation(h_hi[:, k, :], hf[k % 2][:, :], ACT.Copy).then_inc(s_hhi, 1)

                def queries_and_keys(b, first=False):
                    for m in range(KC):
                        src = bank("q", b, m)
                        if not first:
                            act.wait_ge(s_p1, b * ROW)
                        act.activation(qf[:, m, :], src, ACT.Identity, bias=BQ(m)).then_inc(s_ev, 1)
                        act.wait_ge(s_ev, place("q", b, m) + 1)
                        if not first:
                            act.wait_ge(s_mm, place("ka", b - 1, KC - 1) + 1)
                        act.activation(m_hi[:, m, :], qf[:, m, :], ACT.Copy).then_inc(s_qhi, 1)
                    if first:
                        split_hi("qa")
                        split_hi("v")
                    for m in range(KC):
                        act.activation(kf[:, m, :], bank("k", b, m), ACT.Identity, bias=BK(m)).then_inc(s_ev, 1)

                def exponentials(kind, b, column, free_sem, free_value):
                    for m in range(KC):
                        src = bank(kind, b, m)
                        if free_sem is not None:
                            act.wait_ge(free_sem, free_value)
                        act.activation(expw[m][:, :], src, ACT.Exp, bias=scaled[:, column + m:column + m + 1],
                                       scale=SCALE).then_inc(s_ev, 1)

                def split_mixed(b):
                    for m in range(KC):
                        act.wait_ge(s_p1, b * ROW + (m + 1) * 6)
                        act.wait_ge(s_mm, place("qa", b, KC - 1) + 1)
                        act.activation(m_hi[:, m, :], mixed[:, m, :], ACT.Copy).then_inc(s_mhi, 1)

                def prologue():
                    split_hi("q")
                    split_hi("k")
                    turn(0, True)
                    queries_and_keys(0, True)
                    exponentials("qa", 0, 0, None, 0)
                    split_hi("ka")
                    split_mixed(0)

                def slot(b, nxt):
                    for m in range(KC):
                        src = bank("v", b, m)
                        act.wait_ge(s_p2, b * ROW + 1)
                        act.activation(vf[:, m, :], src, ACT.Identity, bias=BV(m)).then_inc(s_ev, 1)
                    exponentials("ka", b, KC, s_p1, b * ROW + ROW)
                    if nxt is not None:
                        turn(nxt)
                        queries_and_keys(nxt)
                        exponentials("qa", nxt, 0, s_p2, b * ROW + (ROW + 1))
                        split_mixed(nxt)

                in_slots(act, prologue, slot)

            @block.gpsimd
            def _(pool):
                def weight_lo(at):
                    n = ORDER[at]
                    pool.wait_ge(s_whi, at + 1)
                    pool.tensor_tensor(w_lo[n][:, :, :], staging[n][:, :, :], f32(w_hi[n][:, :, :]),
                                       ALU.subtract).then_inc(s_wlo_p, 1)

                def split_lo(hi_sem, lo_sem, hi, lo, src, b):
                    for m in range(KC):
                        pool.wait_ge(hi_sem, b * KC + (m + 1))
                        pool.tensor_tensor(lo[:, m, :], src(m), f32(hi[:, m, :]), ALU.subtract).then_inc(lo_sem, 1)

                def root(b, steps, n, src, out, done):
                    pool.wait_ge(steps, b * n + 3 * TPB)
                    pool.tensor_tensor(out[:, :], src[:, :], mem["minus_half"][:, 0:TPB], ALU.pow).then_inc(done, 1)

                def front_lo(b):
                    split_lo(s_hhi, s_hlo, h_hi, h_lo, lambda m: hf[m % 2][:, :], b)
                    split_lo(s_qhi, s_qlo, m_hi, m_lo, lambda m: qf[:, m, :], b)

                def prologue():
                    root(0, s_n1, N1, var, rstd, s_r1)
                    split_lo(s_hhi, s_hlo, h_hi, h_lo, lambda m: hf[m % 2][:, :], 0)
                    weight_lo(1)
                    split_lo(s_qhi, s_qlo, m_hi, m_lo, lambda m: qf[:, m, :], 0)
                    weight_lo(3)
                    split_lo(s_mhi, s_mlo, m_hi, m_lo, lambda m: mixed[:, m, :], 0)

                def slot(b, nxt):
                    if nxt is not None:
                        root(nxt, s_n1, N1, var, rstd, s_r1)
                        front_lo(nxt)
                    root(b, s_n2, N2, var2, rstd2, s_r2)
                    if nxt is not None:
                        split_lo(s_mhi, s_mlo, m_hi, m_lo, lambda m: mixed[:, m, :], nxt)

                in_slots(pool, prologue, slot)

            @block.vector
            def _(dve):
                dve.sem_inc(s_p2, 1)
                dve.sem_inc(s_add, 2)

                def row(b, t):
                    return x_tok[:, (b * TPB + t) * HID:(b * TPB + t + 1) * HID] if isinstance(b, int) else \
                        x_tok[:, bass.ds(b * (TPB * HID) + t * HID, HID)]

                def weight_lo(at):
                    n = ORDER[at]
                    dve.wait_ge(s_whi, at + 1)
                    dve.tensor_tensor(w_lo[n][:, :, :], staging[n][:, :, :], f32(w_hi[n][:, :, :]),
                                      ALU.subtract).then_inc(s_wlo_d, 1)

                def first_norm(b, first=False):
                    wait_apart(dve, s_x, b * 16 + 16)
                    at = b * N1
                    for t in range(TPB):
                        dve.bn_stats(stats[:, t, :], row(b, t)).then_inc(s_n1, 1)
                    for t in range(TPB):
                        wait_apart(dve, s_n1, at + (t + 1))
                        dve.bn_aggr(mv[:, t, :], stats[:, t, :]).then_inc(s_n1, 1)
                    for t in range(TPB):
                        dve.wait_ge(s_n1, at + (TPB + t + 1))
                        dve.tensor_scalar(var[:, t:t + 1], mv[:, t, 1:2], LN_EPS, None, ALU.add).then_inc(s_n1, 1)
                    dve.wait_ge(s_r1, b + 1)
                    if not first:
                        dve.wait_ge(s_t, b * KC)
                    for t in range(TPB):
                        dve.tensor_scalar(xn[:, t, :], row(b, t), mv[:, t, 0:1], rstd[:, t:t + 1],
                                          ALU.subtract, ALU.mult).then_inc(s_n1, 1)

                def pooling(kind, b, m, sem_, at, gain, by, out):
                    chain = Chain(dve, sem_, at)
                    dve.wait_ge(s_ev, place(kind, b, m) + 1)
                    e = expw[m]
                    chain.link(dve.tensor_tensor_scan(cum[:, :], ones[:, :].to_broadcast([P, SEQ]), e[:, :], 0.0, ALU.mult, ALU.add))
                    chain.link(dve.reciprocal(cum[:, :], cum[:, :]))
                    chain.link(dve.tensor_tensor(e[:, :], e[:, :], cum[:, :], ALU.mult))
                    chain.link(dve.tensor_tensor(e[:, :], e[:, :], gain, ALU.mult))
                    chain.link(dve.tensor_tensor_scan(cum[:, :], ones[:, :].to_broadcast([P, SEQ]), e[:, :], 0.0, ALU.mult, ALU.add))
                    chain.link(dve.tensor_tensor(out, cum[:, :], by, ALU.mult))

                def first_pooling(b, first=False):
                    if not first:
                        dve.wait_ge(s_mlo, b * KC)
                    for m in range(KC):
                        pooling("qa", b, m, s_p1, b * ROW + 6 * m, qf[:, m, :], kf[:, m, :], mixed[:, m, :])

                def second_pooling(b):
                    dve.wait_ge(s_add, b * TPB + 2)
                    for m in range(KC):
                        pooling("ka", b, m, s_p2, b * ROW + (6 * m + 1), mixed[:, m, :], vf[:, m, :], res[:, m, :])

                def second_norm(b):
                    at = b * N2
                    for t in range(TPB):
                        dve.wait_ge(s_b, b * TPB + (t + 1))
                        dve.tensor_tensor(row(b, t), row(b, t), back[t % 2][:, :], ALU.add).then_inc(s_add, 1)
                        wait_apart(dve, s_add, b * TPB + (t + 3))
                        dve.bn_stats(stats2[:, t, :], row(b, t)).then_inc(s_n2, 1)
                    for t in range(TPB):
                        wait_apart(dve, s_n2, at + (t + 1))
                        dve.bn_aggr(mv2[:, t, :], stats2[:, t, :]).then_inc(s_n2, 1)
                    for t in range(TPB):
                        dve.wait_ge(s_n2, at + (TPB + t + 1))
                        dve.tensor_scalar(var2[:, t:t + 1], mv2[:, t, 1:2], LN_EPS, None, ALU.add).then_inc(s_n2, 1)
                    dve.wait_ge(s_r2, b + 1)
                    for t in range(TPB):
                        dve.tensor_scalar(row(b, t), row(b, t), mv2[:, t, 0:1], rstd2[:, t:t + 1],
                                          ALU.subtract, ALU.mult).then_inc(s_n2, 1)

                def prologue():
                    dve.memset(ones[:, :], 1.0).then_inc(s_ones, 1)
                    dve.wait_ge(s_ones, 1)
                    weight_lo(0)
                    first_norm(0, True)
                    weight_lo(2)
                    first_pooling(0, True)
                    weight_lo(4)

                def slot(b, nxt):
                    if nxt is not None:
                        first_norm(nxt)
                    second_pooling(b)
                    second_norm(b)
                    if nxt is not None:
                        first_pooling(nxt)

                in_slots(dve, prologue, slot)


class Projection(Part):

    def __init__(self, nc, ctx, name, mem, w, n, by_token, n_tok, parts, plain, banks, by_feature=None):
        sem = Sems(nc, name)
        self.mem, self.w, self.n, self.n_tok = mem, w, n, n_tok
        self.by_token, self.by_feature = by_token, by_feature
        (self.w_hi, self.w_lo), (self.w_f, self.rows) = parts, plain
        self.prod, self.turned = banks
        self.s_w, self.s_hi, self.s_lo = sem("w"), sem("hi"), sem("lo")
        self.s_p = sem("p")
        self.s_r = sem("r")
        self.s_t = sem("t")
        self.s_c = sem("c")
        self.s_out = sem("out")

    def early(self, sp):
        sp.dma_start(self.w_f, self.w).then_inc(self.s_w, 16)

    def early_scalar(self, act):
        act.wait_ge(self.s_w, 16)
        act.activation(self.w_hi, self.w_f, ACT.Copy).then_inc(self.s_hi, 1)

    def gpsimd(self, pool):
        pool.wait_ge(self.s_hi, 1)
        pool.tensor_tensor(self.w_lo, self.w_f, f32(self.w_hi), ALU.subtract).then_inc(self.s_lo, 1)

    def sync(self, sp):
        if self.by_feature is not None:
            with sp.Fori(0, BATCH) as b:
                wait_apart(sp, self.s_r, b + 1)
                sp.dma_start(self.by_feature[:, bass.ds(b * SEQ, SEQ)], self.rows[0:self.n, :]).then_inc(self.s_out, 16)
            sp.wait_ge(self.s_out, 16 * BATCH)

    def vector(self, dve):
        n = self.n_tok
        with dve.Fori(0, BATCH) as b:
            wait_apart(dve, self.s_t, b + 1)
            dve.tensor_copy(self.by_token[:, bass.ds(b * (TPB * n), TPB * n)].rearrange("p (t n) -> p t n", n=n),
                            self.turned.rearrange("p (t n) -> p t n", n=P)[:, :, 0:n]).then_inc(self.s_c, 1)
        dve.wait_ge(self.s_c, BATCH)

    def scalar(self, act):
        for b in range(BATCH):
            act.wait_ge(self.s_p, b + 1)
            if b:
                act.wait_ge(self.s_t, b)
                if self.by_feature is not None:
                    act.wait_ge(self.s_out, 16 * b)
            act.activation(self.rows, self.prod, ACT.Copy).then_inc(self.s_r, 1)

    def tensor(self, pe):
        xT_hi, xT_lo = self.mem["xT_hi"], self.mem["xT_lo"]
        pe.wait_ge(self.s_lo, 1)
        for b in range(BATCH):
            cols = slice(b * SEQ, (b + 1) * SEQ)
            if b:
                pe.wait_ge(self.s_r, b)
            product(pe, self.prod, [(self.w_hi[:, k * P:(k + 1) * P], self.w_lo[:, k * P:(k + 1) * P]) for k in range(KC)],
                    [(xT_hi[:, k, cols], xT_lo[:, k, cols]) for k in range(KC)]).then_inc(self.s_p, 1)
            pe.wait_ge(self.s_r, b + 1)
            if b:
                pe.wait_ge(self.s_c, b)
            for t in range(TPB):
                last = pe.transpose(self.turned[:, t * P:(t + 1) * P], self.rows[:, t * P:(t + 1) * P],
                                    self.mem["ident"][:, :])
            last.then_inc(self.s_t, 1)
        pe.wait_ge(self.s_c, BATCH)


def lagged_attention(nc, mem, w_heads, w_out, conv, norm_w, tables, band, lag_a, lag_b, saved, before):
    x_tok, xT_hi, xT_lo, ident = mem["x_tok"], mem["xT_hi"], mem["xT_lo"], mem["ident"]
    PAD = LAGS - 1
    BAND = P + PAD
    STEPS = HEADS * BATCH
    CONV = LAGS
    with phase(nc) as ctx:
        sem = Sems(nc, "lag")

        def sb(what, shape, dt=F32):
            return ctx.enter_context(nc.sbuf_tensor(f"lag_{what}", shape, dt))

        def bank(what, shape=(P, SEQ)):
            return ctx.enter_context(nc.psum_tensor(f"lag_{what}", list(shape), F32))

        raw, raw_out = sb("raw", [P, 4, KC, HDIM]), sb("raw_out", [P, HID])
        w_hi = [sb(f"w_hi{p}", [P, 4, KC, HDIM], F32R) for p in range(2)]
        w_lo = [sb(f"w_lo{p}", [P, 4, KC, HDIM], F32R) for p in range(2)]
        wo_hi = [sb(f"wo_hi{p}", [P, HID], F32R) for p in range(2)]
        wo_lo = [sb(f"wo_lo{p}", [P, HID], F32R) for p in range(2)]
        act_in = [[sb(f"silu{n}{p}", [P, PAD + SEQ]) for p in range(2)] for n in "qkv"]
        cq, ck = sb("cq", [P, SEQ]), sb("ck", [P, SEQ])
        cv = [sb(f"cv{p}", [P, SEQ]) for p in range(2)]
        swapped = [sb(f"swapped{n}", [P, SEQ]) for n in "qk"]
        rot_q = [sb(f"rot_q{p}", [P, SEQ + PAD]) for p in range(2)]
        rot_k = [sb(f"rot_k{p}", [P, SEQ]) for p in range(2)]
        squares = sb("squares", [P, 2, SEQ])
        b_row = sb("b_row", [P, SEQ + PAD])
        gate = sb("gate", [P, TPB, BAND])
        prob = sb("prob", [P, TPB, BAND])
        values = sb("values", [P, TPB, HDIM])
        o_tok = sb("o_tok", [P, TPB, HDIM])
        y = sb("y", [P, SEQ])
        y_hi, y_lo = sb("y_hi", [P, SEQ], F32R), sb("y_lo", [P, SEQ], F32R)
        cos_sin = sb("cos_sin", [P, 2, SEQ])
        band_t, conv_t, norm_t = sb("band", [P, BAND]), sb("conv", [P, HEADS * 3 * LAGS]), sb("norm", [P, HEADS])
        norm2 = sb("norm2", [P, 2 * TPB])
        rnorm = [sb(f"rnorm{p}", [P, 2 * TPB]) for p in range(2)]
        ones = sb("ones", [P, 1])
        ssum = mem["ssum"]

        A, B = bank("A"), bank("B")
        scores = bank("scores", (P, TPB, 256))
        NORM_AT = 160
        VT, O = bank("VT"), bank("O")
        OP = [bank(f"OP{j}") for j in range(2)]

        ahead = before(ctx, [t[:, :] for t in (*swapped, cq, ck, y, cv[0])], [wo_hi[1][:, :], wo_lo[1][:, :]],
                       [t[:, :] for t in (VT, O, *OP, A, B)])

        s_const = sem("const")
        s_init = sem("init")
        s_rows = sem("rows")
        s_save = sem("save")
        s_raw = sem("raw")
        s_whi, s_wlo = sem("whi"), sem("wlo")
        s_q, s_k, s_v, s_z = sem("q"), sem("k"), sem("v"), sem("z")
        s_sq, s_sk, s_sv, s_sz = sem("sq"), sem("sk"), sem("sv"), sem("sz")
        s_cqk = sem("cqk")
        s_cv = sem("cv")
        s_swap = [sem(f"swap_{n}") for n in "qk"]
        s_cos = sem("cos")
        s_rot = sem("rot")
        s_sqr = sem("sqr")
        s_s = sem("s")
        s_n2 = sem("n2")
        s_rn = sem("rn")
        s_b = sem("b")
        s_gate = sem("gate")
        s_p1 = sem("p1")
        s_p2 = sem("p2")
        s_vt, s_val = sem("vt"), sem("val")
        s_o, s_otok, s_ot = sem("o"), sem("otok"), sem("ot")
        s_osq = sem("osq")
        s_y, s_yhi, s_ylo = sem("y"), sem("yhi"), sem("ylo")
        s_op = sem("op")
        s_acc = sem("acc")

        def slots(eng, task):
            def slot(i, c):
                steps = []
                for lag in range(4):
                    ok = not isinstance(i, int) or 0 <= 8 * i + c - lag < STEPS
                    steps.append(Step(i, c - lag) if ok else None)
                task(*steps)

            for c in range(3):
                slot(0, c)
            with eng.Fori(0, STEPS // 8 - 1) as i:
                for c in range(3, 11):
                    slot(i, c)
            for c in range(3, 11):
                slot(STEPS // 8 - 1, c)

        class Step:

            def __init__(self, i, c):
                if not isinstance(i, int):
                    self.s, self.head = i * 8 + c, i * 2 + c // BATCH
                else:
                    self.s, self.head = 8 * i + c, 2 * i + c // BATCH
                self.b, self.buf, self.wbuf = c % BATCH, c % 2, (c // BATCH) % 2
                self.known = isinstance(i, int)

            def past(self, eng, sem_, per=1, back=1):
                until(eng, sem_, (self.s - (back - 1)) * per)

            def past_apart(self, eng, sem_):
                self.past(eng, sem_)
                if not self.known:
                    eng.nop(nofuse=True)

            def now(self, eng, sem_, per=1, part=None):
                eng.wait_ge(sem_, self.s * per + (per if part is None else part))

        def next_head(st):
            return not st.known or st.head + 1 < HEADS

        def at(t, col):
            return t[:, bass.ds(col, 1)]

        with nc.Block() as block:
            @block.sync
            def _(sp):
                def load(head):
                    one = slice(head, head + 1) if isinstance(head, int) else bass.ds(head, 1)
                    sp.dma_start(raw[:, :, :, :].rearrange("p a k n -> p (a k n)"),
                                 w_heads[one, :, :].rearrange("a p n -> (a p) n")).then_inc(s_raw, 16)
                    sp.dma_start(raw_out[:, :], w_out[one, :, :].rearrange("a p n -> (a p) n")).then_inc(s_raw, 16)

                for part in ahead:
                    part.early(sp)
                load(0)
                for t, src in ((cos_sin[:, :, :].rearrange("p a n -> p (a n)"), tables), (band_t[:, :], band),
                               (conv_t[:, :], conv), (norm_t[:, :], norm_w)):
                    sp.dma_start(t, src).then_inc(s_const, 16)
                for part in ahead:
                    part.sync(sp)
                sp.wait_ge(s_rows, 1)
                sp.dma_start(saved, x_tok[:, :]).then_inc(s_save, 16)

                def task(f, l1, l2, l3):
                    if f:
                        if f.b == 0 and next_head(f):
                            wait_apart(sp, s_wlo, f.head * 5 + 5)
                            load(f.head + 1)
                        f.past_apart(sp, s_gate)
                        row = f.head + HEADS
                        src = lag_b[slice(row, row + 1) if isinstance(row, int) else bass.ds(row, 1),
                                    f.b * SEQ:(f.b + 1) * SEQ]
                        sp.dma_start(b_row[:, 0:SEQ], src.to_broadcast([P, SEQ])).then_inc(s_b, 16)
                        for n, c in enumerate((cq, ck)):
                            f.now(sp, s_cqk, 8, 7 + n)
                            if not f.known:
                                sp.nop(nofuse=True)
                            f.past(sp, s_rot, 4)
                            for half in range(2):
                                to, of = half * 64, 64 - half * 64
                                sp.dma_start(swapped[n][to:to + 64, :], c[of:of + 64, :]).then_inc(s_swap[n], 16)

                slots(sp, task)

            @block.tensor
            def _(pe):
                def projection(st, n, out, done):
                    cols = slice(st.b * SEQ, (st.b + 1) * SEQ)
                    product(pe, out[:, :],
                            [(w_hi[st.wbuf][:, n, k, :], w_lo[st.wbuf][:, n, k, :]) for k in range(KC)],
                            [(xT_hi[:, k, cols], xT_lo[:, k, cols]) for k in range(KC)]).then_inc(done, 1)

                def task(f, l1, l2, l3):
                    if f:
                        if f.b == 0:
                            pe.wait_ge(s_wlo, f.head * 5 + 5)
                        f.past(pe, s_sv)
                        projection(f, 0, A, s_q)
                        if l3:
                            l3.now(pe, s_sz)
                        projection(f, 1, B, s_k)
                    if l2:
                        l2.now(pe, s_p2)
                        l2.now(pe, s_val)
                        l2.past(pe, s_y)
                        for t in range(TPB):
                            out = O[:, t * HDIM:(t + 1) * HDIM]
                            last = pe.matmul(out, prob[:, t, 0:P], values[:, t, :], start=True, stop=True)
                            if t:
                                last = pe.matmul(out[0:PAD, :], prob[:, t - 1, P:BAND], values[:, t - 1, :],
                                                 start=False, stop=True, skip_group_check=True)
                        last.then_inc(s_o, 1)
                    if f:
                        f.now(pe, s_sq)
                        projection(f, 2, A, s_v)
                    if l2:
                        l2.now(pe, s_otok)
                        for t in range(TPB):
                            last = pe.transpose(O[:, t * P:(t + 1) * P], o_tok[:, t, :], ident[:, :])
                        last.then_inc(s_ot, 1)
                        if f:
                            f.now(pe, s_sk)
                        elif l1:
                            l1.now(pe, s_sk)
                        if l3:
                            l3.now(pe, s_sz)
                        projection(l2, 3, B, s_z)
                    if l3:
                        l3.now(pe, s_ylo)
                        for t in range(TPB):
                            pe.wait_ge(s_acc, l3.s * TPB + (t + 1))
                            tok = slice(t * P, (t + 1) * P)
                            product(pe, OP[t % 2][:, :], [(y_hi[:, tok], y_lo[:, tok])],
                                    [(wo_hi[l3.wbuf][:, :], wo_lo[l3.wbuf][:, :])]).then_inc(s_op, 1)
                    if l1:
                        l1.now(pe, s_sqr, 2)
                        l1.past(pe, s_p1)
                        for n in range(2):
                            for t in range(TPB):
                                col = NORM_AT + n * TPB + t
                                pe.matmul(scores[:, 0, col:col + 1], squares[:, n, t * P:(t + 1) * P], ones[:, :],
                                          start=True, stop=True)
                        l1.now(pe, s_rot, 4)
                        for t in range(TPB):
                            last = pe.matmul(scores[:, t, 0:BAND], rot_k[l1.buf][:, t * P:(t + 1) * P],
                                             rot_q[l1.buf][:, t * P:t * P + BAND], start=True, stop=True)
                        last.then_inc(s_s, 1)
                        l1.now(pe, s_cv, CONV)
                        l1.past(pe, s_val)
                        for t in range(TPB):
                            last = pe.transpose(VT[:, t * P:(t + 1) * P], cv[l1.buf][:, t * P:(t + 1) * P], ident[:, :])
                        last.then_inc(s_vt, 1)

                for part in ahead:
                    part.tensor(pe)
                pe.wait_ge(s_init, 2)
                slots(pe, task)

            @block.scalar
            def _(act):
                def split_hi(head, buf, mats):
                    act.wait_ge(s_raw, head * 32 + 32)
                    for n in mats:
                        if n < 4:
                            act.activation(w_hi[buf][:, n, :, :], raw[:, n, :, :], ACT.Copy).then_inc(s_whi, 1)
                        else:
                            act.activation(wo_hi[buf][:, :], raw_out[:, :], ACT.Copy).then_inc(s_whi, 1)

                split_hi(0, 0, range(5))
                for part in ahead:
                    part.early_scalar(act)
                for part in ahead:
                    part.scalar(act)
                act.wait_ge(s_init, 2)

                def task(f, l1, l2, l3):
                    if f:
                        for n, (done, src, out) in enumerate(((s_q, A, s_sq), (s_k, B, s_sk))):
                            f.now(act, done)
                            f.past(act, s_cqk, 8, 2)
                            act.activation(act_in[n][f.buf][:, PAD:], src[:, :], ACT.Silu).then_inc(out, 1)
                    if l2:
                        l2.now(act, s_o)
                        l2.past(act, s_ot)
                        l2.past(act, s_osq)
                        for t in range(TPB):
                            last = act.activation(o_tok[:, t, :], O[:, t * HDIM:(t + 1) * HDIM], ACT.Copy,
                                                  scale=rnorm[l2.buf][:, t:t + 1])
                        last.then_inc(s_otok, 1)
                    if f:
                        f.now(act, s_v)
                        f.past(act, s_cv, CONV, 2)
                        act.activation(act_in[2][f.buf][:, PAD:], A[:, :], ACT.Silu).then_inc(s_sv, 1)
                    if l1:
                        l1.now(act, s_b, 16)
                        l1.past_apart(act, s_p1)
                        for t in range(TPB):
                            tok = l1.b * TPB + t
                            last = act.activation(gate[:, t, :], b_row[:, t * P:t * P + BAND], ACT.Tanh,
                                                  scale=at(lag_a, l1.head + tok * HEADS))
                        last.then_inc(s_gate, 1)
                    if l2:
                        l2.now(act, s_otok)
                        l2.past_apart(act, s_ylo)
                        for t in range(TPB):
                            tok = l2.b * TPB + t
                            last = act.activation(y[:, t * P:(t + 1) * P], o_tok[:, t, :], ACT.Square,
                                                  accum_out=at(ssum, l2.head + tok * HEADS))
                        last.then_inc(s_osq, 1)
                        l2.now(act, s_z)
                        l2.now(act, s_osq)
                        act.activation(y[:, :], B[:, :], ACT.Silu).then_inc(s_sz, 1)
                        l2.now(act, s_y)
                        l2.past(act, s_op, TPB)
                        act.activation(y_hi[:, :], y[:, :], ACT.Copy).then_inc(s_yhi, 1)
                    if f:
                        f.past(act, s_s)
                        for n, c in enumerate((cq, ck)):
                            f.now(act, s_cqk, 8, 7 + n)
                            act.activation(squares[:, n, :], c[:, :], ACT.Square).then_inc(s_sqr, 1)
                    if l1:
                        l1.now(act, s_vt)
                        l1.now(act, s_rn)
                        l1.past(act, s_o)
                        for t in range(TPB):
                            last = act.activation(values[:, t, :], VT[:, t * P:(t + 1) * P], ACT.Copy,
                                                  scale=rnorm[l1.buf][:, TPB + t:TPB + t + 1])
                        last.then_inc(s_val, 1)
                    if f and f.b >= 2 and next_head(f):
                        if f.b == 3:
                            f.past(act, s_op, TPB, 3)
                        else:
                            f.past(act, s_z, 1, 3)
                        split_hi(f.head + 1, 1 - f.wbuf, range(3) if f.b == 2 else range(3, 5))

                slots(act, task)

            @block.gpsimd
            def _(pool):
                def split_lo(head, buf, mats):
                    for n in mats:
                        pool.wait_ge(s_whi, head * 5 + (n + 1))
                        if n < 4:
                            pool.tensor_tensor(w_lo[buf][:, n, :, :], raw[:, n, :, :], f32(w_hi[buf][:, n, :, :]),
                                               ALU.subtract).then_inc(s_wlo, 1)
                        else:
                            pool.tensor_tensor(wo_lo[buf][:, :], raw_out[:, :], f32(wo_hi[buf][:, :]),
                                               ALU.subtract).then_inc(s_wlo, 1)

                for part in ahead:
                    part.gpsimd(pool)
                split_lo(0, 0, range(5))
                pool.wait_ge(s_const, 64)

                def task(f, l1, l2, l3):
                    if f:
                        f.past(pool, s_s, 1, 2)
                        for n, (c, out) in enumerate(((cq, rot_q[f.buf][:, 0:SEQ]), (ck, rot_k[f.buf][:, :]))):
                            f.now(pool, s_cqk, 8, 7 + n)
                            pool.tensor_tensor(out, c[:, :], cos_sin[:, 0, :], ALU.mult).then_inc(s_cos, 1)
                    if l2:
                        l2.now(pool, s_yhi)
                        pool.tensor_tensor(y_lo[:, :], y[:, :], f32(y_hi[:, :]), ALU.subtract).then_inc(s_ylo, 1)
                    if l1:
                        l1.now(pool, s_n2)
                        pool.tensor_tensor(rnorm[l1.buf][:, :], norm2[:, :], mem["minus_half"][:, 0:2 * TPB],
                                           ALU.pow).then_inc(s_rn, 1)
                        l1.now(pool, s_p1)
                        pool.tensor_tensor(prob[:, :, :], prob[:, :, :],
                                           band_t[:, :].unsqueeze(1).to_broadcast([P, TPB, BAND]),
                                           ALU.mult).then_inc(s_p2, 1)
                    if f and f.b >= 2 and next_head(f):
                        split_lo(f.head + 1, 1 - f.wbuf, range(3) if f.b == 2 else range(3, 5))

                slots(pool, task)

            @block.vector
            def _(dve):
                for part in ahead:
                    part.vector(dve)
                dve.sem_inc(s_rows, 1)
                dve.sem_inc(s_acc, 2)
                for n in range(3):
                    for p in range(2):
                        dve.memset(act_in[n][p][:, 0:PAD], 0.0)
                for p in range(2):
                    dve.memset(rot_q[p][:, SEQ:], 0.0)
                dve.memset(b_row[:, SEQ:], 0.0)
                dve.memset(ones[:, :], 1.0).then_inc(s_init, 1)
                dve.tensor_scalar(lag_a, lag_a, 0.5, None, ALU.mult).then_inc(s_init, 1)
                dve.wait_ge(s_save, 16)
                dve.memset(x_tok[:, :], 0.0)
                dve.wait_ge(s_const, 64)

                def tap(n, st, src, out, j):
                    wj = at(conv_t, st.head * (3 * LAGS) + (n * LAGS + j))
                    x = src[:, j:j + SEQ]
                    if j == 0:
                        return dve.tensor_scalar(out, x, wj, None, ALU.mult)
                    return dve.scalar_tensor_tensor(out, x, wj, out, op0=ALU.mult, op1=ALU.add)

                def task(f, l1, l2, l3):
                    if f:
                        f.now(dve, s_sq)
                        for n in range(2):
                            f.past(dve, s_swap[n], 32)
                        f.past(dve, s_cos, 2)
                        f.past(dve, s_sqr, 2)
                        for j in range(LAGS):
                            for n, out in enumerate((cq, ck)):
                                if j == 0 and n == 1:
                                    f.now(dve, s_sk)
                                if j:
                                    f.now(dve, s_cqk, 8, 2 * j + n - 1)
                                tap(n, f, act_in[n][f.buf], out[:, :], j).then_inc(s_cqk, 1)
                    if f:
                        f.now(dve, s_sv)
                        for j in range(LAGS):
                            if j:
                                f.now(dve, s_cv, CONV, j)
                            tap(2, f, act_in[2][f.buf], cv[f.buf][:, :], j).then_inc(s_cv, 1)
                    if l2:
                        l2.now(dve, s_ot)
                        l2.now(dve, s_sz)
                        dve.scalar_tensor_tensor(y[:, :], O[:, :], at(norm_t, l2.head), y[:, :],
                                                 op0=ALU.mult, op1=ALU.mult).then_inc(s_y, 1)
                    if l3:
                        for t in range(TPB):
                            row = x_tok[:, (l3.b * TPB + t) * HID:(l3.b * TPB + t + 1) * HID]
                            dve.wait_ge(s_op, l3.s * TPB + (t + 1))
                            dve.wait_ge(s_acc, l3.s * TPB + (t + 1))
                            dve.tensor_tensor(row, OP[t % 2][:, :], row, ALU.add).then_inc(s_acc, 1)
                    if f:
                        for n, (rot, sw) in enumerate(((rot_q[f.buf][:, 0:SEQ], swapped[0]),
                                                       (rot_k[f.buf][:, :], swapped[1]))):
                            f.now(dve, s_swap[n], 32)
                            dve.tensor_tensor(sw[:, :], sw[:, :], cos_sin[:, 1, :], ALU.mult).then_inc(s_rot, 1)
                        for n, (rot, sw) in enumerate(((rot_q[f.buf][:, 0:SEQ], swapped[0]),
                                                       (rot_k[f.buf][:, :], swapped[1]))):
                            f.now(dve, s_cos, 2, n + 1)
                            f.now(dve, s_rot, 4, n + 1)
                            dve.tensor_tensor(rot, rot, sw[:, :], ALU.add).then_inc(s_rot, 1)
                    if l1:
                        l1.now(dve, s_s)
                        l1.past(dve, s_rn)
                        dve.tensor_scalar(norm2[:, :], scores[:, 0, NORM_AT:NORM_AT + 2 * TPB], 1e-24, None,
                                          ALU.max).then_inc(s_n2, 1)
                        l1.now(dve, s_gate)
                        l1.past(dve, s_o)
                        dve.scalar_tensor_tensor(prob[:, :, :], gate[:, :, :], 1.0, scores[:, :, 0:BAND],
                                                 op0=ALU.add, op1=ALU.mult).then_inc(s_p1, 1)

                slots(dve, task)


class Route(Part):
    CENTER, LOWER, UPPER = 1.0 / math.e, 0.5 - math.log(4.0 / 3.0), 0.5

    def __init__(self, nc, ctx, logits, temperature, number):
        sem = Sems(nc, "route")

        def small(what, shape):
            return ctx.enter_context(nc.sbuf_tensor(f"route_{what}", shape, F32))[:, :]

        def tile(what):
            return small(what, [P, NTT * EXPERTS]).rearrange("p (j e) -> p j e", e=EXPERTS)

        self.inh, self.dist, self.zone, self.wz, self.fb = (tile(n) for n in ("inh", "dist", "zone", "wz", "fb"))
        self.key, self.picked, self.both, self.left = (tile(n) for n in ("key", "picked", "both", "left"))
        self.best, self.total, self.none, self.some = (small(n, [P, NTT]) for n in ("best", "total", "none", "some"))
        self.num, self.temp, self.inv_t = small("num", [P, EXPERTS]), small("temp", [P, 1]), small("inv_t", [P, 1])
        self.s_in, self.s_own, self.s_t = sem("in"), sem("own"), sem("t")
        self.s_inh, self.s_dist, self.s_exp = sem("inh"), sem("dist"), sem("exp")
        self.out = logits.rearrange("p (j e) -> p j e", e=EXPERTS)
        self.temperature, self.number = temperature, number

    def early(self, sp):
        sp.dma_start(self.num, self.number).then_inc(self.s_in, 16)
        sp.dma_start(self.temp, self.temperature.rearrange("(a n) -> a n", a=1).to_broadcast([P, 1])).then_inc(self.s_in, 16)

    def scalar(self, act):
        act.wait_ge(self.s_t, 1)
        act.activation(self.inh, self.out, ACT.Sigmoid, scale=self.inv_t).then_inc(self.s_inh, 1)
        act.wait_ge(self.s_dist, 1)
        act.activation(self.dist, self.dist, ACT.Abs).then_inc(self.s_exp, 1)
        act.wait_ge(self.s_exp, 1)
        act.activation(self.wz, self.dist, ACT.Exp, scale=-1.0 / 0.1).then_inc(self.s_exp, 1)
        act.activation(self.fb, self.dist, ACT.Exp, scale=-1.0 / 0.3).then_inc(self.s_exp, 1)

    def vector(self, dve):
        inh, dist, zone, wz, fb, out = self.inh, self.dist, self.zone, self.wz, self.fb, self.out
        key, picked, both, left = self.key, self.picked, self.both, self.left
        best, total, none, some = self.best, self.total, self.none, self.some
        CENTER, LOWER, UPPER, E = self.CENTER, self.LOWER, self.UPPER, EXPERTS
        over = lambda t: t.unsqueeze(2).to_broadcast([P, NTT, E])
        dve.wait_ge(self.s_in, 32)
        dve.reciprocal(self.inv_t, self.temp).then_inc(self.s_t, 1)
        step = Chain(dve, self.s_own).link
        dve.wait_ge(self.s_inh, 1)
        dve.tensor_scalar(dist, inh, CENTER, None, ALU.subtract).then_inc(self.s_dist, 1)
        step(dve.tensor_scalar(zone, inh, LOWER, None, ALU.is_ge))
        step(dve.scalar_tensor_tensor(zone, inh, UPPER, zone, op0=ALU.is_le, op1=ALU.mult))
        dve.wait_ge(self.s_exp, 3)
        step(dve.tensor_tensor(wz, wz, zone, ALU.mult))
        step(dve.tensor_reduce(total, wz, AX.X, ALU.add))
        step(dve.tensor_scalar(none, total, 1e-8, None, ALU.is_lt))
        step(dve.tensor_copy(left, fb))
        for n in range(2):
            step(dve.tensor_reduce(best, left, AX.X, ALU.max))
            step(dve.tensor_tensor(key, left, over(best), ALU.is_ge))
            step(dve.scalar_tensor_tensor(key, key, -float(E),
                                          self.num.unsqueeze(1).to_broadcast([P, NTT, E]),
                                          op0=ALU.mult, op1=ALU.add))
            step(dve.tensor_reduce(best, key, AX.X, ALU.min))
            step(dve.tensor_tensor(picked, key, over(best), ALU.is_equal))
            if n == 0:
                step(dve.tensor_copy(both, picked))
                step(dve.scalar_tensor_tensor(left, picked, -4.0, left, op0=ALU.mult, op1=ALU.add))
            else:
                step(dve.tensor_tensor(both, both, picked, ALU.add))
        step(dve.tensor_tensor(fb, fb, both, ALU.mult))
        step(dve.tensor_reduce(total, fb, AX.X, ALU.add))
        step(dve.tensor_scalar(total, total, 1e-8, None, ALU.max))
        step(dve.reciprocal(total, total))
        step(dve.tensor_tensor(fb, fb, over(total), ALU.mult))
        step(dve.tensor_scalar(some, none, -1.0, 1.0, ALU.mult, ALU.add))
        step(dve.tensor_tensor(wz, wz, over(some), ALU.mult))
        step(dve.tensor_tensor(fb, fb, over(none), ALU.mult))
        step(dve.tensor_tensor(wz, wz, fb, ALU.add))
        step(dve.tensor_reduce(total, wz, AX.X, ALU.add))
        step(dve.tensor_scalar(total, total, 1e-8, None, ALU.max))
        step(dve.reciprocal(total, total))
        step(dve.tensor_tensor(out, wz, over(total), ALU.mult))


def program(nc, a, out):
    lag_b = nc.dram_tensor("lag_b_scratch", [2 * HEADS, TOK], F32, kind="Internal").ap()
    saved = nc.dram_tensor("residual_scratch", [P, NTT * HID], F32, kind="Internal").ap()
    with ExitStack() as ctx:
        mem = {}
        for name, shape in (("x_tok", [P, NTT * HID]), ("ident", [P, P]), ("minus_half", [P, NTT])):
            mem[name] = ctx.enter_context(nc.sbuf_tensor(name, shape, F32))
        s_id = ctx.enter_context(nc.semaphore("s_ident"))
        with nc.Block() as block:
            @block.sync
            def _(sp):
                sp.dma_start(mem["ident"][:, :], a["identity"]).then_inc(s_id, 16)
                sp.wait_ge(s_id, 16)

            @block.vector
            def _(dve):
                dve.memset(mem["minus_half"][:, :], -0.5)

        pooled_attention(nc, mem, a["x"], {n: a["w_" + n] for n in ("q", "qa", "k", "ka", "v")}, a["columns"])
        for name in ("xT_hi", "xT_lo"):
            mem[name] = ctx.enter_context(nc.sbuf_tensor(name, [P, KC, TOK], F32R))
        gated_units(nc, "dense", mem, a["dense_gate"], a["dense_up"], a["dense_down"], INNER // UNIT,
                    lambda ctx, plain, parts, banks: [Norm(nc, ctx, "turn0", mem, plain[0:TPB], banks[0:TPB],
                                                            normalise=False)],
                    scales=(a["dense_gate_scale"], a["dense_up_scale"], a["dense_down_scale"].to_broadcast([P, HID])))
        with nc.sbuf_tensor("lag_a", [P, NTT * HEADS], F32) as lag_a, nc.sbuf_tensor("ssum", [P, NTT * HEADS], F32) as ssum:
            mem["ssum"] = ssum

            def before_heads(ctx, plain, parts, banks):
                return [Norm(nc, ctx, "norm1", mem, plain[0:TPB], banks[0:TPB]),
                        Projection(nc, ctx, "factors", mem, a["head_factors"], 2 * HEADS, lag_a[:, :], HEADS,
                                   parts, plain[TPB:], banks[TPB:], by_feature=lag_b)]

            lagged_attention(nc, mem, a["head_weights"], a["head_out"], a["conv"], a["head_norm"], a["rotation"],
                             a["band"], lag_a[:, :], lag_b, saved, before_heads)

            with nc.sbuf_tensor("expert_weight", [P, NTT * EXPERTS], F32) as expert_weight:
                def before_experts(ctx, plain, parts, banks):
                    return [Norm(nc, ctx, "norm2", mem, plain[0:TPB], banks[0:TPB], rms=(saved, plain[-TPB:], ssum[:, :])),
                            Projection(nc, ctx, "router", mem, a["router"], EXPERTS, expert_weight[:, :], EXPERTS,
                                       parts, plain[TPB:TPB + 2], banks[TPB:TPB + 2]),
                            Route(nc, ctx, expert_weight[:, :], a["temperature"], a["numbers"])]

                gated_units(nc, "experts", mem, a["expert_gate"], a["expert_up"], a["expert_down"],
                            EXPERTS * EXPERT_WIDTH // UNIT, before_experts, expert_weight=expert_weight[:, :])
        with phase(nc) as stack:
            last = Norm(nc, stack, "norm3", mem, store=out)
            with nc.Block() as block:
                block.sync(last.sync)
                block.vector(last.vector)
                block.gpsimd(last.gpsimd)


def kernel(**inputs):
    import concourse.bacc as bacc
    from concourse.bass_utils import run_bass_kernel_spmd

    v = {k: np.asarray(t) for k, t in inputs.items()}

    def rows_first(w):
        return w.reshape(KC, P, -1).transpose(1, 0, 2).reshape(P, -1)

    def padded(w):
        return np.pad(w, ((0, 0), (0, P - w.shape[1])))

    def columns(t):
        return t.reshape(-1, P).T

    def by_unit_in(w):
        return w.reshape(KC, P, -1, UNIT).transpose(2, 1, 0, 3).reshape(-1, P, KC * UNIT)

    def by_unit_out(w):
        return w.reshape(-1, FPU, P, HID).transpose(0, 2, 1, 3).reshape(-1, P, FPU * HID)

    def experts_in(w):
        return w.reshape(EXPERTS, KC, P, -1, UNIT).transpose(0, 3, 2, 1, 4).reshape(-1, P, KC * UNIT)

    inv = (1.0 / ROPE_BASE ** (np.arange(0, HDIM, 2, dtype=np.float32) / HDIM)).astype(np.float32)
    angle = np.arange(SEQ, dtype=np.float32)[:, None] * inv[None, :]
    cos, sin = np.cos(angle).astype(np.float32).T, np.sin(angle).astype(np.float32).T
    rotation = np.concatenate([np.concatenate([cos, cos], 0), np.concatenate([-sin, sin], 0)], 1)
    lag = np.arange(P + LAGS - 1)[None, :] - np.arange(P)[:, None]
    band = np.where((lag >= 0) & (lag < LAGS), 0.5 / math.sqrt(HDIM), 0.0).astype(np.float32)

    arrays = {
        "x": v["L0_attn_hidden_states"],
        "identity": np.eye(P, dtype=np.float32),
        "columns": np.concatenate([columns(v["L0_attn_" + n]) for n in
                                   ("ln_g", "ln_b", "bq", "bqa", "bk", "bka", "bv")], 1),
        **{"w_" + n: rows_first(v["L0_attn_W" + n].T) for n in ("q", "qa", "k", "ka", "v")},
        "dense_gate": by_unit_in(v["L0_ffn_gate_w"].T),
        "dense_up": by_unit_in(v["L0_ffn_up_w"].T),
        "dense_down": by_unit_out(v["L0_ffn_down_w"].T),
        "dense_gate_scale": columns(v["L0_ffn_gate_scale"]),
        "dense_up_scale": columns(v["L0_ffn_up_scale"]),
        "dense_down_scale": v["L0_ffn_down_scale"].reshape(1, HID),
        "head_weights": np.stack([v["L1_attn_W" + n].reshape(KC, P, HEADS, HDIM) for n in "qkvz"], 0)
                          .transpose(3, 2, 0, 1, 4).reshape(HEADS, P, 4 * KC * HDIM),
        "head_out": v["L1_attn_Wout"].reshape(HEADS, P, HID),
        "head_factors": rows_first(padded(np.concatenate([v["L1_attn_Wa"], v["L1_attn_Wb"]], 1))),
        "conv": np.stack([v[f"L1_attn_conv_{n}_w"].reshape(HEADS, HDIM, LAGS) for n in "qkv"], 0)
                  .transpose(2, 1, 0, 3).reshape(P, HEADS * 3 * LAGS),
        "head_norm": v["L1_attn_norm_w"].reshape(HEADS, P).T,
        "rotation": rotation,
        "band": band,
        "router": rows_first(padded(v["L1_ffn_Wr"])),
        "temperature": v["L1_ffn_temperature"],
        "numbers": np.broadcast_to(np.arange(EXPERTS, dtype=np.float32), (P, EXPERTS)),
        "expert_gate": experts_in(v["L1_ffn_Wg"]),
        "expert_up": experts_in(v["L1_ffn_Wu"]),
        "expert_down": by_unit_out(v["L1_ffn_Wd"].reshape(-1, HID)),
    }
    nc = bacc.Bacc("TRN2", target_bir_lowering=False, num_devices=1)
    host, dram = {}, {}
    for name, t in arrays.items():
        host["in_" + name] = np.ascontiguousarray(t)
        dram[name] = nc.dram_tensor("in_" + name, t.shape, mybir.dt.from_np(t.dtype), kind="ExternalInput").ap()
    out = nc.dram_tensor("out", (TOK, HID), F32, kind="ExternalOutput").ap()
    program(nc, dram, out)
    result = run_bass_kernel_spmd(nc, [host], core_ids=[0])
    return result.results[0]["out"].reshape(BATCH, SEQ, HID)
```

```python
import math
from contextlib import ExitStack, contextmanager

import numpy as np

import concourse.bass as bass
from concourse import mybir

F32 = mybir.dt.float32
F32R = mybir.dt.float32r
I32 = mybir.dt.int32
ALU = mybir.AluOpType
ACT = mybir.ActivationFunctionType
AX = mybir.AxisListType

P = 128
BATCH, SEQ, HID = 4, 512, 512
TOK = BATCH * SEQ
KC = HID // P
NTT = TOK // P
TPB = SEQ // P
HEADS, HDIM, LAGS = 16, 128, 4
INNER = 2048
EXPERTS, EXPERT_WIDTH = 8, 512
UNIT = 256
FPU = UNIT // P
LN_EPS = 1e-5
RMS_EPS = 1e-6
ROPE_BASE = 1000000.0


def f32(ap):
    return ap.bitcast(F32)


def product(pe, out, left, right, first=True, last=True):
    n = len(left)
    for k in range(n):
        (lh, ll), (rh, rl) = left[k], right[k]
        pe.matmul(out, lh, rh, start=first and k == 0, stop=False)
        pe.matmul(out, lh, rl, start=False, stop=False)
        done = pe.matmul(out, ll, rh, start=False, stop=last and k == n - 1)
    return done


class Sems:

    def __init__(self, nc, prefix):
        self.nc, self.prefix = nc, prefix

    def __call__(self, name):
        return self.nc.alloc_semaphore(name=f"{self.prefix}_{name}")


@contextmanager
def phase(nc):
    with nc.cleanup_on_exit(), ExitStack() as ctx:
        yield ctx


def wait_apart(eng, sem, value):
    eng.wait_ge(sem, value)
    if not isinstance(value, int):
        eng.nop(nofuse=True)


class Chain:

    def __init__(self, eng, sem):
        self.eng, self.sem, self.n = eng, sem, 0

    def link(self, ins):
        ins.then_inc(self.sem, 1)
        self.n += 1
        self.eng.wait_ge(self.sem, self.n)


class Part:

    def early(self, sp):
        pass

    early_scalar = sync = scalar = vector = tensor = early


class Norm(Part):

    def __init__(self, nc, ctx, name, mem, rows=None, banks=None, normalise=True, rms=None, store=None,
                 then=None):
        sem = Sems(nc, name)
        self.mem, self.normalise, self.turn, self.rms, self.store = mem, normalise, banks is not None, rms, store
        self.rows, self.then = rows, then
        self.turned = banks and [b.rearrange("p (k n) -> p k n", n=P) for b in banks]
        small = lambda what, shape: ctx.enter_context(nc.sbuf_tensor(f"{name}_{what}", shape, F32))
        self.stats, self.mv = small("stats", [P, TPB, 6]), small("mv", [P, TPB, 2])
        self.std, self.rstd = small("std", [P, TPB]), small("rstd", [P, TPB])
        if rms:
            self.ms = small("ms", [P, NTT])
            self.saved, self.res, self.ssum = rms
            self.s_ms = sem("ms")
            self.s_root = sem("root")
            self.s_res = sem("res")
            self.s_sum = sem("sum")
        self.s_stat = sem("stat")
        self.s_aggr = sem("aggr")
        self.s_var = sem("var")
        self.s_std = sem("std")
        self.s_row = sem("row")
        self.s_xn = sem("xn")
        self.s_turn = sem("turn")
        self.s_hi = sem("hi")
        self.s_lo = sem("lo")
        self.s_store = sem("store")

    def row(self, g, t):
        return self.mem["x_tok"][:, bass.ds((g * TPB + t) * HID, HID)]

    def load(self, sp, g):
        for t in range(TPB):
            sp.dma_start(self.res[t], self.saved[:, bass.ds((g * TPB + t) * HID, HID)]).then_inc(self.s_res, 16)

    def early(self, sp):
        if self.rms:
            self.load(sp, 0)

    def sync(self, sp):
        if self.rms:
            with sp.Fori(1, BATCH) as g:
                wait_apart(sp, self.s_sum, g * TPB)
                self.load(sp, g)
        if self.store is not None:
            with sp.Fori(0, BATCH) as g:
                wait_apart(sp, self.s_row, g * TPB + TPB)
                sp.dma_start(self.store.rearrange("(j p) n -> p j n", p=P)[:, bass.ds(g * TPB, TPB), :],
                             self.mem["x_tok"][:, bass.ds(g * (TPB * HID), TPB * HID)]
                             .rearrange("p (j n) -> p j n", n=HID)).then_inc(self.s_store, 16)
            sp.wait_ge(self.s_store, 16 * BATCH)

    def statistics(self, dve, g):
        if self.rms:
            wait_apart(dve, self.s_res, (g + 1) * (16 * TPB))
            for t in range(TPB):
                dve.scalar_tensor_tensor(self.row(g, t), self.row(g, t), self.ms[:, bass.ds(g * TPB + t, 1)],
                                         self.res[t], op0=ALU.mult, op1=ALU.add).then_inc(self.s_sum, 1)
            wait_apart(dve, self.s_sum, g * TPB + TPB)
        for t in range(TPB):
            dve.bn_stats(self.stats[:, t, :], self.row(g, t)).then_inc(self.s_stat, 1)
        wait_apart(dve, self.s_stat, g * TPB + TPB)
        for t in range(TPB):
            dve.bn_aggr(self.mv[:, t, :], self.stats[:, t, :]).then_inc(self.s_aggr, 1)
        wait_apart(dve, self.s_aggr, g * TPB + TPB)
        dve.tensor_scalar(self.std[:, :], self.mv[:, :, 1], LN_EPS, None, ALU.add).then_inc(self.s_var, 1)

    def normalised(self, dve, g, t, out):
        return dve.tensor_scalar(out, self.row(g, t), self.mv[:, t, 0:1], self.rstd[:, t:t + 1],
                                 ALU.subtract, ALU.mult)

    def put(self, dve, g, t):
        if self.normalise:
            self.normalised(dve, g, t, self.rows[t]).then_inc(self.s_xn, 1)
        else:
            dve.tensor_copy(self.rows[t], self.row(g, t)).then_inc(self.s_xn, 1)

    def vector(self, dve):
        dve.sem_inc(self.s_lo, TPB)
        if self.rms:
            dve.tensor_reduce(self.ms[:, :], self.ssum.rearrange("p (j h) -> p j h", h=HEADS), AX.X,
                              ALU.add).then_inc(self.s_ms, 1)
            dve.wait_ge(self.s_ms, 1)
            dve.tensor_scalar(self.ms[:, :], self.ms[:, :], 1.0 / (HEADS * HDIM), RMS_EPS,
                              ALU.mult, ALU.add).then_inc(self.s_ms, 1)
            dve.wait_ge(self.s_root, 1)

        def remainder(g, t):
            wait_apart(dve, self.s_hi, g * TPB + (t + 1))
            cols = bass.ds((g * TPB + t) * P, P)
            dve.tensor_tensor(self.mem["xT_lo"][:, :, cols], self.turned[t],
                              f32(self.mem["xT_hi"][:, :, cols]), ALU.subtract).then_inc(self.s_lo, 1)

        if self.normalise:
            self.statistics(dve, 0)
            dve.wait_ge(self.s_std, 1)
        for t in range(TPB):
            self.put(dve, 0, t)
        with dve.Fori(0, BATCH - 1) as g:
            if self.normalise:
                self.statistics(dve, g + 1)
            for t in range(TPB):
                remainder(g, t)
                if self.normalise:
                    if t == 0:
                        dve.wait_ge(self.s_std, g + 2)
                    wait_apart(dve, self.s_row, g * TPB + (t + 1))
                self.put(dve, g + 1, t)
        for t in range(TPB):
            remainder(BATCH - 1, t)

    def rows_done(self, dve, g):
        self.statistics(dve, g)
        dve.wait_ge(self.s_std, g + 1)
        for t in range(TPB):
            self.normalised(dve, g, t, self.row(g, t)).then_inc(self.s_row, 1)

    def root(self, pool, g):
        wait_apart(pool, self.s_var, g + 1)
        pool.tensor_tensor(self.rstd[:, :], self.std[:, :], self.mem["minus_half"][:, 0:TPB],
                           ALU.pow).then_inc(self.s_std, 1)

    def gpsimd(self, pool, between):
        half = self.mem["minus_half"]
        if self.rms:
            pool.wait_ge(self.s_ms, 2)
            pool.tensor_tensor(self.ms[:, :], self.ms[:, :], half[:, 0:NTT], ALU.pow).then_inc(self.s_root, 1)
        if self.then:
            self.then.split(pool)
        for g in range(BATCH):
            if self.normalise:
                self.root(pool, g)
            if g < len(between):
                between[g](pool)

    def scalar(self, act, between=None):
        if self.turn:
            for g in range(BATCH):
                if between and g == 1:
                    between(act)
                for t in range(TPB):
                    wait_apart(act, self.s_turn, g * TPB + (t + 1))
                    cols = bass.ds((g * TPB + t) * P, P)
                    act.activation(self.mem["xT_hi"][:, :, cols], self.turned[t], ACT.Copy).then_inc(self.s_hi, 1)
                    if self.normalise:
                        act.activation(self.row(g, t), self.rows[t], ACT.Copy).then_inc(self.s_row, 1)
                if self.then and g:
                    self.then.scalar_row(act, g - 1)
            if self.then:
                self.then.scalar_row(act, BATCH - 1)

    def tensor(self, pe):
        if self.turn:
            for g in range(BATCH):
                for t in range(TPB):
                    pe.wait_ge(self.s_xn, g * TPB + (t + 1))
                    pe.wait_ge(self.s_lo, g * TPB + (t + 1))
                    for k in range(KC):
                        last = pe.transpose(self.turned[t][:, k, :], self.rows[t][:, k * P:(k + 1) * P],
                                            self.mem["ident"][:, :])
                    last.then_inc(self.s_turn, 1)
                if self.then and g:
                    self.project(pe, g - 1)
            pe.wait_ge(self.s_lo, NTT + TPB)
            if self.then:
                self.project(pe, BATCH - 1)
                self.then.turn_row(pe, BATCH - 1)

    def project(self, pe, g):
        if g:
            self.then.turn_row(pe, g - 1)
        pe.wait_ge(self.s_lo, (g + 2) * TPB)
        self.then.product_row(pe, g)


def gated_units(nc, name, mem, w_gate, w_up, w_down, units, before, name_after, scales=None, expert_weight=None,
                store=None):
    x_tok, xT_hi, xT_lo = mem["x_tok"], mem["xT_hi"], mem["xT_lo"]
    quantised = scales is not None
    with phase(nc) as ctx:
        sem = Sems(nc, name)

        def sb(what, shape, dt=F32):
            return ctx.enter_context(nc.sbuf_tensor(f"{name}_{what}", shape, dt))

        def bank(what):
            return ctx.enter_context(nc.psum_tensor(f"{name}_{what}", [P, 512], F32))

        W = KC * UNIT
        raw = [[sb(f"raw{p}{m}", [P, W], I32 if quantised else F32) for m in range(3)] for p in range(2)]
        w_hi = [[sb(f"whi{p}{m}", [P, W], F32R) for m in range(3)] for p in range(2)]
        w_lo = [[sb(f"wlo{p}{m}", [P, W], F32R) for m in range(3)] for p in range(2)]
        gated = [sb(f"gated{r}", [P, SEQ]) for r in range(2)]
        inner = [sb(f"inner{r}", [P, SEQ]) for r in range(2)]
        in_hi = [sb(f"inhi{r}", [P, FPU, SEQ], F32R) for r in range(2)]
        in_lo = [sb(f"inlo{r}", [P, FPU, SEQ], F32R) for r in range(2)]
        if quantised:
            scale_gate = sb("sgate", [P, units * FPU])
            scale_up = sb("sup", [P, units * FPU])
            scale_down = sb("sdown", [P, HID])
            flat = [[raw[p][m][:, :].bitcast(F32) for m in range(3)] for p in range(2)]
        else:
            flat = [[raw[p][m][:, :] for m in range(3)] for p in range(2)]
        G = [bank(f"G{r}") for r in range(2)]
        U = [bank(f"U{r}") for r in range(2)]
        D = [bank(f"D{r}") for r in range(TPB)]

        s_const = sem("const")
        s_raw = [sem(f"raw{p}") for p in range(2)]
        s_deq = sem("deq")
        s_whi = sem("whi")
        s_wlo = sem("wlo")
        s_g = sem("g")
        s_u = sem("u")
        s_silu = sem("silu")
        s_h = sem("h")
        s_hhi = sem("hhi")
        s_hlo = sem("hlo")
        s_d = sem("d")
        s_acc = sem("acc")
        spare = [flat[1][m][:, k * HID:(k + 1) * HID] for m in range(3) for k in range(W // HID)]
        spare += [t[:, :] for t in (*gated, *inner)]
        s_ahead = sem("ahead")
        ahead = before(ctx, spare, [w_hi[1][0][:, k * HID:(k + 1) * HID] for k in range(2)],
                       [b[:, :] for b in (*D, *G, *U)])
        after = Norm(nc, ctx, name_after, mem, store=store)
        NB = 2
        CH = FPU * BATCH

        def rotated(eng, before, body):
            before()
            with eng.Fori(0, units // 2 - 1) as i:
                body(i, False)
            body(units // 2 - 1, True)

        def weight_split_hi(act, pair, u, p):
            for m in range(3):
                if quantised:
                    act.wait_ge(s_deq, u * 3 + (m + 1))
                elif m == 0:
                    act.wait_ge(s_raw[p], pair * 48 + 48)
                act.activation(w_hi[p][m][:, :], flat[p][m], ACT.Copy).then_inc(s_whi, 1)

        with nc.Block() as block:
            @block.sync
            def _(sp):
                if quantised:
                    for t, src in ((scale_gate, scales[0]), (scale_up, scales[1]), (scale_down, scales[2])):
                        sp.dma_start(t[:, :], src).then_inc(s_const, 16)

                def load(u, p):
                    for m, w in enumerate((w_gate, w_up, w_down)):
                        src = w[u, :, :] if isinstance(u, int) else w[bass.ds(u, 1), :, :].rearrange("a p n -> (a p) n")
                        sp.dma_start(raw[p][m][:, :], src).then_inc(s_raw[p], 16)

                for part in ahead:
                    part.early(sp)
                load(0, 0)
                for part in ahead:
                    part.sync(sp)
                sp.wait_ge(s_ahead, 1)
                load(1, 1)
                with sp.Fori(1, units // 2) as i:
                    for p in range(2):
                        wait_apart(sp, s_wlo, (2 * i + (p - 1)) * 3)
                        load(2 * i + p, p)
                after.sync(sp)

            @block.tensor
            def _(pe):
                for part in ahead:
                    part.tensor(pe)
                pe.sem_inc(s_ahead, 1)
                pe.sem_inc(s_d, 2 * TPB)

                def gate_up(u, t, p):
                    if t == 0:
                        pe.wait_ge(s_wlo, u * 3 + 2)
                    for f in range(FPU):
                        r = u * CH + (t * FPU + f)
                        pe.wait_ge(s_h, r + 1)
                        cols = slice(t * SEQ, (t + 1) * SEQ)
                        for m, (out, done) in enumerate(((G, s_g), (U, s_u))):
                            left = [(w_hi[p][m][:, k * UNIT + f * P:k * UNIT + (f + 1) * P],
                                     w_lo[p][m][:, k * UNIT + f * P:k * UNIT + (f + 1) * P]) for k in range(KC)]
                            right = [(xT_hi[:, k, cols], xT_lo[:, k, cols]) for k in range(KC)]
                            product(pe, out[f][:, :], left, right).then_inc(done, 1)

                def down(u, t, p):
                    s = u * BATCH + t
                    if t == 0:
                        pe.wait_ge(s_wlo, u * 3 + 3)
                    pe.wait_ge(s_hlo, s * FPU + 2 + FPU)
                    for tt in range(TPB):
                        pe.wait_ge(s_acc, s * TPB + (tt + 1))
                        at = slice(tt * P, (tt + 1) * P)
                        left = [(in_hi[t % 2][:, f, at], in_lo[t % 2][:, f, at]) for f in range(FPU)]
                        right = [(w_hi[p][2][:, f * HID:(f + 1) * HID], w_lo[p][2][:, f * HID:(f + 1) * HID])
                                 for f in range(FPU)]
                        product(pe, D[tt][:, :], left, right).then_inc(s_d, 1)

                def body(i, last):
                    steps = [(2 * i + p, t, p) for p in range(2) for t in range(BATCH)]
                    for n, step in enumerate(steps):
                        if n + 1 < len(steps):
                            gate_up(*steps[n + 1])
                        elif not last:
                            gate_up(2 * i + 2, 0, 0)
                        down(*step)

                rotated(pe, lambda: gate_up(0, 0, 0), body)

            @block.scalar
            def _(act):
                if quantised:
                    act.wait_ge(s_const, 48)
                for part in ahead:
                    part.early_scalar(act)
                if quantised:
                    ahead[0].scalar(act)
                    weight_split_hi(act, 0, 0, 0)
                else:
                    ahead[0].scalar(act, lambda act: weight_split_hi(act, 0, 0, 0))
                for part in ahead[1:]:
                    part.scalar(act)

                def step(u, t, p):
                    for f in range(FPU):
                        r = u * CH + (t * FPU + f)
                        act.wait_ge(s_g, r + 1)
                        wait_apart(act, s_h, r + 1)
                        if quantised:
                            sc = scale_gate[:, bass.ds(u * FPU + f, 1)]
                            act.activation(gated[f][:, :], G[f][:, :], ACT.Silu, scale=sc).then_inc(s_silu, 1)
                        else:
                            act.activation(gated[f][:, :], G[f][:, :], ACT.Silu).then_inc(s_silu, 1)
                        act.wait_ge(s_h, r + 3)
                        act.wait_ge(s_d, (u * BATCH + t) * TPB + TPB)
                        act.activation(in_hi[t % 2][:, f, :], inner[f][:, :], ACT.Copy).then_inc(s_hhi, 1)

                def body(i, last):
                    for p in range(2):
                        for t in range(BATCH):
                            step(2 * i + p, t, p)
                            if t == 1 and not (last and p):
                                act.wait_ge(s_d, (2 * i + p) * (BATCH * TPB) + 2 * TPB)
                                weight_split_hi(act, i + p, 2 * i + p + 1, 1 - p)

                rotated(act, lambda: None, body)

            @block.gpsimd
            def _(pool):
                pool.sem_inc(s_hlo, 2)

                def weight_split_lo(u, p, mats=range(3)):
                    for m in mats:
                        pool.wait_ge(s_whi, u * 3 + (m + 1))
                        pool.tensor_tensor(w_lo[p][m][:, :], flat[p][m], f32(w_hi[p][m][:, :]),
                                           ALU.subtract).then_inc(s_wlo, 1)

                ahead[0].gpsimd(pool, [lambda pool, m=m: weight_split_lo(0, 0, (m,)) for m in range(3)])

                def body(i, last):
                    for p in range(2):
                        for t in range(BATCH):
                            for f in range(FPU):
                                r = (2 * i + p) * CH + (t * FPU + f)
                                pool.wait_ge(s_hhi, r + 1)
                                pool.tensor_tensor(in_lo[t % 2][:, f, :], inner[f][:, :],
                                                   f32(in_hi[t % 2][:, f, :]), ALU.subtract).then_inc(s_hlo, 1)
                            if t == 1 and not (last and p):
                                weight_split_lo(2 * i + p + 1, 1 - p)
                            if last and p and t:
                                after.root(pool, t - 1)
                    if last:
                        after.root(pool, BATCH - 1)

                rotated(pool, lambda: None, body)

            @block.vector
            def _(dve):
                dve.sem_inc(s_h, NB)
                dve.sem_inc(s_acc, TPB)

                def dequantise(pair, p):
                    dve.wait_ge(s_raw[p], pair * 48 + 48)
                    for m in range(2):
                        dve.tensor_scalar(flat[p][m], raw[p][m][:, :], 128.0, None,
                                          ALU.subtract).then_inc(s_deq, 1)
                    for f in range(FPU):
                        last = dve.scalar_tensor_tensor(flat[p][2][:, f * HID:(f + 1) * HID],
                                                        raw[p][2][:, f * HID:(f + 1) * HID], 128.0,
                                                        scale_down[:, :], op0=ALU.subtract, op1=ALU.mult)
                    last.then_inc(s_deq, 1)

                def inner_chunks(u, t, p):
                    for f in range(FPU):
                        r = u * CH + (t * FPU + f)
                        dve.wait_ge(s_silu, r + 1)
                        dve.wait_ge(s_u, r + 1)
                        dve.wait_ge(s_hlo, r + 1)
                        if quantised:
                            ins = dve.scalar_tensor_tensor(inner[f][:, :], U[f][:, :],
                                                           scale_up[:, bass.ds(u * FPU + f, 1)], gated[f][:, :],
                                                           op0=ALU.mult, op1=ALU.mult)
                        else:
                            ins = dve.tensor_tensor(inner[f][:, :], U[f][:, :], gated[f][:, :], ALU.mult)
                        ins.then_inc(s_h, 1)

                def add(u, t, p, e):
                    for tt in range(TPB):
                        s = (u * BATCH + t) * TPB + tt
                        dve.wait_ge(s_d, s + 2 * TPB + 1)
                        dve.wait_ge(s_acc, s + 1)
                        j = t * TPB + tt
                        row = x_tok[:, j * HID:(j + 1) * HID]
                        if expert_weight is None:
                            ins = dve.tensor_tensor(row, D[tt][:, :], row, ALU.add)
                        else:
                            ins = dve.scalar_tensor_tensor(row, D[tt][:, :],
                                                           expert_weight[:, bass.ds(e + j * EXPERTS, 1)], row,
                                                           op0=ALU.mult, op1=ALU.add)
                        ins.then_inc(s_acc, 1)

                for part in ahead:
                    part.vector(dve)
                if quantised:
                    dve.wait_ge(s_const, 48)
                    dequantise(0, 0)

                def rows_done(u, t):
                    dve.wait_ge(s_acc, (u * BATCH + t) * TPB + 2 * TPB)
                    after.rows_done(dve, t)

                def body(i, last):
                    steps = [(2 * i + p, t, p) for p in range(2) for t in range(BATCH)]
                    for n, (u, t, p) in enumerate(steps):
                        if n + 1 < len(steps):
                            inner_chunks(*steps[n + 1])
                        elif not last:
                            inner_chunks(2 * i + 2, 0, 0)
                        if quantised and t == 0 and not (last and p):
                            dequantise(i + p, 1 - p)
                        if last and p and t:
                            rows_done(u, t - 1)
                        add(u, t, p, i)
                    if last:
                        rows_done(u, BATCH - 1)

                rotated(dve, lambda: inner_chunks(0, 0, 0), body)


def until(eng, sem, value):
    if not isinstance(value, int) or value > 0:
        eng.wait_ge(sem, value)


def pooled_attention(nc, mem, x, w, biases):
    x_tok, ident = mem["x_tok"], mem["ident"]
    NAMES = ("q", "qa", "k", "ka", "v")
    SCALE = 1.0 / math.sqrt(HID)
    with phase(nc) as ctx:
        sem = Sems(nc, "pool")

        def sb(what, shape, dt=F32):
            return ctx.enter_context(nc.sbuf_tensor(f"pool_{what}", shape, dt))

        w_hi = {n: sb(f"w{n}_hi", [P, KC, HID], F32R) for n in NAMES}
        w_lo = {n: sb(f"w{n}_lo", [P, KC, HID], F32R) for n in NAMES}
        h_hi, h_lo = sb("h_hi", [P, KC, SEQ], F32R), sb("h_lo", [P, KC, SEQ], F32R)
        m_hi, m_lo = sb("m_hi", [P, KC, SEQ], F32R), sb("m_lo", [P, KC, SEQ], F32R)
        xn = sb("xn", [P, TPB, HID])
        hf = [sb(f"hf{j}", [P, SEQ]) for j in range(2)]
        qf, kf, vf = sb("qf", [P, KC, SEQ]), sb("kf", [P, KC, SEQ]), sb("vf", [P, KC, SEQ])
        mixed, res = sb("mixed", [P, KC, SEQ]), sb("res", [P, KC, SEQ])
        expw = [sb(f"expw{j}", [P, SEQ]) for j in range(KC)]
        ones = sb("ones", [P, 1])
        col = sb("col", [P, 7 * KC])
        scaled = sb("scaled", [P, 2 * KC])
        stats, mv = sb("stats", [P, TPB, 6]), sb("mv", [P, TPB, 2])
        var, rstd = sb("var", [P, TPB]), sb("rstd", [P, TPB])
        stats2, mv2 = sb("stats2", [P, TPB, 6]), sb("mv2", [P, TPB, 2])
        var2, rstd2 = sb("var2", [P, TPB]), sb("rstd2", [P, TPB])
        banks = [ctx.enter_context(nc.psum_tensor(f"pool_bank{j}", [P, SEQ], F32)) for j in range(4)]
        turned = [ctx.enter_context(nc.psum_tensor(f"pool_turned{j}", [P, TPB, P], F32)) for j in range(2)]
        back = [ctx.enter_context(nc.psum_tensor(f"pool_back{j}", [P, HID], F32)) for j in range(2)]
        G_, B_, BQ, BQA, BK, BKA, BV = (lambda k, n=n: col[:, n * KC + k:n * KC + k + 1] for n in range(7))
        staging = {"q": qf, "k": kf, "qa": mixed, "v": vf, "ka": res}
        ORDER = ("q", "k", "qa", "v", "ka")

        s_x = sem("x")
        s_col = sem("col")
        s_raw = {n: sem(f"raw_{n}") for n in NAMES}
        s_whi = sem("whi")
        s_wlo_d = sem("wlod")
        s_wlo_p = sem("wlop")
        s_scaled = sem("scaled")
        s_ones = sem("ones")
        s_n1 = sem("n1")
        s_r1 = sem("r1")
        s_t = sem("t")
        s_hf = sem("hf")
        s_hhi, s_hlo = sem("hhi"), sem("hlo")
        s_mm = sem("mm")
        s_ev = sem("ev")
        s_qhi, s_qlo = sem("qhi"), sem("qlo")
        s_mhi, s_mlo = sem("mhi"), sem("mlo")
        s_step = {k: sem(f"step_{k}") for k in ("qa", "ka")}
        s_gain = {k: sem(f"gain_{k}") for k in ("qa", "ka")}
        s_out = {k: sem(f"out_{k}") for k in ("qa", "ka")}
        s_b = sem("b")
        s_add = sem("add")
        s_n2 = sem("n2")
        s_r2 = sem("r2")
        N1 = 4 * TPB
        N2 = 4 * TPB
        ROW = 4 * KC
        FRONT, SLOT = 3 * KC, 5 * KC

        def place(kind, b, m):
            if isinstance(b, int) and b == 0 and kind in ("q", "k", "qa"):
                return ("q", "k", "qa").index(kind) * KC + m
            if isinstance(b, int) and b == BATCH - 1 and kind == "ka":
                return FRONT + b * SLOT + KC + m
            own = b if kind in ("v", "ka") else b - 1
            return FRONT + own * SLOT + ("v", "q", "ka", "k", "qa").index(kind) * KC + m

        def step(b, m, n):
            return b * ROW + (m // 2 * 8 + n * 2 + m % 2)

        def in_slots(eng, prologue, slot):
            prologue()
            slot(0, 1)
            with eng.Fori(1, BATCH - 1) as i:
                slot(i, i + 1)
            slot(BATCH - 1, None)

        def later(b):
            return not isinstance(b, int) or b > 0

        with nc.Block() as block:
            @block.sync
            def _(sp):
                view = x_tok[:, :].rearrange("p (j n) -> p j n", n=HID)

                def row(b):
                    if b:
                        sp.wait_ge(s_x, b * 16)
                    sp.dma_start(view[:, b * TPB:(b + 1) * TPB, :],
                                 x[b, :, :].rearrange("(j p) n -> p j n", p=P)).then_inc(s_x, 16)

                def weight(n):
                    sp.dma_start(staging[n][:, :, :].rearrange("p a b -> p (a b)"), w[n]).then_inc(s_raw[n], 16)

                row(0)
                weight("q")
                sp.dma_start(col[:, :], biases).then_inc(s_col, 16)
                for n in ORDER[1:]:
                    weight(n)
                for b in range(1, BATCH):
                    row(b)

            @block.tensor
            def _(pe):
                def weights_ready(n):
                    at = ORDER.index(n)
                    pe.wait_ge(s_wlo_p if at % 2 else s_wlo_d, at // 2 + 1)

                def chunks(kind, b, rh, rl):
                    for m in range(KC):
                        at = place(kind, b, m)
                        until(pe, s_ev, at - 3)
                        product(pe, banks[m][:, :],
                                [(w_hi[kind][:, k, m * P:(m + 1) * P], w_lo[kind][:, k, m * P:(m + 1) * P])
                                 for k in range(KC)],
                                [(rh[:, k, :], rl[:, k, :]) for k in range(KC)]).then_inc(s_mm, 1)

                def turn(b):
                    pe.wait_ge(s_n1, b * N1 + N1)
                    for k in range(KC):
                        until(pe, s_hf, b * KC + (k - 1))
                        for t in range(TPB):
                            last = pe.transpose(turned[k % 2][:, t, :], xn[:, t, k * P:(k + 1) * P], ident[:, :])
                        last.then_inc(s_t, 1)

                def queries(b):
                    pe.wait_ge(s_hlo, b * KC + KC)
                    chunks("q", b, h_hi, h_lo)

                def query_weights(b):
                    pe.wait_ge(s_qlo, b * KC + KC)
                    chunks("qa", b, m_hi, m_lo)

                def prologue():
                    turn(0)
                    weights_ready("q")
                    queries(0)
                    weights_ready("k")
                    chunks("k", 0, h_hi, h_lo)
                    weights_ready("qa")
                    query_weights(0)
                    weights_ready("v")
                    weights_ready("ka")

                def turn_back(b):
                    pe.wait_ge(s_out["ka"], b * KC + KC)
                    for t in range(TPB):
                        pe.wait_ge(s_add, b * TPB + (t + 1))
                        for m in range(KC):
                            last = pe.transpose(back[t % 2][:, m * P:(m + 1) * P], res[:, m, t * P:(t + 1) * P],
                                                ident[:, :])
                        last.then_inc(s_b, 1)

                def slot(b, nxt):
                    chunks("v", b, h_hi, h_lo)
                    if nxt is not None:
                        turn(nxt)
                        queries(nxt)
                    if later(b):
                        turn_back(b - 1)
                    pe.wait_ge(s_mlo, b * KC + KC)
                    chunks("ka", b, m_hi, m_lo)
                    if nxt is not None:
                        chunks("k", nxt, h_hi, h_lo)
                        query_weights(nxt)

                in_slots(pe, prologue, slot)
                turn_back(BATCH - 1)

            @block.scalar
            def _(act):
                act.wait_ge(s_col, 16)
                for n, c in ((0, 3), (1, 5)):
                    act.activation(scaled[:, n * KC:(n + 1) * KC], col[:, c * KC:(c + 1) * KC], ACT.Copy,
                                   scale=SCALE).then_inc(s_scaled, 1)
                act.wait_ge(s_scaled, 2)

                def split_hi(n):
                    act.wait_ge(s_raw[n], 16)
                    act.activation(w_hi[n][:, :, :], staging[n][:, :, :], ACT.Copy).then_inc(s_whi, 1)

                def bank(kind, b, m):
                    act.wait_ge(s_mm, place(kind, b, m) + 1)
                    return banks[m][:, :]

                def turn(b):
                    for k in range(KC):
                        act.wait_ge(s_t, b * KC + (k + 1))
                        until(act, s_hlo, b * KC + (k - 1))
                        act.activation(hf[k % 2][:, :], turned[k % 2][:, :, :].rearrange("p a b -> p (a b)"),
                                       ACT.Identity, bias=B_(k), scale=G_(k)).then_inc(s_hf, 1)
                        act.wait_ge(s_hf, b * KC + (k + 1))
                        if later(b):
                            act.wait_ge(s_mm, place("v", b - 1, KC - 1) + 1)
                        act.activation(h_hi[:, k, :], hf[k % 2][:, :], ACT.Copy).then_inc(s_hhi, 1)

                def queries(b):
                    for m in range(KC):
                        src = bank("q", b, m)
                        until(act, s_gain["qa"], b * KC)
                        act.activation(qf[:, m, :], src, ACT.Identity, bias=BQ(m)).then_inc(s_ev, 1)

                def split_queries(b):
                    for m in range(KC):
                        act.wait_ge(s_ev, place("q", b, m) + 1)
                        if later(b):
                            act.wait_ge(s_mm, place("ka", b - 1, KC - 1) + 1)
                        act.activation(m_hi[:, m, :], qf[:, m, :], ACT.Copy).then_inc(s_qhi, 1)

                def keys(b):
                    for m in range(KC):
                        src = bank("k", b, m)
                        until(act, s_out["qa"], b * KC)
                        act.activation(kf[:, m, :], src, ACT.Identity, bias=BK(m)).then_inc(s_ev, 1)

                def exponentials(kind, b, column, other, rows_of_other):
                    for m in range(KC):
                        src = bank(kind, b, m)
                        if later(rows_of_other):
                            act.wait_ge(s_out[other], (rows_of_other - 1) * KC + (m + 1))
                        act.activation(expw[m][:, :], src, ACT.Exp, bias=scaled[:, column + m:column + m + 1],
                                       scale=SCALE).then_inc(s_ev, 1)

                def split_mixed(b):
                    for m in range(KC):
                        act.wait_ge(s_out["qa"], b * KC + (m + 1))
                        act.wait_ge(s_mm, place("qa", b, KC - 1) + 1)
                        act.activation(m_hi[:, m, :], mixed[:, m, :], ACT.Copy).then_inc(s_mhi, 1)

                def prologue():
                    split_hi("q")
                    turn(0)
                    split_hi("k")
                    queries(0)
                    split_queries(0)
                    split_hi("qa")
                    keys(0)
                    split_hi("v")
                    split_hi("ka")
                    exponentials("qa", 0, 0, "ka", 0)

                def slot(b, nxt):
                    for m in range(KC):
                        src = bank("v", b, m)
                        until(act, s_out["ka"], b * KC)
                        act.activation(vf[:, m, :], src, ACT.Identity, bias=BV(m)).then_inc(s_ev, 1)
                    if nxt is not None:
                        turn(nxt)
                        queries(nxt)
                    split_mixed(b)
                    exponentials("ka", b, KC, "qa", b + 1)
                    if nxt is not None:
                        split_queries(nxt)
                        keys(nxt)
                        exponentials("qa", nxt, 0, "ka", nxt)

                in_slots(act, prologue, slot)

            @block.gpsimd
            def _(pool):
                def weight_lo(at):
                    n = ORDER[at]
                    pool.wait_ge(s_whi, at + 1)
                    pool.tensor_tensor(w_lo[n][:, :, :], staging[n][:, :, :], f32(w_hi[n][:, :, :]),
                                       ALU.subtract).then_inc(s_wlo_p, 1)

                def split_lo(hi_sem, lo_sem, hi, lo, src, b):
                    for m in range(KC):
                        pool.wait_ge(hi_sem, b * KC + (m + 1))
                        pool.tensor_tensor(lo[:, m, :], src(m), f32(hi[:, m, :]), ALU.subtract).then_inc(lo_sem, 1)

                def root(b, steps, n, src, out, done):
                    pool.wait_ge(steps, b * n + 3 * TPB)
                    pool.tensor_tensor(out[:, :], src[:, :], mem["minus_half"][:, 0:TPB], ALU.pow).then_inc(done, 1)

                def split_h(b):
                    split_lo(s_hhi, s_hlo, h_hi, h_lo, lambda m: hf[m % 2][:, :], b)

                def gain(kind, b, pair, by):
                    for m in (2 * pair, 2 * pair + 1):
                        pool.wait_ge(s_step[kind], step(b, m, 0) + 1)
                        pool.tensor_tensor(expw[m][:, :], expw[m][:, :], by[:, m, :],
                                           ALU.mult).then_inc(s_gain[kind], 1)

                def result(kind, b, pair, by, out):
                    for m in (2 * pair, 2 * pair + 1):
                        pool.wait_ge(s_step[kind], step(b, m, 3) + 1)
                        pool.tensor_tensor(out[:, m, :], expw[m][:, :], by[:, m, :], ALU.mult).then_inc(s_out[kind], 1)

                def prologue():
                    root(0, s_n1, N1, var, rstd, s_r1)
                    split_h(0)
                    weight_lo(1)
                    split_lo(s_qhi, s_qlo, m_hi, m_lo, lambda m: qf[:, m, :], 0)
                    weight_lo(3)

                def slot(b, nxt):
                    if nxt is not None:
                        root(nxt, s_n1, N1, var, rstd, s_r1)
                    gain("qa", b, 0, qf)
                    if nxt is not None:
                        split_h(nxt)
                    result("qa", b, 0, kf, mixed)
                    gain("qa", b, 1, qf)
                    result("qa", b, 1, kf, mixed)
                    split_lo(s_mhi, s_mlo, m_hi, m_lo, lambda m: mixed[:, m, :], b)
                    if later(b):
                        root(b - 1, s_n2, N2, var2, rstd2, s_r2)
                    gain("ka", b, 0, mixed)
                    if nxt is not None:
                        split_lo(s_qhi, s_qlo, m_hi, m_lo, lambda m: qf[:, m, :], nxt)
                    until(pool, s_b, b * TPB)
                    result("ka", b, 0, vf, res)
                    gain("ka", b, 1, mixed)
                    result("ka", b, 1, vf, res)

                in_slots(pool, prologue, slot)
                root(BATCH - 1, s_n2, N2, var2, rstd2, s_r2)

            @block.vector
            def _(dve):
                dve.sem_inc(s_add, 2)

                def row(b, t):
                    return x_tok[:, (b * TPB + t) * HID:(b * TPB + t + 1) * HID] if isinstance(b, int) else \
                        x_tok[:, bass.ds(b * (TPB * HID) + t * HID, HID)]

                def weight_lo(at):
                    n = ORDER[at]
                    dve.wait_ge(s_whi, at + 1)
                    dve.tensor_tensor(w_lo[n][:, :, :], staging[n][:, :, :], f32(w_hi[n][:, :, :]),
                                      ALU.subtract).then_inc(s_wlo_d, 1)

                def first_norm(b):
                    wait_apart(dve, s_x, b * 16 + 16)
                    at = b * N1
                    for t in range(TPB):
                        dve.bn_stats(stats[:, t, :], row(b, t)).then_inc(s_n1, 1)
                    for t in range(TPB):
                        wait_apart(dve, s_n1, at + (t + 1))
                        dve.bn_aggr(mv[:, t, :], stats[:, t, :]).then_inc(s_n1, 1)
                    for t in range(TPB):
                        dve.wait_ge(s_n1, at + (TPB + t + 1))
                        dve.tensor_scalar(var[:, t:t + 1], mv[:, t, 1:2], LN_EPS, None, ALU.add).then_inc(s_n1, 1)
                    dve.wait_ge(s_r1, b + 1)
                    if later(b):
                        dve.wait_ge(s_t, b * KC)
                    for t in range(TPB):
                        dve.tensor_scalar(xn[:, t, :], row(b, t), mv[:, t, 0:1], rstd[:, t:t + 1],
                                          ALU.subtract, ALU.mult).then_inc(s_n1, 1)

                def pooling(kind, b, out):
                    every = ones[:, :].to_broadcast([P, SEQ])
                    done = s_step[kind]

                    def own(m, n):
                        dve.wait_ge(done, step(b, m, n) + 1)

                    for pair in range(KC // 2):
                        both = [(m, expw[m][:, :], out[:, m, :]) for m in (2 * pair, 2 * pair + 1)]
                        for m, e, c in both:
                            dve.wait_ge(s_ev, place(kind, b, m) + 1)
                            dve.tensor_tensor_scan(c, every, e, 0.0, ALU.mult, ALU.add).then_inc(done, 1)
                        for m, e, c in both:
                            own(m, 0)
                            dve.reciprocal(c, c).then_inc(done, 1)
                        for m, e, c in both:
                            own(m, 1)
                            dve.wait_ge(s_gain[kind], b * KC + (m + 1))
                            dve.tensor_tensor(c, e, c, ALU.mult).then_inc(done, 1)
                        for m, e, c in both:
                            own(m, 2)
                            dve.tensor_tensor_scan(e, every, c, 0.0, ALU.mult, ALU.add).then_inc(done, 1)

                def second_norm(b):
                    at = b * N2
                    for t in range(TPB):
                        dve.wait_ge(s_b, b * TPB + (t + 1))
                        dve.tensor_tensor(row(b, t), row(b, t), back[t % 2][:, :], ALU.add).then_inc(s_add, 1)
                        wait_apart(dve, s_add, b * TPB + (t + 3))
                        dve.bn_stats(stats2[:, t, :], row(b, t)).then_inc(s_n2, 1)
                    for t in range(TPB):
                        wait_apart(dve, s_n2, at + (t + 1))
                        dve.bn_aggr(mv2[:, t, :], stats2[:, t, :]).then_inc(s_n2, 1)
                    for t in range(TPB):
                        dve.wait_ge(s_n2, at + (TPB + t + 1))
                        dve.tensor_scalar(var2[:, t:t + 1], mv2[:, t, 1:2], LN_EPS, None, ALU.add).then_inc(s_n2, 1)
                    dve.wait_ge(s_r2, b + 1)
                    for t in range(TPB):
                        dve.tensor_scalar(row(b, t), row(b, t), mv2[:, t, 0:1], rstd2[:, t:t + 1],
                                          ALU.subtract, ALU.mult).then_inc(s_n2, 1)

                def prologue():
                    dve.memset(ones[:, :], 1.0).then_inc(s_ones, 1)
                    dve.wait_ge(s_ones, 1)
                    first_norm(0)
                    weight_lo(0)
                    weight_lo(2)
                    weight_lo(4)

                def slot(b, nxt):
                    if nxt is not None:
                        first_norm(nxt)
                    pooling("qa", b, mixed)
                    if later(b):
                        second_norm(b - 1)
                    pooling("ka", b, res)

                in_slots(dve, prologue, slot)
                second_norm(BATCH - 1)


class Projection(Part):

    def __init__(self, nc, ctx, name, mem, w, n, by_token, n_tok, parts, plain, banks, by_feature=None):
        sem = Sems(nc, name)
        self.mem, self.w, self.n, self.n_tok = mem, w, n, n_tok
        self.by_token, self.by_feature = by_token, by_feature
        (self.w_hi, self.w_lo), (self.w_f, self.rows) = parts, plain
        self.prod, self.turned = banks
        self.s_w, self.s_hi, self.s_lo = sem("w"), sem("hi"), sem("lo")
        self.s_p = sem("p")
        self.s_r = sem("r")
        self.s_t = sem("t")
        self.s_c = sem("c")
        self.s_out = sem("out")

    def early(self, sp):
        sp.dma_start(self.w_f, self.w).then_inc(self.s_w, 16)

    def early_scalar(self, act):
        act.wait_ge(self.s_w, 16)
        act.activation(self.w_hi, self.w_f, ACT.Copy).then_inc(self.s_hi, 1)

    def split(self, pool):
        pool.wait_ge(self.s_hi, 1)
        pool.tensor_tensor(self.w_lo, self.w_f, f32(self.w_hi), ALU.subtract).then_inc(self.s_lo, 1)

    def sync(self, sp):
        if self.by_feature is not None:
            with sp.Fori(0, BATCH) as b:
                wait_apart(sp, self.s_r, b + 1)
                sp.dma_start(self.by_feature[:, bass.ds(b * SEQ, SEQ)], self.rows[0:self.n, :]).then_inc(self.s_out, 16)
            sp.wait_ge(self.s_out, 16 * BATCH)

    def product_row(self, pe, b):
        xT_hi, xT_lo = self.mem["xT_hi"], self.mem["xT_lo"]
        cols = slice(b * SEQ, (b + 1) * SEQ)
        if b:
            pe.wait_ge(self.s_r, b)
        else:
            pe.wait_ge(self.s_lo, 1)
        product(pe, self.prod, [(self.w_hi[:, k * P:(k + 1) * P], self.w_lo[:, k * P:(k + 1) * P]) for k in range(KC)],
                [(xT_hi[:, k, cols], xT_lo[:, k, cols]) for k in range(KC)]).then_inc(self.s_p, 1)

    def scalar_row(self, act, b):
        act.wait_ge(self.s_p, b + 1)
        if b:
            act.wait_ge(self.s_t, b)
            if self.by_feature is not None:
                act.wait_ge(self.s_out, 16 * b)
        act.activation(self.rows, self.prod, ACT.Copy).then_inc(self.s_r, 1)

    def turn_row(self, pe, b):
        pe.wait_ge(self.s_r, b + 1)
        for t in range(TPB):
            at = (b * TPB + t) * self.n_tok
            last = pe.matmul(self.turned[:, at:at + self.n_tok], self.rows[:, t * P:(t + 1) * P],
                             self.mem["ident"][:, 0:self.n_tok], start=True, stop=True)
        last.then_inc(self.s_t, 1)

    def vector(self, dve):
        dve.wait_ge(self.s_t, BATCH)
        dve.tensor_copy(self.by_token, self.turned[:, 0:NTT * self.n_tok]).then_inc(self.s_c, 1)
        dve.wait_ge(self.s_c, 1)
        if self.by_feature is not None:
            dve.wait_ge(self.s_out, 16 * BATCH)

    def tensor(self, pe):
        pe.wait_ge(self.s_c, 1)


def lagged_attention(nc, mem, w_heads, w_out, conv, norm_w, tables, band, lag_a, lag_b, saved, before):
    x_tok, xT_hi, xT_lo, ident = mem["x_tok"], mem["xT_hi"], mem["xT_lo"], mem["ident"]
    PAD = LAGS - 1
    BAND = P + PAD
    STEPS = HEADS * BATCH
    CONV = LAGS
    SPLIT_AT = {1: (0, 1), 2: (2, 3), 3: (4,)}
    with phase(nc) as ctx:
        sem = Sems(nc, "lag")

        def sb(what, shape, dt=F32):
            return ctx.enter_context(nc.sbuf_tensor(f"lag_{what}", shape, dt))

        def bank(what, shape=(P, SEQ)):
            return ctx.enter_context(nc.psum_tensor(f"lag_{what}", list(shape), F32))

        raw, raw_out = sb("raw", [P, 4, KC, HDIM]), sb("raw_out", [P, HID])
        w_hi = [sb(f"w_hi{p}", [P, 4, KC, HDIM], F32R) for p in range(2)]
        w_lo = [sb(f"w_lo{p}", [P, 4, KC, HDIM], F32R) for p in range(2)]
        wo_hi = [sb(f"wo_hi{p}", [P, HID], F32R) for p in range(2)]
        wo_lo = [sb(f"wo_lo{p}", [P, HID], F32R) for p in range(2)]
        act_in = [[sb(f"silu{n}{p}", [P, PAD + SEQ]) for p in range(2)] for n in "qkv"]
        cq, ck = sb("cq", [P, SEQ]), sb("ck", [P, SEQ])
        cv = [sb(f"cv{p}", [P, SEQ]) for p in range(2)]
        swapped = [sb(f"swapped{n}", [P, SEQ]) for n in "qk"]
        rot_q = [sb(f"rot_q{p}", [P, SEQ + PAD]) for p in range(2)]
        rot_k = [sb(f"rot_k{p}", [P, SEQ]) for p in range(2)]
        squares = sb("squares", [P, 2, SEQ])
        b_row = sb("b_row", [P, SEQ + PAD])
        gate = sb("gate", [P, TPB, BAND])
        prob = sb("prob", [P, TPB, BAND])
        values = sb("values", [P, TPB, HDIM])
        o_tok = sb("o_tok", [P, TPB, HDIM])
        y = sb("y", [P, SEQ])
        y_hi, y_lo = sb("y_hi", [P, SEQ], F32R), sb("y_lo", [P, SEQ], F32R)
        cos_sin = sb("cos_sin", [P, 2, SEQ])
        band_t, conv_t, norm_t = sb("band", [P, BAND]), sb("conv", [P, HEADS * 3 * LAGS]), sb("norm", [P, HEADS])
        norm2 = sb("norm2", [P, 2 * TPB])
        rnorm = [sb(f"rnorm{p}", [P, 2 * TPB]) for p in range(2)]
        ones = sb("ones", [P, 1])
        ssum = mem["ssum"]

        A, B = bank("A"), bank("B")
        scores = bank("scores", (P, TPB, 256))
        NORM_AT = 160
        VT, O = bank("VT"), bank("O")
        OP = [bank(f"OP{j}") for j in range(2)]

        ahead = before(ctx, [t[:, :] for t in (*swapped, cq, ck, y, cv[0])], [wo_hi[1][:, :], wo_lo[1][:, :]],
                       [t[:, :] for t in (VT, O, *OP, A, B)])

        s_const = sem("const")
        s_init = sem("init")
        s_save = sem("save")
        s_zero = sem("zero")
        s_raw = sem("raw")
        s_whi, s_wlo = sem("whi"), sem("wlo")
        s_q, s_k, s_v, s_z = sem("q"), sem("k"), sem("v"), sem("z")
        s_sq, s_sk, s_sv, s_sz = sem("sq"), sem("sk"), sem("sv"), sem("sz")
        s_cqk = sem("cqk")
        s_cv = sem("cv")
        s_swap = [sem(f"swap_{n}") for n in "qk"]
        s_cos = sem("cos")
        s_rot = sem("rot")
        s_sqr = sem("sqr")
        s_s = sem("s")
        s_n2 = sem("n2")
        s_rn = sem("rn")
        s_b = sem("b")
        s_gate = sem("gate")
        s_p1 = sem("p1")
        s_p2 = sem("p2")
        s_vt, s_val = sem("vt"), sem("val")
        s_o, s_otok, s_ot = sem("o"), sem("otok"), sem("ot")
        s_osq = sem("osq")
        s_y, s_yhi, s_ylo = sem("y"), sem("yhi"), sem("ylo")
        s_op = sem("op")
        s_acc = sem("acc")

        def slots(eng, task):
            def slot(i, c):
                steps = []
                for lag in range(4):
                    ok = not isinstance(i, int) or 0 <= 8 * i + c - lag < STEPS
                    steps.append(Step(i, c - lag) if ok else None)
                task(*steps)

            for c in range(3):
                slot(0, c)
            with eng.Fori(0, STEPS // 8 - 1) as i:
                for c in range(3, 11):
                    slot(i, c)
            for c in range(3, 11):
                slot(STEPS // 8 - 1, c)

        class Step:

            def __init__(self, i, c):
                if not isinstance(i, int):
                    self.s, self.head = i * 8 + c, i * 2 + c // BATCH
                else:
                    self.s, self.head = 8 * i + c, 2 * i + c // BATCH
                self.b, self.buf, self.wbuf = c % BATCH, c % 2, (c // BATCH) % 2
                self.known = isinstance(i, int)

            def past(self, eng, sem_, per=1, back=1):
                until(eng, sem_, (self.s - (back - 1)) * per)

            def past_apart(self, eng, sem_):
                self.past(eng, sem_)
                if not self.known:
                    eng.nop(nofuse=True)

            def now(self, eng, sem_, per=1, part=None):
                eng.wait_ge(sem_, self.s * per + (per if part is None else part))

        def next_head(st):
            return not st.known or st.head + 1 < HEADS

        def at(t, col):
            return t[:, bass.ds(col, 1)]

        with nc.Block() as block:
            @block.sync
            def _(sp):
                def load(head):
                    one = slice(head, head + 1) if isinstance(head, int) else bass.ds(head, 1)
                    sp.dma_start(raw[:, :, :, :].rearrange("p a k n -> p (a k n)"),
                                 w_heads[one, :, :].rearrange("a p n -> (a p) n")).then_inc(s_raw, 16)
                    sp.dma_start(raw_out[:, :], w_out[one, :, :].rearrange("a p n -> (a p) n")).then_inc(s_raw, 16)

                for part in ahead:
                    part.early(sp)
                load(0)
                for t, src in ((cos_sin[:, :, :].rearrange("p a n -> p (a n)"), tables), (band_t[:, :], band),
                               (conv_t[:, :], conv), (norm_t[:, :], norm_w)):
                    sp.dma_start(t, src).then_inc(s_const, 16)
                sp.dma_start(saved, x_tok[:, :]).then_inc(s_save, 16)
                for part in ahead:
                    part.sync(sp)

                def task(f, l1, l2, l3):
                    if f:
                        if f.b == 0 and next_head(f):
                            wait_apart(sp, s_wlo, f.head * 5 + 5)
                            load(f.head + 1)
                        f.past_apart(sp, s_gate)
                        row = f.head + HEADS
                        src = lag_b[slice(row, row + 1) if isinstance(row, int) else bass.ds(row, 1),
                                    f.b * SEQ:(f.b + 1) * SEQ]
                        sp.dma_start(b_row[:, 0:SEQ], src.to_broadcast([P, SEQ])).then_inc(s_b, 16)
                        for n, c in enumerate((cq, ck)):
                            f.now(sp, s_cqk, 8, 7 + n)
                            if not f.known:
                                sp.nop(nofuse=True)
                            f.past(sp, s_rot, 4)
                            for half in range(2):
                                to, of = half * 64, 64 - half * 64
                                sp.dma_start(swapped[n][to:to + 64, :], c[of:of + 64, :]).then_inc(s_swap[n], 16)

                slots(sp, task)

            @block.tensor
            def _(pe):
                def projection(st, n, out, done):
                    cols = slice(st.b * SEQ, (st.b + 1) * SEQ)
                    product(pe, out[:, :],
                            [(w_hi[st.wbuf][:, n, k, :], w_lo[st.wbuf][:, n, k, :]) for k in range(KC)],
                            [(xT_hi[:, k, cols], xT_lo[:, k, cols]) for k in range(KC)]).then_inc(done, 1)

                def out_projection(st, tiles):
                    for t in tiles:
                        pe.wait_ge(s_acc, st.s * TPB + (t + 1))
                        tok = slice(t * P, (t + 1) * P)
                        product(pe, OP[t % 2][:, :], [(y_hi[:, tok], y_lo[:, tok])],
                                [(wo_hi[st.wbuf][:, :], wo_lo[st.wbuf][:, :])]).then_inc(s_op, 1)

                def task(f, l1, l2, l3):
                    if f:
                        if f.b == 0:
                            pe.wait_ge(s_wlo, f.head * 5 + 3)
                        f.past(pe, s_sv)
                        projection(f, 0, A, s_q)
                        if l3:
                            l3.now(pe, s_sz)
                        projection(f, 1, B, s_k)
                    if l2:
                        l2.now(pe, s_p2)
                        l2.now(pe, s_val)
                        l2.past(pe, s_y)
                        for t in range(TPB):
                            out = O[:, t * HDIM:(t + 1) * HDIM]
                            last = pe.matmul(out, prob[:, t, 0:P], values[:, t, :], start=True, stop=True)
                            if t:
                                last = pe.matmul(out[0:PAD, :], prob[:, t - 1, P:BAND], values[:, t - 1, :],
                                                 start=False, stop=True, skip_group_check=True)
                        last.then_inc(s_o, 1)
                    if f:
                        f.now(pe, s_sq)
                        projection(f, 2, A, s_v)
                    if l2:
                        l2.now(pe, s_otok)
                        for t in range(TPB):
                            last = pe.transpose(O[:, t * P:(t + 1) * P], o_tok[:, t, :], ident[:, :])
                        last.then_inc(s_ot, 1)
                        if f:
                            f.now(pe, s_sk)
                        elif l1:
                            l1.now(pe, s_sk)
                        if l3:
                            l3.now(pe, s_sz)
                        if l2.b == 0:
                            pe.wait_ge(s_wlo, l2.head * 5 + 4)
                        projection(l2, 3, B, s_z)
                    if l3:
                        if l3.b == 0:
                            pe.wait_ge(s_wlo, l3.head * 5 + 5)
                        l3.now(pe, s_ylo)
                        out_projection(l3, (0, 1))
                    if l1:
                        l1.now(pe, s_sqr, 2)
                        l1.past(pe, s_p1)
                        for n in range(2):
                            for t in range(TPB):
                                col = NORM_AT + n * TPB + t
                                pe.matmul(scores[:, 0, col:col + 1], squares[:, n, t * P:(t + 1) * P], ones[:, :],
                                          start=True, stop=True)
                        l1.now(pe, s_rot, 4)
                        for t in range(TPB):
                            last = pe.matmul(scores[:, t, 0:BAND], rot_k[l1.buf][:, t * P:(t + 1) * P],
                                             rot_q[l1.buf][:, t * P:t * P + BAND], start=True, stop=True)
                        last.then_inc(s_s, 1)
                    if l3:
                        out_projection(l3, (2, 3))
                    if l1:
                        l1.now(pe, s_cv, CONV)
                        l1.past(pe, s_val)
                        for t in range(TPB):
                            last = pe.transpose(VT[:, t * P:(t + 1) * P], cv[l1.buf][:, t * P:(t + 1) * P], ident[:, :])
                        last.then_inc(s_vt, 1)

                for part in ahead:
                    part.tensor(pe)
                pe.wait_ge(s_init, 2)
                slots(pe, task)

            @block.scalar
            def _(act):
                def split_hi(head, buf, mats):
                    act.wait_ge(s_raw, head * 32 + 32)
                    for n in mats:
                        if n < 4:
                            act.activation(w_hi[buf][:, n, :, :], raw[:, n, :, :], ACT.Copy).then_inc(s_whi, 1)
                        else:
                            act.activation(wo_hi[buf][:, :], raw_out[:, :], ACT.Copy).then_inc(s_whi, 1)

                for part in ahead:
                    part.early_scalar(act)
                ahead[0].scalar(act, lambda act: split_hi(0, 0, range(5)))
                for part in ahead[1:]:
                    part.scalar(act)
                act.wait_ge(s_init, 2)

                def task(f, l1, l2, l3):
                    if f:
                        for n, (done, src, out) in enumerate(((s_q, A, s_sq), (s_k, B, s_sk))):
                            f.now(act, done)
                            f.past(act, s_cqk, 8, 2)
                            act.activation(act_in[n][f.buf][:, PAD:], src[:, :], ACT.Silu).then_inc(out, 1)
                    if l2:
                        l2.now(act, s_o)
                        l2.past(act, s_ot)
                        l2.past(act, s_osq)
                        for t in range(TPB):
                            last = act.activation(o_tok[:, t, :], O[:, t * HDIM:(t + 1) * HDIM], ACT.Copy,
                                                  scale=rnorm[l2.buf][:, t:t + 1])
                        last.then_inc(s_otok, 1)
                    if f:
                        f.now(act, s_v)
                        f.past(act, s_cv, CONV, 2)
                        act.activation(act_in[2][f.buf][:, PAD:], A[:, :], ACT.Silu).then_inc(s_sv, 1)
                    if l1:
                        l1.now(act, s_b, 16)
                        l1.past_apart(act, s_p1)
                        for t in range(TPB):
                            tok = l1.b * TPB + t
                            last = act.activation(gate[:, t, :], b_row[:, t * P:t * P + BAND], ACT.Tanh,
                                                  scale=at(lag_a, l1.head + tok * HEADS))
                        last.then_inc(s_gate, 1)
                    if l2:
                        l2.now(act, s_otok)
                        l2.past_apart(act, s_ylo)
                        for t in range(TPB):
                            tok = l2.b * TPB + t
                            last = act.activation(y[:, t * P:(t + 1) * P], o_tok[:, t, :], ACT.Square,
                                                  accum_out=at(ssum, l2.head + tok * HEADS))
                        last.then_inc(s_osq, 1)
                        l2.now(act, s_z)
                        l2.now(act, s_osq)
                        act.activation(y[:, :], B[:, :], ACT.Silu).then_inc(s_sz, 1)
                        l2.now(act, s_y)
                        l2.past(act, s_op, TPB)
                        act.activation(y_hi[:, :], y[:, :], ACT.Copy).then_inc(s_yhi, 1)
                    if f:
                        f.past(act, s_s)
                        for n, c in enumerate((cq, ck)):
                            f.now(act, s_cqk, 8, 7 + n)
                            act.activation(squares[:, n, :], c[:, :], ACT.Square).then_inc(s_sqr, 1)
                    if l1:
                        l1.now(act, s_vt)
                        l1.now(act, s_rn)
                        l1.past(act, s_o)
                        for t in range(TPB):
                            last = act.activation(values[:, t, :], VT[:, t * P:(t + 1) * P], ACT.Copy,
                                                  scale=rnorm[l1.buf][:, TPB + t:TPB + t + 1])
                        last.then_inc(s_val, 1)
                    if f and f.b and next_head(f):
                        if f.b == 1:
                            f.past(act, s_v, 1, 2)
                        elif f.b == 2:
                            f.past(act, s_z, 1, 3)
                        else:
                            f.past(act, s_op, TPB, 3)
                        split_hi(f.head + 1, 1 - f.wbuf, SPLIT_AT[f.b])

                slots(act, task)

            @block.gpsimd
            def _(pool):
                def split_lo(head, buf, mats):
                    for n in mats:
                        pool.wait_ge(s_whi, head * 5 + (n + 1))
                        if n < 4:
                            pool.tensor_tensor(w_lo[buf][:, n, :, :], raw[:, n, :, :], f32(w_hi[buf][:, n, :, :]),
                                               ALU.subtract).then_inc(s_wlo, 1)
                        else:
                            pool.tensor_tensor(wo_lo[buf][:, :], raw_out[:, :], f32(wo_hi[buf][:, :]),
                                               ALU.subtract).then_inc(s_wlo, 1)

                ahead[0].gpsimd(pool, [lambda pool: split_lo(0, 0, range(5))])
                pool.wait_ge(s_const, 64)

                def task(f, l1, l2, l3):
                    if f:
                        f.past(pool, s_s, 1, 2)
                        for n, (c, out) in enumerate(((cq, rot_q[f.buf][:, 0:SEQ]), (ck, rot_k[f.buf][:, :]))):
                            f.now(pool, s_cqk, 8, 7 + n)
                            pool.tensor_tensor(out, c[:, :], cos_sin[:, 0, :], ALU.mult).then_inc(s_cos, 1)
                    if l2:
                        l2.now(pool, s_yhi)
                        pool.tensor_tensor(y_lo[:, :], y[:, :], f32(y_hi[:, :]), ALU.subtract).then_inc(s_ylo, 1)
                    if l1:
                        l1.now(pool, s_n2)
                        pool.tensor_tensor(rnorm[l1.buf][:, :], norm2[:, :], mem["minus_half"][:, 0:2 * TPB],
                                           ALU.pow).then_inc(s_rn, 1)
                        l1.now(pool, s_p1)
                        pool.tensor_tensor(prob[:, :, :], prob[:, :, :],
                                           band_t[:, :].unsqueeze(1).to_broadcast([P, TPB, BAND]),
                                           ALU.mult).then_inc(s_p2, 1)
                    if f and f.b and next_head(f):
                        split_lo(f.head + 1, 1 - f.wbuf, SPLIT_AT[f.b])
                    if f and f.known and f.s == 1:
                        pool.wait_ge(s_save, 16)
                        pool.memset(x_tok[:, :], 0.0).then_inc(s_zero, 1)

                slots(pool, task)

            @block.vector
            def _(dve):
                for part in ahead:
                    part.vector(dve)
                dve.sem_inc(s_acc, 2)
                for n in range(3):
                    for p in range(2):
                        dve.memset(act_in[n][p][:, 0:PAD], 0.0)
                for p in range(2):
                    dve.memset(rot_q[p][:, SEQ:], 0.0)
                dve.memset(b_row[:, SEQ:], 0.0)
                dve.memset(ones[:, :], 1.0).then_inc(s_init, 1)
                dve.tensor_scalar(lag_a, lag_a, 0.5, None, ALU.mult).then_inc(s_init, 1)
                dve.wait_ge(s_const, 64)

                def tap(n, st, src, out, j):
                    wj = at(conv_t, st.head * (3 * LAGS) + (n * LAGS + j))
                    x = src[:, j:j + SEQ]
                    if j == 0:
                        return dve.tensor_scalar(out, x, wj, None, ALU.mult)
                    return dve.scalar_tensor_tensor(out, x, wj, out, op0=ALU.mult, op1=ALU.add)

                def task(f, l1, l2, l3):
                    if f:
                        f.now(dve, s_sq)
                        for n in range(2):
                            f.past(dve, s_swap[n], 32)
                        f.past(dve, s_cos, 2)
                        f.past(dve, s_sqr, 2)
                        for j in range(LAGS):
                            for n, out in enumerate((cq, ck)):
                                if j == 0 and n == 1:
                                    f.now(dve, s_sk)
                                if j:
                                    f.now(dve, s_cqk, 8, 2 * j + n - 1)
                                tap(n, f, act_in[n][f.buf], out[:, :], j).then_inc(s_cqk, 1)
                    if f:
                        f.now(dve, s_sv)
                        for j in range(LAGS):
                            if j:
                                f.now(dve, s_cv, CONV, j)
                            tap(2, f, act_in[2][f.buf], cv[f.buf][:, :], j).then_inc(s_cv, 1)
                    if l2:
                        l2.now(dve, s_ot)
                        l2.now(dve, s_sz)
                        dve.scalar_tensor_tensor(y[:, :], O[:, :], at(norm_t, l2.head), y[:, :],
                                                 op0=ALU.mult, op1=ALU.mult).then_inc(s_y, 1)
                    if l3:
                        for t in range(TPB):
                            row = x_tok[:, (l3.b * TPB + t) * HID:(l3.b * TPB + t + 1) * HID]
                            dve.wait_ge(s_op, l3.s * TPB + (t + 1))
                            dve.wait_ge(s_acc, l3.s * TPB + (t + 1))
                            dve.tensor_tensor(row, OP[t % 2][:, :], row, ALU.add).then_inc(s_acc, 1)
                    if f:
                        for n, (rot, sw) in enumerate(((rot_q[f.buf][:, 0:SEQ], swapped[0]),
                                                       (rot_k[f.buf][:, :], swapped[1]))):
                            f.now(dve, s_swap[n], 32)
                            dve.tensor_tensor(sw[:, :], sw[:, :], cos_sin[:, 1, :], ALU.mult).then_inc(s_rot, 1)
                        for n, (rot, sw) in enumerate(((rot_q[f.buf][:, 0:SEQ], swapped[0]),
                                                       (rot_k[f.buf][:, :], swapped[1]))):
                            f.now(dve, s_cos, 2, n + 1)
                            f.now(dve, s_rot, 4, n + 1)
                            dve.tensor_tensor(rot, rot, sw[:, :], ALU.add).then_inc(s_rot, 1)
                    if l1:
                        l1.now(dve, s_s)
                        l1.past(dve, s_rn)
                        dve.tensor_scalar(norm2[:, :], scores[:, 0, NORM_AT:NORM_AT + 2 * TPB], 1e-24, None,
                                          ALU.max).then_inc(s_n2, 1)
                        l1.now(dve, s_gate)
                        l1.past(dve, s_o)
                        dve.scalar_tensor_tensor(prob[:, :, :], gate[:, :, :], 1.0, scores[:, :, 0:BAND],
                                                 op0=ALU.add, op1=ALU.mult).then_inc(s_p1, 1)
                    if f and f.known and f.s == 2:
                        dve.wait_ge(s_zero, 1)

                slots(dve, task)


class Route(Part):
    CENTER, LOWER, UPPER = 1.0 / math.e, 0.5 - math.log(4.0 / 3.0), 0.5

    def __init__(self, nc, ctx, logits, temperature, number):
        sem = Sems(nc, "route")

        def small(what, shape):
            return ctx.enter_context(nc.sbuf_tensor(f"route_{what}", shape, F32))[:, :]

        def tile(what):
            return small(what, [P, NTT * EXPERTS]).rearrange("p (j e) -> p j e", e=EXPERTS)

        self.inh, self.dist, self.zone, self.wz, self.fb = (tile(n) for n in ("inh", "dist", "zone", "wz", "fb"))
        self.key, self.picked, self.both, self.left = (tile(n) for n in ("key", "picked", "both", "left"))
        self.best, self.total, self.none, self.some = (small(n, [P, NTT]) for n in ("best", "total", "none", "some"))
        self.num, self.temp, self.inv_t = small("num", [P, EXPERTS]), small("temp", [P, 1]), small("inv_t", [P, 1])
        self.s_in, self.s_own, self.s_t = sem("in"), sem("own"), sem("t")
        self.s_inh, self.s_dist, self.s_exp = sem("inh"), sem("dist"), sem("exp")
        self.out = logits.rearrange("p (j e) -> p j e", e=EXPERTS)
        self.temperature, self.number = temperature, number

    def early(self, sp):
        sp.dma_start(self.num, self.number).then_inc(self.s_in, 16)
        sp.dma_start(self.temp, self.temperature.rearrange("(a n) -> a n", a=1).to_broadcast([P, 1])).then_inc(self.s_in, 16)

    def scalar(self, act):
        act.wait_ge(self.s_t, 1)
        act.activation(self.inh, self.out, ACT.Sigmoid, scale=self.inv_t).then_inc(self.s_inh, 1)
        act.wait_ge(self.s_dist, 1)
        act.activation(self.dist, self.dist, ACT.Abs).then_inc(self.s_exp, 1)
        act.wait_ge(self.s_exp, 1)
        act.activation(self.wz, self.dist, ACT.Exp, scale=-1.0 / 0.1).then_inc(self.s_exp, 1)
        act.activation(self.fb, self.dist, ACT.Exp, scale=-1.0 / 0.3).then_inc(self.s_exp, 1)

    def vector(self, dve):
        inh, dist, zone, wz, fb, out = self.inh, self.dist, self.zone, self.wz, self.fb, self.out
        key, picked, both, left = self.key, self.picked, self.both, self.left
        best, total, none, some = self.best, self.total, self.none, self.some
        CENTER, LOWER, UPPER, E = self.CENTER, self.LOWER, self.UPPER, EXPERTS
        over = lambda t: t.unsqueeze(2).to_broadcast([P, NTT, E])
        dve.wait_ge(self.s_in, 32)
        dve.reciprocal(self.inv_t, self.temp).then_inc(self.s_t, 1)
        step = Chain(dve, self.s_own).link
        dve.wait_ge(self.s_inh, 1)
        dve.tensor_scalar(dist, inh, CENTER, None, ALU.subtract).then_inc(self.s_dist, 1)
        step(dve.tensor_scalar(zone, inh, LOWER, None, ALU.is_ge))
        step(dve.scalar_tensor_tensor(zone, inh, UPPER, zone, op0=ALU.is_le, op1=ALU.mult))
        dve.wait_ge(self.s_exp, 3)
        step(dve.tensor_tensor(wz, wz, zone, ALU.mult))
        step(dve.tensor_reduce(total, wz, AX.X, ALU.add))
        step(dve.tensor_scalar(none, total, 1e-8, None, ALU.is_lt))
        step(dve.tensor_copy(left, fb))
        for n in range(2):
            step(dve.tensor_reduce(best, left, AX.X, ALU.max))
            step(dve.tensor_tensor(key, left, over(best), ALU.is_ge))
            step(dve.scalar_tensor_tensor(key, key, -float(E),
                                          self.num.unsqueeze(1).to_broadcast([P, NTT, E]),
                                          op0=ALU.mult, op1=ALU.add))
            step(dve.tensor_reduce(best, key, AX.X, ALU.min))
            step(dve.tensor_tensor(picked, key, over(best), ALU.is_equal))
            if n == 0:
                step(dve.tensor_copy(both, picked))
                step(dve.scalar_tensor_tensor(left, picked, -4.0, left, op0=ALU.mult, op1=ALU.add))
            else:
                step(dve.tensor_tensor(both, both, picked, ALU.add))
        step(dve.tensor_tensor(fb, fb, both, ALU.mult))
        step(dve.tensor_reduce(total, fb, AX.X, ALU.add))
        step(dve.tensor_scalar(total, total, 1e-8, None, ALU.max))
        step(dve.reciprocal(total, total))
        step(dve.tensor_tensor(fb, fb, over(total), ALU.mult))
        step(dve.tensor_scalar(some, none, -1.0, 1.0, ALU.mult, ALU.add))
        step(dve.tensor_tensor(wz, wz, over(some), ALU.mult))
        step(dve.tensor_tensor(fb, fb, over(none), ALU.mult))
        step(dve.tensor_tensor(wz, wz, fb, ALU.add))
        step(dve.tensor_reduce(total, wz, AX.X, ALU.add))
        step(dve.tensor_scalar(total, total, 1e-8, None, ALU.max))
        step(dve.reciprocal(total, total))
        step(dve.tensor_tensor(out, wz, over(total), ALU.mult))


def program(nc, a, out):
    lag_b = nc.dram_tensor("lag_b_scratch", [2 * HEADS, TOK], F32, kind="Internal").ap()
    saved = nc.dram_tensor("residual_scratch", [P, NTT * HID], F32, kind="Internal").ap()
    with ExitStack() as ctx:
        mem = {}
        for name, shape in (("x_tok", [P, NTT * HID]), ("ident", [P, P]), ("minus_half", [P, NTT])):
            mem[name] = ctx.enter_context(nc.sbuf_tensor(name, shape, F32))
        s_id = ctx.enter_context(nc.semaphore("s_ident"))
        with nc.Block() as block:
            @block.sync
            def _(sp):
                sp.dma_start(mem["ident"][:, :], a["identity"]).then_inc(s_id, 16)
                sp.wait_ge(s_id, 16)

            @block.vector
            def _(dve):
                dve.memset(mem["minus_half"][:, :], -0.5)

        pooled_attention(nc, mem, a["x"], {n: a["w_" + n] for n in ("q", "qa", "k", "ka", "v")}, a["columns"])
        for name in ("xT_hi", "xT_lo"):
            mem[name] = ctx.enter_context(nc.sbuf_tensor(name, [P, KC, TOK], F32R))
        gated_units(nc, "dense", mem, a["dense_gate"], a["dense_up"], a["dense_down"], INNER // UNIT,
                    lambda ctx, plain, parts, banks: [Norm(nc, ctx, "turn0", mem, plain[0:TPB], banks[0:TPB],
                                                            normalise=False)],
                    "norm1",
                    scales=(a["dense_gate_scale"], a["dense_up_scale"], a["dense_down_scale"].to_broadcast([P, HID])))
        with nc.sbuf_tensor("lag_a", [P, NTT * HEADS], F32) as lag_a, nc.sbuf_tensor("ssum", [P, NTT * HEADS], F32) as ssum:
            mem["ssum"] = ssum

            def before_heads(ctx, plain, parts, banks):
                factors = Projection(nc, ctx, "factors", mem, a["head_factors"], 2 * HEADS, lag_a[:, :], HEADS,
                                     parts, plain[TPB:], banks[TPB:], by_feature=lag_b)
                return [Norm(nc, ctx, "turn1", mem, plain[0:TPB], banks[0:TPB], normalise=False, then=factors), factors]

            lagged_attention(nc, mem, a["head_weights"], a["head_out"], a["conv"], a["head_norm"], a["rotation"],
                             a["band"], lag_a[:, :], lag_b, saved, before_heads)

            with nc.sbuf_tensor("expert_weight", [P, NTT * EXPERTS], F32) as expert_weight:
                def before_experts(ctx, plain, parts, banks):
                    router = Projection(nc, ctx, "router", mem, a["router"], EXPERTS, expert_weight[:, :], EXPERTS,
                                        parts, plain[TPB:TPB + 2], banks[TPB:TPB + 2])
                    return [Norm(nc, ctx, "norm2", mem, plain[0:TPB], banks[0:TPB],
                                 rms=(saved, plain[-TPB:], ssum[:, :]), then=router),
                            router,
                            Route(nc, ctx, expert_weight[:, :], a["temperature"], a["numbers"])]

                gated_units(nc, "experts", mem, a["expert_gate"], a["expert_up"], a["expert_down"],
                            EXPERTS * EXPERT_WIDTH // UNIT, before_experts, "norm3", expert_weight=expert_weight[:, :],
                            store=out)


def kernel(**inputs):
    import concourse.bacc as bacc
    from concourse.bass_utils import run_bass_kernel_spmd

    v = {k: np.asarray(t) for k, t in inputs.items()}

    def rows_first(w):
        return w.reshape(KC, P, -1).transpose(1, 0, 2).reshape(P, -1)

    def padded(w):
        return np.pad(w, ((0, 0), (0, P - w.shape[1])))

    def columns(t):
        return t.reshape(-1, P).T

    def by_unit_in(w):
        return w.reshape(KC, P, -1, UNIT).transpose(2, 1, 0, 3).reshape(-1, P, KC * UNIT)

    def by_unit_out(w):
        return w.reshape(-1, FPU, P, HID).transpose(0, 2, 1, 3).reshape(-1, P, FPU * HID)

    def experts_in(w):
        return w.reshape(EXPERTS, KC, P, -1, UNIT).transpose(0, 3, 2, 1, 4).reshape(-1, P, KC * UNIT)

    inv = (1.0 / ROPE_BASE ** (np.arange(0, HDIM, 2, dtype=np.float32) / HDIM)).astype(np.float32)
    angle = np.arange(SEQ, dtype=np.float32)[:, None] * inv[None, :]
    cos, sin = np.cos(angle).astype(np.float32).T, np.sin(angle).astype(np.float32).T
    rotation = np.concatenate([np.concatenate([cos, cos], 0), np.concatenate([-sin, sin], 0)], 1)
    lag = np.arange(P + LAGS - 1)[None, :] - np.arange(P)[:, None]
    band = np.where((lag >= 0) & (lag < LAGS), 0.5 / math.sqrt(HDIM), 0.0).astype(np.float32)

    arrays = {
        "x": v["L0_attn_hidden_states"],
        "identity": np.eye(P, dtype=np.float32),
        "columns": np.concatenate([columns(v["L0_attn_" + n]) for n in
                                   ("ln_g", "ln_b", "bq", "bqa", "bk", "bka", "bv")], 1),
        **{"w_" + n: rows_first(v["L0_attn_W" + n].T) for n in ("q", "qa", "k", "ka", "v")},
        "dense_gate": by_unit_in(v["L0_ffn_gate_w"].T),
        "dense_up": by_unit_in(v["L0_ffn_up_w"].T),
        "dense_down": by_unit_out(v["L0_ffn_down_w"].T),
        "dense_gate_scale": columns(v["L0_ffn_gate_scale"]),
        "dense_up_scale": columns(v["L0_ffn_up_scale"]),
        "dense_down_scale": v["L0_ffn_down_scale"].reshape(1, HID),
        "head_weights": np.stack([v["L1_attn_W" + n].reshape(KC, P, HEADS, HDIM) for n in "qkvz"], 0)
                          .transpose(3, 2, 0, 1, 4).reshape(HEADS, P, 4 * KC * HDIM),
        "head_out": v["L1_attn_Wout"].reshape(HEADS, P, HID),
        "head_factors": rows_first(padded(np.concatenate([v["L1_attn_Wa"], v["L1_attn_Wb"]], 1))),
        "conv": np.stack([v[f"L1_attn_conv_{n}_w"].reshape(HEADS, HDIM, LAGS) for n in "qkv"], 0)
                  .transpose(2, 1, 0, 3).reshape(P, HEADS * 3 * LAGS),
        "head_norm": v["L1_attn_norm_w"].reshape(HEADS, P).T,
        "rotation": rotation,
        "band": band,
        "router": rows_first(padded(v["L1_ffn_Wr"])),
        "temperature": v["L1_ffn_temperature"],
        "numbers": np.broadcast_to(np.arange(EXPERTS, dtype=np.float32), (P, EXPERTS)),
        "expert_gate": experts_in(v["L1_ffn_Wg"]),
        "expert_up": experts_in(v["L1_ffn_Wu"]),
        "expert_down": by_unit_out(v["L1_ffn_Wd"].reshape(-1, HID)),
    }
    nc = bacc.Bacc("TRN2", target_bir_lowering=False, num_devices=1)
    host, dram = {}, {}
    for name, t in arrays.items():
        host["in_" + name] = np.ascontiguousarray(t)
        dram[name] = nc.dram_tensor("in_" + name, t.shape, mybir.dt.from_np(t.dtype), kind="ExternalInput").ap()
    out = nc.dram_tensor("out", (TOK, HID), F32, kind="ExternalOutput").ap()
    program(nc, dram, out)
    result = run_bass_kernel_spmd(nc, [host], core_ids=[0])
    return result.results[0]["out"].reshape(BATCH, SEQ, HID)
```
